# Optimizing a Trainium2 kernel written in Bass

```python
import numpy as np
import jax
import jax.numpy as jnp

def _softmax(x, axis=-1):
    return jax.nn.softmax(x, axis=axis)

def _gelu(x):
    return jax.nn.gelu(x, approximate=True)

def _silu(x):
    return jax.nn.silu(x)

def _sigmoid(x):
    return jax.nn.sigmoid(x)

def _layernorm(x, axis=-1, eps=1e-05):
    m = jnp.mean(x, axis=axis, keepdims=True)
    v = jnp.var(x, axis=axis, keepdims=True)
    return (x - m) / jnp.sqrt(v + eps)

def _scatter_add(tgt, idx, src, axis=0):
    return tgt.at[idx].add(src)

def _segment_sum(src, seg, n):
    return jax.ops.segment_sum(src, seg, n)
kernel_name = 'mk_decoder_postln_d2_seqx_r8_4506e2'

def setup_inputs(seed: int=0):
    np.random.seed(seed)
    _w = jnp.asarray

    def _rec_inputs():
        import jax
        import jax.numpy as jnp
        _rk = jax.random.key(seed)
        x = -0.0002928 + 1 * jax.random.normal(jax.random.fold_in(_rk, 1), (4, 256, 256), jnp.float32)
        _lenS = 256 - jax.random.randint(jax.random.fold_in(_rk, 7), (4,), 0, max(1, 256 // 4) + 1, jnp.int32)
        _lenS2 = 64 - jax.random.randint(jax.random.fold_in(_rk, 8), (4,), 0, max(1, 64 // 4) + 1, jnp.int32)
        _ctx_2048P = jax.random.normal(jax.random.fold_in(_rk, 11), (4, 16, 256), jnp.float32)
        _ctx_2048c = jax.random.dirichlet(jax.random.fold_in(_rk, 511), 0.3 * jnp.ones((16,), jnp.float32), (4, 64))
        _ctx_2048t = jnp.einsum('bsk,bkd->bsd', _ctx_2048c, _ctx_2048P)
        _ctx_2048t = _ctx_2048t * jax.lax.rsqrt(jnp.mean(jnp.square(_ctx_2048t)) + 1e-12) * 0.953939
        ctx_2048 = 4.13588e-05 + 0.999923 * (_ctx_2048t + 0.3 * jax.random.normal(jax.random.fold_in(_rk, 611), (4, 64, 256), jnp.float32))
        _validS = jnp.arange(256)[None, :] < _lenS[:, None]
        _validS2 = jnp.arange(64)[None, :] < _lenS2[:, None]
        _causal = jnp.tril(jnp.ones((256, 256), dtype=bool))
        mask_1xSxS2_ff0 = jnp.where(jnp.ones((1, 256, 64), dtype=bool), 0.0, -1000000000.0).astype(jnp.float32)
        return (x, ctx_2048, mask_1xSxS2_ff0)
    x, ctx_2048, mask_1xSxS2_ff0 = _rec_inputs()

    def _L0_attn_setup():
        import jax, jax.numpy as jnp
        import numpy as np
        BATCH, SEQ, D_MODEL, N_HEADS, D_HEAD = (2, 256, 256, 16, 128)
        ATTN_SCALE = np.sqrt(D_HEAD).astype(np.float32)
        IGNORE = jnp.float32(-100000.0)
        key = jax.random.key(seed)
        ks = jax.random.split(key, 5)
        init = 1.0 / np.sqrt(D_MODEL)
        return {'x': jax.random.normal(ks[0], (BATCH, SEQ, D_MODEL), jnp.float32), 'W_Q': jax.random.normal(ks[1], (N_HEADS, D_MODEL, D_HEAD), jnp.float32) * init, 'W_K': jax.random.normal(ks[2], (N_HEADS, D_MODEL, D_HEAD), jnp.float32) * init, 'W_V': jax.random.normal(ks[3], (N_HEADS, D_MODEL, D_HEAD), jnp.float32) * init, 'W_O': jax.random.normal(ks[4], (N_HEADS, D_HEAD, D_MODEL), jnp.float32) * init, 'b_Q': jnp.zeros((N_HEADS, D_HEAD), jnp.float32), 'b_K': jnp.zeros((N_HEADS, D_HEAD), jnp.float32), 'b_V': jnp.zeros((N_HEADS, D_HEAD), jnp.float32), 'b_O': jnp.zeros((D_MODEL,), jnp.float32)}
    _L0_attn_all = _L0_attn_setup()
    _L0_attn_in = {k: v for k, v in _L0_attn_all.items() if k in ('W_Q', 'W_K', 'W_V', 'W_O', 'b_Q', 'b_K', 'b_V', 'b_O')}
    del _L0_attn_all

    def _L0_xattn_setup():
        import jax, jax.numpy as jnp
        import numpy as np
        H = 256
        NH = 16
        NKV = 4
        HD = 128
        GROUPS = NH // NKV
        EPS = 1e-06
        B, S, SE = (1, 256, 512)

        def _rmsnorm(x, w, eps=EPS):
            xf = x.astype(jnp.float32)
            var = jnp.mean(xf * xf, axis=-1, keepdims=True)
            return (xf * jax.lax.rsqrt(var + eps)).astype(x.dtype) * w
        key = jax.random.key(seed)
        ks = jax.random.split(key, 12)
        sc = 0.02
        return {'hidden_states': jax.random.normal(ks[0], (B, S, H), jnp.float32), 'encoder_hidden_states': jax.random.normal(ks[1], (B, SE, H), jnp.float32), 'attention_mask': jnp.zeros((B, S, SE), jnp.float32), 'Wq': jax.random.normal(ks[2], (H, NH * HD), jnp.float32) * sc, 'bq': jax.random.normal(ks[3], (NH * HD,), jnp.float32) * sc, 'Wk': jax.random.normal(ks[4], (H, NKV * HD), jnp.float32) * sc, 'bk': jax.random.normal(ks[5], (NKV * HD,), jnp.float32) * sc, 'Wv': jax.random.normal(ks[6], (H, NKV * HD), jnp.float32) * sc, 'bv': jax.random.normal(ks[7], (NKV * HD,), jnp.float32) * sc, 'Wo': jax.random.normal(ks[8], (NH * HD, H), jnp.float32) * sc, 'qn_w': jnp.ones((HD,), jnp.float32), 'kn_w': jnp.ones((HD,), jnp.float32)}
    _L0_xattn_all = _L0_xattn_setup()
    _L0_xattn_in = {k: v for k, v in _L0_xattn_all.items() if k in ('Wq', 'bq', 'Wk', 'bk', 'Wv', 'bv', 'Wo', 'qn_w', 'kn_w')}
    del _L0_xattn_all

    def _L0_ffn_setup():
        import jax, jax.numpy as jnp
        import numpy as np
        N_HEAD = 16
        N_EMBD = 256
        R = 8
        HEAD_DIM = N_EMBD // N_HEAD
        D_STD = HEAD_DIM - R
        THRESHOLD = 0.1
        B, T = (4, 128)
        key = jax.random.key(seed)
        k1, k2, k3, k4, k5 = jax.random.split(key, 5)
        fused_dim = 2 * N_HEAD * D_STD + N_EMBD + 2 * N_HEAD * R
        x = jax.random.normal(k1, (B, T, N_EMBD), dtype=jnp.float32)
        Wa = jax.random.normal(k2, (N_EMBD, fused_dim), dtype=jnp.float32) * 0.02
        Wp = jax.random.normal(k3, (N_EMBD, N_EMBD), dtype=jnp.float32) * 0.02
        w_std = jax.random.uniform(k4, (N_HEAD,), dtype=jnp.float32, minval=0.3, maxval=0.7)
        w_rec = jax.random.uniform(k5, (N_HEAD,), dtype=jnp.float32)
        return {'x': x, 'Wa': Wa, 'Wp': Wp, 'w_std': w_std, 'w_rec': w_rec}
    _L0_ffn_all = _L0_ffn_setup()
    _L0_ffn_in = {k: v for k, v in _L0_ffn_all.items() if k in ('Wa', 'Wp', 'w_std', 'w_rec')}
    del _L0_ffn_all

    def _L1_attn_setup():
        import jax, jax.numpy as jnp
        import numpy as np
        DIM = 256
        H = 16
        D = DIM // H // 2
        LAYER_NUM = 12
        LAM_INIT = 0.8 - 0.6 * float(np.exp(-0.3 * LAYER_NUM))
        SCALE = D ** (-0.5)
        EPS = 1e-05

        def _split_qk(y, b, n):
            y = y.reshape(b, n, H, D, 2)
            y = y.transpose(0, 1, 4, 2, 3)
            return y.reshape(b, n, 2 * H, D)
        key = jax.random.key(seed)
        ks = jax.random.split(key, 10)
        B, N = (4, 512)
        return {'x': jax.random.normal(ks[0], (B, N, DIM), dtype=jnp.float32), 'Wq': jax.random.normal(ks[1], (DIM, DIM), dtype=jnp.float32) * DIM ** (-0.5), 'Wk': jax.random.normal(ks[2], (DIM, DIM), dtype=jnp.float32) * DIM ** (-0.5), 'Wv': jax.random.normal(ks[3], (DIM, DIM), dtype=jnp.float32) * DIM ** (-0.5), 'Wo': jax.random.normal(ks[4], (DIM, DIM), dtype=jnp.float32) * DIM ** (-0.5), 'bo': jax.random.normal(ks[5], (DIM,), dtype=jnp.float32) * 0.01, 'lq1': jax.random.normal(ks[6], (D,), dtype=jnp.float32) * 0.1, 'lq2': jax.random.normal(ks[7], (D,), dtype=jnp.float32) * 0.1, 'lk1': jax.random.normal(ks[8], (D,), dtype=jnp.float32) * 0.1, 'lk2': jax.random.normal(ks[9], (D,), dtype=jnp.float32) * 0.1}
    _L1_attn_all = _L1_attn_setup()
    _L1_attn_in = {k: v for k, v in _L1_attn_all.items() if k in ('Wq', 'Wk', 'Wv', 'Wo', 'bo', 'lq1', 'lq2', 'lk1', 'lk2')}
    del _L1_attn_all

    def _L1_xattn_setup():
        import jax, jax.numpy as jnp
        import numpy as np
        B, S, D = (8, 128, 256)
        H, HD = (16, 128)
        key = jax.random.key(seed)
        ks = jax.random.split(key, 6)
        fan_in = 1.0 / np.sqrt(D)
        return {'inputs_q': jax.random.normal(ks[0], (B, S, D), jnp.float32), 'inputs_kv': jax.random.normal(ks[1], (B, S, D), jnp.float32), 'Wq': jax.random.normal(ks[2], (D, H * HD), jnp.float32) * fan_in, 'Wk': jax.random.normal(ks[3], (D, H * HD), jnp.float32) * fan_in, 'Wv': jax.random.normal(ks[4], (D, H * HD), jnp.float32) * fan_in, 'Wo': jax.random.normal(ks[5], (H * HD, D), jnp.float32) * (1.0 / np.sqrt(H * HD))}
    _L1_xattn_all = _L1_xattn_setup()
    _L1_xattn_in = {k: v for k, v in _L1_xattn_all.items() if k in ('Wq', 'Wk', 'Wv', 'Wo')}
    del _L1_xattn_all

    def _L1_ffn_setup():
        import jax, jax.numpy as jnp
        import numpy as np
        TOP_K = 8

        def _masked_routing(router_logits):
            T, E = router_logits.shape
            sel_w, sel_e = jax.lax.top_k(router_logits, TOP_K)
            sel_w = jax.nn.softmax(sel_w.astype(jnp.float32), axis=1)
            rows = jnp.arange(T)[:, None]
            masked = jnp.zeros((T, E), dtype=jnp.float32).at[rows, sel_e].set(sel_w)
            count = jnp.zeros((E,), dtype=jnp.int32).at[sel_e.reshape(-1)].add(1)
            return (masked, count)
        key = jax.random.key(seed)
        k1, k2, k3, k4, k5 = jax.random.split(key, 5)
        B, S, H, E, I = (1, 256, 256, 32, 96)
        return {'hidden_states': jax.random.normal(k1, (B, S, H), dtype=jnp.float32), 'gate_w': jax.random.normal(k2, (E, H), dtype=jnp.float32) * H ** (-0.5), 'w_gate_proj': jax.random.normal(k3, (E, I, H), dtype=jnp.float32) * H ** (-0.5), 'w_up_proj': jax.random.normal(k4, (E, I, H), dtype=jnp.float32) * H ** (-0.5), 'w_down_proj': jax.random.normal(k5, (E, H, I), dtype=jnp.float32) * I ** (-0.5)}
    _L1_ffn_all = _L1_ffn_setup()
    _L1_ffn_in = {k: v for k, v in _L1_ffn_all.items() if k in ('gate_w', 'w_gate_proj', 'w_up_proj', 'w_down_proj')}
    del _L1_ffn_all
    return {'x': x, 'ctx_2048': ctx_2048, 'mask_1xSxS2_ff0': mask_1xSxS2_ff0, 'L0_attn_W_Q': _L0_attn_in['W_Q'], 'L0_attn_W_K': _L0_attn_in['W_K'], 'L0_attn_W_V': _L0_attn_in['W_V'], 'L0_attn_W_O': _L0_attn_in['W_O'], 'L0_attn_b_Q': _L0_attn_in['b_Q'], 'L0_attn_b_K': _L0_attn_in['b_K'], 'L0_attn_b_V': _L0_attn_in['b_V'], 'L0_attn_b_O': _L0_attn_in['b_O'], 'L0_xattn_Wq': _L0_xattn_in['Wq'], 'L0_xattn_bq': _L0_xattn_in['bq'], 'L0_xattn_Wk': _L0_xattn_in['Wk'], 'L0_xattn_bk': _L0_xattn_in['bk'], 'L0_xattn_Wv': _L0_xattn_in['Wv'], 'L0_xattn_bv': _L0_xattn_in['bv'], 'L0_xattn_Wo': _L0_xattn_in['Wo'], 'L0_xattn_qn_w': _L0_xattn_in['qn_w'], 'L0_xattn_kn_w': _L0_xattn_in['kn_w'], 'L0_ffn_Wa': _L0_ffn_in['Wa'], 'L0_ffn_Wp': _L0_ffn_in['Wp'], 'L0_ffn_w_std': _L0_ffn_in['w_std'], 'L0_ffn_w_rec': _L0_ffn_in['w_rec'], 'L1_attn_Wq': _L1_attn_in['Wq'], 'L1_attn_Wk': _L1_attn_in['Wk'], 'L1_attn_Wv': _L1_attn_in['Wv'], 'L1_attn_Wo': _L1_attn_in['Wo'], 'L1_attn_bo': _L1_attn_in['bo'], 'L1_attn_lq1': _L1_attn_in['lq1'], 'L1_attn_lq2': _L1_attn_in['lq2'], 'L1_attn_lk1': _L1_attn_in['lk1'], 'L1_attn_lk2': _L1_attn_in['lk2'], 'L1_xattn_Wq': _L1_xattn_in['Wq'], 'L1_xattn_Wk': _L1_xattn_in['Wk'], 'L1_xattn_Wv': _L1_xattn_in['Wv'], 'L1_xattn_Wo': _L1_xattn_in['Wo'], 'L1_ffn_gate_w': _L1_ffn_in['gate_w'], 'L1_ffn_w_gate_proj': _L1_ffn_in['w_gate_proj'], 'L1_ffn_w_up_proj': _L1_ffn_in['w_up_proj'], 'L1_ffn_w_down_proj': _L1_ffn_in['w_down_proj']}

def reference(x, ctx_2048, mask_1xSxS2_ff0, L0_attn_W_Q, L0_attn_W_K, L0_attn_W_V, L0_attn_W_O, L0_attn_b_Q, L0_attn_b_K, L0_attn_b_V, L0_attn_b_O, L0_xattn_Wq, L0_xattn_bq, L0_xattn_Wk, L0_xattn_bk, L0_xattn_Wv, L0_xattn_bv, L0_xattn_Wo, L0_xattn_qn_w, L0_xattn_kn_w, L0_ffn_Wa, L0_ffn_Wp, L0_ffn_w_std, L0_ffn_w_rec, L1_attn_Wq, L1_attn_Wk, L1_attn_Wv, L1_attn_Wo, L1_attn_bo, L1_attn_lq1, L1_attn_lq2, L1_attn_lk1, L1_attn_lk2, L1_xattn_Wq, L1_xattn_Wk, L1_xattn_Wv, L1_xattn_Wo, L1_ffn_gate_w, L1_ffn_w_gate_proj, L1_ffn_w_up_proj, L1_ffn_w_down_proj):
    import jax
    import jax.numpy as jnp

    def _L0_attn_ref(x, W_Q, W_K, W_V, W_O, b_Q, b_K, b_V, b_O):
        import jax, jax.numpy as jnp
        import numpy as np
        BATCH, SEQ, D_MODEL, N_HEADS, D_HEAD = (2, 256, 256, 16, 128)
        ATTN_SCALE = np.sqrt(D_HEAD).astype(np.float32)
        IGNORE = jnp.float32(-100000.0)
        q = jnp.einsum('bpd,hde->bphe', x, W_Q) + b_Q
        k = jnp.einsum('bpd,hde->bphe', x, W_K) + b_K
        v = jnp.einsum('bpd,hde->bphe', x, W_V) + b_V
        scores = jnp.einsum('bqhe,bkhe->bhqk', q, k) / ATTN_SCALE
        S = x.shape[1]
        causal = jnp.tril(jnp.ones((S, S), bool))
        scores = jnp.where(causal, scores, IGNORE)
        attn = jax.nn.softmax(scores, axis=-1)
        z = jnp.einsum('bkhe,bhqk->bqhe', v, attn)
        out = jnp.einsum('bqhe,hed->bqd', z, W_O) + b_O
        return out

    def _L0_xattn_ref(hidden_states, encoder_hidden_states, attention_mask, Wq, bq, Wk, bk, Wv, bv, Wo, qn_w, kn_w):
        import jax, jax.numpy as jnp
        import numpy as np
        H = 256
        NH = 16
        NKV = 4
        HD = 128
        GROUPS = NH // NKV
        EPS = 1e-06
        B, S, SE = (1, 256, 512)

        def _rmsnorm(x, w, eps=EPS):
            xf = x.astype(jnp.float32)
            var = jnp.mean(xf * xf, axis=-1, keepdims=True)
            return (xf * jax.lax.rsqrt(var + eps)).astype(x.dtype) * w
        b, s, _ = hidden_states.shape
        se = encoder_hidden_states.shape[1]
        q = (hidden_states @ Wq + bq).reshape(b, s, NH, HD).transpose(0, 2, 1, 3)
        k = (encoder_hidden_states @ Wk + bk).reshape(b, se, NKV, HD).transpose(0, 2, 1, 3)
        v = (encoder_hidden_states @ Wv + bv).reshape(b, se, NKV, HD).transpose(0, 2, 1, 3)
        k = jnp.repeat(k, GROUPS, axis=1)
        v = jnp.repeat(v, GROUPS, axis=1)
        q = _rmsnorm(q, qn_w)
        k = _rmsnorm(k, kn_w)
        scale = 1.0 / np.sqrt(HD).astype(np.float32)
        scores = jnp.einsum('bhsd,bhed->bhse', q, k) * scale
        scores = scores + attention_mask[:, None, :, :]
        probs = jax.nn.softmax(scores.astype(jnp.float32), axis=-1).astype(q.dtype)
        out = jnp.einsum('bhse,bhed->bhsd', probs, v)
        out = out.transpose(0, 2, 1, 3).reshape(b, s, NH * HD)
        return out @ Wo

    def _L0_ffn_ref(x, Wa, Wp, w_std, w_rec):
        import jax, jax.numpy as jnp
        import numpy as np
        N_HEAD = 16
        N_EMBD = 256
        R = 8
        HEAD_DIM = N_EMBD // N_HEAD
        D_STD = HEAD_DIM - R
        THRESHOLD = 0.1
        B, T = (4, 128)
        Bx, Tx, C = x.shape
        H, D, Ds, r = (N_HEAD, HEAD_DIM, D_STD, R)
        s_std = jnp.sqrt(jnp.clip(w_std, 1e-08, None))
        s_rec = jnp.sqrt(jnp.clip(w_rec, 1e-08, None))
        col_scale = jnp.concatenate([jnp.repeat(s_std, Ds), jnp.repeat(s_std, Ds), jnp.ones((C,), dtype=x.dtype), jnp.repeat(s_rec, r), jnp.repeat(s_rec, r)])
        Wb = Wa * col_scale[None, :]
        fused = x @ Wb
        q_std_end = H * Ds
        k_std_end = q_std_end + H * Ds
        v_end = k_std_end + C
        q_low_end = v_end + H * r

        def heads(t, d):
            return t.reshape(Bx, Tx, H, d).transpose(0, 2, 1, 3)
        Q_std = heads(fused[..., :q_std_end], Ds)
        K_std = heads(fused[..., q_std_end:k_std_end], Ds)
        V = heads(fused[..., k_std_end:v_end], D)
        Q_low = heads(fused[..., v_end:q_low_end], r)
        K_low = heads(fused[..., q_low_end:], r)
        use_ra = (w_rec > THRESHOLD)[None, :, None, None]
        q_tail = jnp.where(use_ra, K_low, Q_low)
        k_tail = jnp.where(use_ra, Q_low, K_low)
        Qf = jnp.concatenate([Q_std, q_tail], axis=-1)
        Kf = jnp.concatenate([K_std, k_tail], axis=-1)
        scale = 1.0 / jnp.sqrt(jnp.asarray(D, dtype=x.dtype))
        scores = jnp.einsum('bhtd,bhsd->bhts', Qf, Kf) * scale
        causal = jnp.tril(jnp.ones((Tx, Tx), dtype=bool))
        scores = jnp.where(causal[None, None], scores, jnp.finfo(scores.dtype).min)
        attn = jax.nn.softmax(scores, axis=-1)
        out = jnp.einsum('bhts,bhsd->bhtd', attn, V)
        y = out.transpose(0, 2, 1, 3).reshape(Bx, Tx, C)
        return y @ Wp

    def _L1_attn_ref(x, Wq, Wk, Wv, Wo, bo, lq1, lq2, lk1, lk2):
        import jax, jax.numpy as jnp
        import numpy as np
        DIM = 256
        H = 16
        D = DIM // H // 2
        LAYER_NUM = 12
        LAM_INIT = 0.8 - 0.6 * float(np.exp(-0.3 * LAYER_NUM))
        SCALE = D ** (-0.5)
        EPS = 1e-05

        def _split_qk(y, b, n):
            y = y.reshape(b, n, H, D, 2)
            y = y.transpose(0, 1, 4, 2, 3)
            return y.reshape(b, n, 2 * H, D)
        b, n, _ = x.shape
        q = _split_qk(x @ Wq.T, b, n) * SCALE
        k = _split_qk(x @ Wk.T, b, n)
        v = (x @ Wv.T).reshape(b, n, H, 2 * D).transpose(0, 2, 1, 3)
        att = jnp.einsum('bnqd,bnkd->bnqk', q, k)
        att = jnp.nan_to_num(att)
        att = jax.nn.softmax(att.astype(jnp.float32), axis=-1)
        lam = jnp.exp(jnp.sum(lq1 * lk1)) - jnp.exp(jnp.sum(lq2 * lk2)) + LAM_INIT
        diff = att[:, :, :H, :H] - lam * att[:, :, H:, H:]
        out = jnp.einsum('bnah,bhnd->bnad', diff, v)
        out = out * jax.lax.rsqrt(jnp.mean(out * out, axis=-1, keepdims=True) + EPS)
        out = out * (1.0 - LAM_INIT)
        out = out.reshape(b, n, DIM)
        return out @ Wo.T + bo

    def _L1_xattn_ref(inputs_q, inputs_kv, Wq, Wk, Wv, Wo):
        import jax, jax.numpy as jnp
        import numpy as np
        B, S, D = (8, 128, 256)
        H, HD = (16, 128)
        b, sq, _ = inputs_q.shape
        skv = inputs_kv.shape[1]
        q = (inputs_q @ Wq).reshape(b, sq, H, HD) * (1.0 / np.sqrt(HD))
        k = (inputs_kv @ Wk).reshape(b, skv, H, HD)
        v = (inputs_kv @ Wv).reshape(b, skv, H, HD)
        scores = jnp.einsum('bqhd,bkhd->bhqk', q, k)
        attn = jax.nn.softmax(scores, axis=-1)
        ctx = jnp.einsum('bhqk,bkhd->bqhd', attn, v).reshape(b, sq, H * HD)
        return ctx @ Wo

    def _L1_ffn_ref(hidden_states, gate_w, w_gate_proj, w_up_proj, w_down_proj):
        import jax, jax.numpy as jnp
        import numpy as np
        TOP_K = 8

        def _masked_routing(router_logits):
            T, E = router_logits.shape
            sel_w, sel_e = jax.lax.top_k(router_logits, TOP_K)
            sel_w = jax.nn.softmax(sel_w.astype(jnp.float32), axis=1)
            rows = jnp.arange(T)[:, None]
            masked = jnp.zeros((T, E), dtype=jnp.float32).at[rows, sel_e].set(sel_w)
            count = jnp.zeros((E,), dtype=jnp.int32).at[sel_e.reshape(-1)].add(1)
            return (masked, count)
        B, S, H = hidden_states.shape
        x = hidden_states.reshape(-1, H)
        router_logits = x @ gate_w.T
        masked_w, _count = _masked_routing(router_logits)
        g = jnp.einsum('th,eih->tei', x, w_gate_proj)
        u = jnp.einsum('th,eih->tei', x, w_up_proj)
        h = jax.nn.silu(g) * u
        h = h * masked_w[:, :, None]
        out = jnp.einsum('tei,ehi->th', h, w_down_proj)
        return out.reshape(B, S, H)
    x = _layernorm(x + _L0_attn_ref(x, L0_attn_W_Q, L0_attn_W_K, L0_attn_W_V, L0_attn_W_O, L0_attn_b_Q, L0_attn_b_K, L0_attn_b_V, L0_attn_b_O), axis=-1)
    x = _layernorm(x + _L0_xattn_ref(x, ctx_2048, mask_1xSxS2_ff0, L0_xattn_Wq, L0_xattn_bq, L0_xattn_Wk, L0_xattn_bk, L0_xattn_Wv, L0_xattn_bv, L0_xattn_Wo, L0_xattn_qn_w, L0_xattn_kn_w), axis=-1)
    x = _layernorm(x + _L0_ffn_ref(x, L0_ffn_Wa, L0_ffn_Wp, L0_ffn_w_std, L0_ffn_w_rec), axis=-1)
    x = _layernorm(x + _L1_attn_ref(x, L1_attn_Wq, L1_attn_Wk, L1_attn_Wv, L1_attn_Wo, L1_attn_bo, L1_attn_lq1, L1_attn_lq2, L1_attn_lk1, L1_attn_lk2), axis=-1)
    x = _layernorm(x + _L1_xattn_ref(x, ctx_2048, L1_xattn_Wq, L1_xattn_Wk, L1_xattn_Wv, L1_xattn_Wo), axis=-1)
    x = _layernorm(x + _L1_ffn_ref(x, L1_ffn_gate_w, L1_ffn_w_gate_proj, L1_ffn_w_up_proj, L1_ffn_w_down_proj), axis=-1)
    return x

_drawn_inputs = setup_inputs


def setup_inputs(seed=0):
    import zlib

    import numpy as np

    out = dict(_drawn_inputs(seed))
    spreads = {'L0_attn_b_Q': (0.0, 0.1),
     'L0_attn_b_K': (0.0, 2.0),
     'L0_attn_b_V': (0.0, 0.1),
     'L0_attn_b_O': (0.0, 0.1),
     'L0_xattn_qn_w': (1.0, 0.6),
     'L0_xattn_kn_w': (1.0, 0.6)}
    factors = {'L0_xattn_bq': 6.674,
     'L0_xattn_bk': 22.309,
     'L0_ffn_w_std': 64.0,
     'L0_ffn_w_rec': 64.0,
     'L1_attn_bo': 3.773,
     'L1_attn_lq1': 5.164,
     'L1_attn_lq2': 4.461,
     'L1_attn_lk1': 3.528,
     'L1_attn_lk2': 5.748}
    for name, (base, spread) in spreads.items():
        noise = np.random.default_rng([zlib.crc32(name.encode()), seed]).standard_normal(out[name].shape)
        drawn = base * np.exp(spread * noise) if base else spread * noise
        out[name] = jnp.asarray(drawn.astype(out[name].dtype))
    for name, factor in factors.items():
        out[name] = (out[name] * factor).astype(out[name].dtype)
    return out
```

```python
from contextlib import ExitStack

import numpy as np

import concourse.bass as bass
from concourse import mybir

F32 = mybir.dt.float32
F16 = mybir.dt.float16
BF16 = mybir.dt.bfloat16
ALU = mybir.AluOpType
ACT = mybir.ActivationFunctionType
X_AXIS = mybir.AxisListType.X

P = 128
BATCH = 4
SEQ = 256
KEYS = 64
DM = 256
DC = DM // P
TOK = BATCH * SEQ
TILES = TOK // P
CTX = BATCH * KEYS
HEADS = 16
HD = 128
BANK = 512
HALVES = TOK // BANK
EXPERTS = 32
INNER = 96
FTILES = EXPERTS * INNER // P
TOP_K = 8
LN_EPS = 1e-5
MASKED = -1e30
LARGEST = float(np.finfo(np.float32).max)
LAM_INIT = 0.8 - 0.6 * float(np.exp(-0.3 * 12))


class Memory:

    def __init__(self, nc):
        self.nc = nc
        self.stack = ExitStack()

    def __enter__(self):
        return self

    def __exit__(self, *_):
        self.stack.close()

    def sb(self, name, shape, dt=F32):
        return self.stack.enter_context(self.nc.sbuf_tensor(name, shape, dt))

    def psum(self, name, shape, dt=F32):
        return self.stack.enter_context(self.nc.psum_tensor(name, shape, dt))


class State:
    pass


def wait_past(eng, signal, value):
    if not (isinstance(value, int) and value <= 0):
        eng.wait_ge(signal, value)


def tile_cols(t):
    return slice(t * P, (t + 1) * P)



NORM_SIGNALS = ("out_ready", "summed", "stats_done", "moments_done", "std_done", "rstd_done",
                "x_ready", "turned", "xT_ready")


class Norm:
    pass


def norm_signals(sem):
    n = Norm()
    n.out_ready, n.summed, n.stats_done, n.moments_done, n.std_done, n.rstd_done, n.x_ready, n.turned, n.xT_ready = (
        sem(f"norm_{name}") for name in NORM_SIGNALS)
    n.base = -TILES
    return n


def norm_tensors(mem, st, stage):
    n = st.norm
    n.base += TILES
    n.stats = mem.sb(f"{stage}_stats", [P, TILES, 6])
    n.moments = mem.sb(f"{stage}_moments", [P, TILES, 2])
    n.std = mem.sb(f"{stage}_std", [P, TILES])
    n.rstd = mem.sb(f"{stage}_rstd", [P, TILES])
    return n


def norm_sum(dve, st, n, part, t):
    dve.wait_ge(n.out_ready, n.base + t + 1)
    dve.tensor_tensor(st.x[:, t, :], part(t), st.x[:, t, :], ALU.add).then_inc(n.summed, 1)
    dve.wait_ge(n.summed, n.base + t + 1)
    dve.bn_stats(n.stats[:, t, :], st.x[:, t, :]).then_inc(n.stats_done, 1)
    dve.wait_ge(n.stats_done, n.base + t + 1)
    dve.bn_aggr(n.moments[:, t, :], n.stats[:, t, :]).then_inc(n.moments_done, 1)


def norm_apply(dve, st, n, t):
    dve.wait_ge(n.std_done, n.base + t + 1)
    dve.reciprocal(n.rstd[:, t:t + 1], n.std[:, t:t + 1]).then_inc(n.rstd_done, 1)
    dve.wait_ge(n.rstd_done, n.base + t + 1)
    dve.tensor_scalar(st.x[:, t, :], st.x[:, t, :], n.moments[:, t, 0:1], n.rstd[:, t:t + 1],
                      ALU.subtract, ALU.mult).then_inc(n.x_ready, 1)


def norm_vector(dve, st, n, part):
    for t in range(TILES + 1):
        if t < TILES:
            norm_sum(dve, st, n, part, t)
        if t > 0:
            norm_apply(dve, st, n, t - 1)


def norm_std(act, st, n, t):
    act.wait_ge(n.moments_done, n.base + t + 1)
    act.activation(n.std[:, t:t + 1], n.moments[:, t, 1:2], ACT.Sqrt,
                   bias=st.eps[:, 0:1]).then_inc(n.std_done, 1)


def norm_keep(act, st, n, turn, t):
    act.wait_ge(n.turned, n.base + t + 1)
    act.activation(st.xT[:, :, tile_cols(t)], turn[t % 2], ACT.Copy).then_inc(n.xT_ready, 1)


def norm_scalar(act, st, n, turn):
    for t in range(TILES + 1):
        if t < TILES:
            norm_std(act, st, n, t)
        if t > 0:
            norm_keep(act, st, n, turn, t - 1)


def norm_tensor(pe, st, n, turn, t, depth=2):
    pe.wait_ge(n.x_ready, n.base + t + 1)
    if t >= depth:
        pe.wait_ge(n.xT_ready, n.base + t - depth + 1)
    for c in range(DC):
        last = pe.transpose(turn[t % 2][:, c, :], st.x[:, t, tile_cols(c)], st.ident[:, :])
    last.then_inc(n.turned, 1)



def self_attention(nc, st, sem, d):
    SCALE = float(HD) ** -0.5
    with Memory(nc) as mem:
        w = [mem.sb(f"sa_w{s}", [P, 3, DC, HD]) for s in range(2)]
        wo = mem.sb("sa_wo", [P, HEADS, DM])
        bias = mem.sb("sa_bias", [P, 3, HEADS])
        headbias = [mem.sb(f"sa_headbias{s}", [P, 2]) for s in range(2)]
        bo = mem.sb("sa_bo", [P, DM])
        maskf = mem.sb("sa_maskf", [P, P])
        qT = [mem.sb(f"sa_qT{s}", [P, TOK]) for s in range(2)]
        kT = [mem.sb(f"sa_kT{s}", [P, TOK]) for s in range(2)]
        v = [mem.sb(f"sa_v{s}", [P, TILES, HD]) for s in range(2)]
        probs = mem.sb("sa_probs", [P, 3 * BANK])
        probsT = mem.sb("sa_probsT", [P, 2, 3 * P])
        negmax = mem.sb("sa_negmax", [P, 8])
        rowsum = mem.sb("sa_rowsum", [P, 8])
        rinv = mem.sb("sa_rinv", [P, 8])
        zT = mem.sb("sa_zT", [P, HEADS, TOK])
        proj = [mem.psum(f"sa_proj{i}", [P, BANK]) for i in range(2)]
        score = [mem.psum(f"sa_score{i}", [P, BANK]) for i in range(3)]
        turn = [mem.psum(f"sa_turn{i}", [P, BANK]) for i in range(2)]
        zbank = mem.psum("sa_z", [P, BANK])
        zout = [zbank, score[0]]

        w_loaded = [sem(f"sa_w_loaded{s}") for s in range(2)]
        rest_loaded = sem("sa_rest_loaded")
        consts_loaded = sem("sa_consts_loaded")
        bq_scaled = sem("sa_bq_scaled")
        bo_added = sem("sa_bo_added")
        proj_ready = sem("sa_proj_ready")
        qk_ready = sem("sa_qk_ready")
        v_ready = sem("sa_v_ready")
        score_ready = sem("sa_score_ready")
        max_ready = sem("sa_max_ready")
        exp_ready = sem("sa_exp_ready")
        rinv_ready = sem("sa_rinv_ready")
        probs_ready = sem("sa_probs_ready")
        turn_ready = sem("sa_turn_ready")
        probsT_even = sem("sa_probsT_even")
        probsT_odd = sem("sa_probsT_odd")
        hb_ready = sem("sa_headbias_ready")
        z_ready = sem("sa_z_ready")
        zT_ready = sem("sa_zT_ready")
        n = norm_tensors(mem, st, "sa")
        out_part = lambda t: [score[1], score[2], proj[0], proj[1]][t % 4][:, 0:DM]
        turns = [turn[i][:, 0:DM].rearrange("p (c n) -> p c n", c=DC) for i in range(2)]

        def score_cols(b, q):
            return (0, b * P, P) if q == 0 else (1 + b // 2, (b % 2) * SEQ, SEQ)

        with nc.Block() as block:
            @block.sync
            def _(sp):
                sp.dma_start(st.xT[:, :, :], d["xT"]).then_inc(st.xT_loaded, 16)
                sp.dma_start(w[0][:], d["sa_w"][0]).then_inc(w_loaded[0], 16)
                sp.dma_start(bias[:], d["sa_bias"]).then_inc(rest_loaded, 16)
                sp.dma_start(maskf[:], d["mask"]).then_inc(consts_loaded, 16)
                sp.dma_start(st.ident[:], d["ident"]).then_inc(consts_loaded, 16)
                sp.dma_start(w[1][:], d["sa_w"][1]).then_inc(w_loaded[1], 16)
                sp.dma_start(st.x[:], d["x"]).then_inc(rest_loaded, 16)
                sp.dma_start(bo[:], d["sa_bo"].partition_broadcast(P)).then_inc(rest_loaded, 16)
                sp.dma_start(wo[:], d["sa_wo"]).then_inc(rest_loaded, 16)
                with sp.Fori(0, HEADS // 2 - 1) as i:
                    for s in range(2):
                        sp.wait_ge(proj_ready, 12 * i + 6 * s + 6)
                        sp.dma_start(w[s][:], d["sa_w"][2 * i + 2 + s]).then_inc(w_loaded[s], 16)

            @block.gpsimd
            def _(pool):
                pool.wait_ge(consts_loaded, 32)
                pool.tensor_copy(st.identb[:], st.ident[:]).then_inc(st.consts_ready, 1)
                pool.tensor_copy(st.mask[:], maskf[:]).then_inc(st.consts_ready, 1)

            @block.tensor
            def _(pe):
                def project(h, s):
                    for f in range(6):
                        if f == 2:
                            pe.wait_ge(qk_ready, 4 * h + 1)
                        elif f == 3:
                            pe.wait_ge(qk_ready, 4 * h + 2)
                        elif f == 4:
                            pe.wait_ge(qk_ready, 4 * h + 3)
                        elif f == 5:
                            pe.wait_ge(qk_ready, 4 * h + 4)
                        if f < 4:
                            for c in range(DC):
                                last = pe.matmul(proj[f % 2][:, :], w[s][:, f // 2, c, :],
                                                 st.xT[:, c, (f % 2) * BANK:(f % 2 + 1) * BANK],
                                                 start=c == 0, stop=c == DC - 1)
                        else:
                            for j in range(4):
                                for c in range(DC):
                                    last = pe.matmul(proj[f % 2][:, j * HD:(j + 1) * HD],
                                                     st.xT[:, c, tile_cols((f - 4) * 4 + j)], w[s][:, 2, c, :],
                                                     start=c == 0, stop=c == DC - 1)
                        last.then_inc(proj_ready, 1)

                def scores(h, s):
                    pe.wait_ge(qk_ready, 4 * h + 4)
                    wait_past(pe, zT_ready, 2 * h)
                    for bank in range(3):
                        for b in range(BATCH):
                            for q in range(2):
                                at, c0, width = score_cols(b, q)
                                if at != bank:
                                    continue
                                k0 = b * SEQ
                                pe.matmul(score[at][:, c0:c0 + width], qT[s][:, k0 + q * P:k0 + q * P + P],
                                          kT[s][:, k0:k0 + width], start=True, stop=False)
                                last = pe.matmul(score[at][:, c0 + width - P:c0 + width], st.identb[:], st.mask[:],
                                                 start=False, stop=True)
                        last.then_inc(score_ready, 1)

                def turn_probs(h, b):
                    pe.wait_ge(probs_ready, 8 * h + 5 + b)
                    if b == 2:
                        pe.wait_ge(probsT_even, 2 * h + 1)
                    if b == 3:
                        pe.wait_ge(probsT_odd, 2 * h + 1)
                    o = turn[b % 2]
                    pe.transpose(o[:, 0:P], probs[:, b * P:(b + 1) * P], st.ident[:])
                    c0 = BANK + b * SEQ
                    pe.transpose(o[:, P:2 * P], probs[:, c0:c0 + P], st.ident[:])
                    pe.transpose(o[:, 2 * P:3 * P], probs[:, c0 + P:c0 + 2 * P], st.ident[:]).then_inc(turn_ready, 1)

                def weigh(h, s, b):
                    if b == 0:
                        pe.wait_ge(v_ready, 2 * h + 2)
                        wait_past(pe, zT_ready, 2 * h)
                    pe.wait_ge((probsT_even, probsT_odd)[b % 2], 2 * h + b // 2 + 1)
                    z = zout[b // 2][:, (b % 2) * SEQ:(b % 2 + 1) * SEQ]
                    pe.matmul(z, v[s][:, 2 * b, :], probsT[:, b % 2, 0:2 * P], start=True, stop=False)
                    last = pe.matmul(z[:, P:2 * P], v[s][:, 2 * b + 1, :], probsT[:, b % 2, 2 * P:3 * P],
                                     start=False, stop=True)
                    if b % 2:
                        last.then_inc(z_ready, 1)

                def attend(h, s):
                    turn_probs(h, 0)
                    turn_probs(h, 1)
                    weigh(h, s, 0)
                    turn_probs(h, 2)
                    weigh(h, s, 1)
                    turn_probs(h, 3)
                    weigh(h, s, 2)
                    weigh(h, s, 3)

                def project_next(h, s, loads):
                    pe.wait_ge(w_loaded[s], 16 * loads)
                    pe.wait_ge(v_ready, 2 * h)
                    project(h, s)

                pe.wait_ge(st.xT_loaded, 16)
                pe.wait_ge(w_loaded[0], 16)
                project(0, 0)
                pe.wait_ge(rest_loaded, 16 * 4)
                pe.wait_ge(consts_loaded, 32)
                pe.wait_ge(st.consts_ready, 2)

                def two_heads(i):
                    scores(2 * i, 0)
                    project_next(2 * i + 1, 1, i + 1)
                    attend(2 * i, 0)
                    scores(2 * i + 1, 1)
                    project_next(2 * i + 2, 0, i + 2)
                    attend(2 * i + 1, 1)

                two_heads(0)
                with pe.Fori(1, HEADS // 2 - 1) as i:
                    two_heads(i)
                h = HEADS - 2
                scores(h, 0)
                project_next(h + 1, 1, HEADS // 2)
                attend(h, 0)
                scores(h + 1, 1)
                attend(h + 1, 1)
                pe.wait_ge(zT_ready, 2 * HEADS)
                for t in range(TILES):
                    if t >= 4:
                        pe.wait_ge(n.summed, n.base + t - 3)
                    for g in range(HEADS):
                        last = pe.matmul(out_part(t), zT[:, g, tile_cols(t)], wo[:, g, :],
                                         start=g == 0, stop=g == HEADS - 1)
                    last.then_inc(n.out_ready, 1)
                    if t >= 2:
                        norm_tensor(pe, st, n, turns, t - 2)
                norm_tensor(pe, st, n, turns, TILES - 2)
                norm_tensor(pe, st, n, turns, TILES - 1)

            @block.scalar
            def _(act):
                def keep_qk(h, s, f):
                    act.wait_ge(proj_ready, 6 * h + f + 1)
                    act.wait_ge(hb_ready, h + 1)
                    dst = (qT if f < 2 else kT)[s][:, (f % 2) * BANK:(f % 2 + 1) * BANK]
                    act.activation(dst, proj[f % 2][:, :], ACT.Identity, bias=headbias[s][:, f // 2:f // 2 + 1],
                                   scale=SCALE if f < 2 else 1.0).then_inc(qk_ready, 1)

                def exps(h, bank):
                    act.wait_ge(max_ready, 3 * h + bank + 1)
                    for j in range(4) if bank == 0 else range(2 * bank + 2, 2 * bank + 4):
                        width = P if bank == 0 else SEQ
                        c0 = j * P if bank == 0 else (j % 2) * SEQ
                        act.activation(probs[:, bank * BANK + c0:bank * BANK + c0 + width],
                                       score[bank][:, c0:c0 + width], ACT.Exp, bias=negmax[:, j:j + 1],
                                       accum_out=rowsum[:, j:j + 1]).then_inc(exp_ready, 1)

                def keep_turned(h, b):
                    act.wait_ge(turn_ready, 4 * h + b + 1)
                    act.activation(probsT[:, b % 2, :], turn[b % 2][:, 0:3 * P], ACT.Copy).then_inc(probsT_odd, 1)

                for f in range(4):
                    keep_qk(0, 0, f)

                def head(h, s, more):
                    for bank in range(3):
                        if more:
                            keep_qk(h + 1, 1 - s, bank)
                        exps(h, bank)
                    if more:
                        keep_qk(h + 1, 1 - s, 3)
                    keep_turned(h, 1)
                    keep_turned(h, 3)

                with act.Fori(0, HEADS // 2 - 1) as i:
                    head(2 * i, 0, True)
                    head(2 * i + 1, 1, True)
                head(HEADS - 2, 0, True)
                head(HEADS - 1, 1, False)
                norm_scalar(act, st, n, turns)

            @block.vector
            def _(dve):
                dve.memset(st.eps[:], LN_EPS)
                dve.wait_ge(rest_loaded, 16 * 4)
                dve.tensor_scalar(bias[:, 0, :], bias[:, 0, :], SCALE, None, ALU.mult).then_inc(bq_scaled, 1)

                def keep_v(h, s, j):
                    dve.wait_ge(proj_ready, 6 * h + 5 + j)
                    dve.tensor_copy(v[s][:, 4 * j:4 * j + 4, :].rearrange("p t e -> p (t e)"),
                                    proj[j][:, :]).then_inc(v_ready, 1)

                def head_bias(h, s):
                    dve.tensor_copy(headbias[s][:, :].unsqueeze(2), bias[:, 0:2, bass.ds(h, 1)]).then_inc(hb_ready, 1)

                def head(h, s, more):
                    if more:
                        head_bias(h + 1, 1 - s)
                    for bank in range(3):
                        groups, first = (4, 0) if bank == 0 else (2, 2 * bank + 2)
                        dve.wait_ge(score_ready, 3 * h + bank + 1)
                        dve.tensor_reduce(negmax[:, first:first + groups],
                                          score[bank][:, :].rearrange("p (g k) -> p g k", g=groups),
                                          X_AXIS, ALU.max, negate=True).then_inc(max_ready, 1)
                    for bank in range(3):
                        groups, first = (4, 0) if bank == 0 else (2, 2 * bank + 2)
                        width = BANK // groups
                        dve.wait_ge(exp_ready, 8 * h + first + groups)
                        dve.reciprocal(rinv[:, first:first + groups],
                                       rowsum[:, first:first + groups]).then_inc(rinv_ready, 1)
                        dve.wait_ge(rinv_ready, 3 * h + bank + 1)
                        for g in range(groups):
                            part = probs[:, bank * BANK + g * width:bank * BANK + (g + 1) * width]
                            dve.tensor_scalar(part, part, rinv[:, first + g:first + g + 1], None,
                                              ALU.mult).then_inc(probs_ready, 1)
                    if more:
                        keep_v(h + 1, 1 - s, 0)
                        keep_v(h + 1, 1 - s, 1)
                    for p in range(2):
                        dve.wait_ge(turn_ready, 4 * h + 2 * p + 1)
                        dve.tensor_copy(probsT[:, 0, :], turn[0][:, 0:3 * P]).then_inc(probsT_even, 1)
                    for p in range(2):
                        dve.wait_ge(z_ready, 2 * h + p + 1)
                        dve.tensor_scalar(zT[:, bass.ds(h, 1), p * BANK:(p + 1) * BANK], zout[p][:, :].unsqueeze(1),
                                          bias[:, 2, bass.ds(h, 1)], None, ALU.add).then_inc(zT_ready, 1)

                dve.wait_ge(bq_scaled, 1)
                head_bias(0, 0)
                keep_v(0, 0, 0)
                keep_v(0, 0, 1)
                with dve.Fori(0, HEADS // 2 - 1) as i:
                    head(2 * i, 0, True)
                    head(2 * i + 1, 1, True)
                head(HEADS - 2, 0, True)
                head(HEADS - 1, 1, False)
                for t in range(TILES):
                    last = dve.tensor_tensor(st.x[:, t, :], st.x[:, t, :], bo[:, :], ALU.add)
                last.then_inc(bo_added, 1)
                dve.wait_ge(bo_added, 1)
                norm_vector(dve, st, n, out_part)



PAIRS = HEADS // 2


def cross_tensors(mem, sem, name, vw=None):
    class C:
        pass
    c = C()
    c.rows = mem.sb(f"{name}_rows", [P, TILES, HEADS, KEYS])
    c.vw = vw if vw is not None else mem.sb(f"{name}_vw", [P, BATCH, PAIRS, DM])
    c.max = mem.sb(f"{name}_max", [P, TILES, HEADS])
    c.sum = mem.sb(f"{name}_sum", [P, TILES, HEADS])
    c.inv = mem.sb(f"{name}_inv", [P, TILES, HEADS])
    c.rowsT = mem.sb(f"{name}_rowsT", [P, 2, PAIRS, P])
    c.max_ready = sem(f"{name}_max_ready")
    c.shifted = sem(f"{name}_shifted")
    c.exp_ready = sem(f"{name}_exp_ready")
    c.sum_ready = sem(f"{name}_sum_ready")
    c.inv_ready = sem(f"{name}_inv_ready")
    c.probs_ready = sem(f"{name}_probs_ready")
    c.turned = sem(f"{name}_rows_turned")
    c.rowsT_ready = sem(f"{name}_rowsT_ready")
    return c


def over_keys(a):
    return a.unsqueeze(2).broadcast_to([P, a.shape[1], KEYS])


def cross_normalise_sum(dve, c, t):
    dve.wait_ge(c.exp_ready, t + 1)
    dve.tensor_reduce(c.sum[:, t, :], c.rows[:, t, :, :], X_AXIS, ALU.add).then_inc(c.sum_ready, 1)
    dve.wait_ge(c.sum_ready, t + 1)
    dve.reciprocal(c.inv[:, t, :], c.sum[:, t, :]).then_inc(c.inv_ready, 1)


def cross_exp(act, c, t):
    act.wait_ge(c.shifted, t + 1)
    act.activation(c.rows[:, t, :, :], c.rows[:, t, :, :], ACT.Exp).then_inc(c.exp_ready, 1)


def cross_weights(pool, c, t):
    pool.wait_ge(c.inv_ready, t + 1)
    pool.tensor_tensor(c.rows[:, t, :, :], c.rows[:, t, :, :], over_keys(c.inv[:, t, :]),
                       ALU.mult).then_inc(c.probs_ready, 1)


def cross_turn(pe, st, c, turn, t):
    pe.wait_ge(c.probs_ready, t + 1)
    if t >= 1:
        pe.wait_ge(c.rowsT_ready, 2 * t)
    for g in range(PAIRS):
        last = pe.transpose(turn[g // 4][:, (g % 4) * P:(g % 4 + 1) * P],
                            c.rows[:, t, 2 * g:2 * g + 2, :].rearrange("p h k -> p (h k)"), st.ident[:])
        if g % 4 == 3:
            last.then_inc(c.turned, 1)


def cross_keep(act, c, turn, t):
    for j in range(2):
        act.wait_ge(c.turned, 2 * t + j + 1)
        act.activation(c.rowsT[:, t % 2, 4 * j:4 * j + 4, :],
                       turn[j][:, :].rearrange("p (g n) -> p g n", g=4), ACT.Copy).then_inc(c.rowsT_ready, 1)


def cross_out(pe, c, n, part, t):
    pe.wait_ge(c.rowsT_ready, 2 * t + 2)
    if t >= 2:
        pe.wait_ge(n.summed, n.base + t - 1)
    for g in range(PAIRS):
        last = pe.matmul(part(t), c.rowsT[:, t % 2, g, :], c.vw[:, t // 2, g, :],
                         start=g == 0, stop=g == PAIRS - 1)
    last.then_inc(n.out_ready, 1)



def context_attention(nc, st, sem, d):
    SCALE = float(HD) ** -0.5
    KV = 4
    GROUP = HEADS // KV
    with Memory(nc) as mem:
        c = cross_tensors(mem, sem, "ca")
        w = [mem.sb(f"ca_w{s}", [P, DC, HD]) for s in range(2)]
        wo = mem.sb("ca_wo", [P, HEADS, DM])
        wk = mem.sb("ca_wk", [P, DC, KV * HD])
        wv = mem.sb("ca_wv", [P, DC, KV * HD])
        bk = mem.sb("ca_bk", [P, KV * HD])
        bq = mem.sb("ca_bq", [P, HEADS])
        bv = mem.sb("ca_bv", [P, KV])
        norms = mem.sb("ca_norms", [P, 2])
        gain = mem.sb("ca_gain", [P, 1])
        amask = mem.sb("ca_amask", [P, 2, KEYS])
        ones = mem.sb("ca_ones", [P, 1])
        rms_eps = mem.sb("ca_rms_eps", [P, 1])
        k = mem.sb("ca_k", [P, 2, KV * HD])
        ksq = mem.sb("ca_ksq", [P, 2, KV * HD])
        kss = mem.sb("ca_kss", [P, 2 * KV])
        kstd = mem.sb("ca_kstd", [P, 2 * KV])
        krms = mem.sb("ca_krms", [P, 2 * KV])
        kT = mem.sb("ca_kT", [P, KV, CTX])
        vT = mem.sb("ca_vT", [P, KV, CTX])
        qT = [mem.sb(f"ca_qT{s}", [P, TOK]) for s in range(2)]
        qsq = [mem.sb(f"ca_qsq{s}", [P, TOK]) for s in range(2)]
        qstd = mem.sb("ca_qstd", [P, 2, TILES])
        qrms = mem.sb("ca_qrms", [P, 2, TILES])
        proj = [mem.psum(f"ca_proj{i}", [P, BANK]) for i in range(4)]
        score = [mem.psum(f"ca_score{i}", [P, BANK]) for i in range(2)]
        square = [mem.psum(f"ca_square{i}", [P, BANK]) for i in range(2)]
        n = norm_tensors(mem, st, "ca")
        part = lambda t: score[t % 2][:, 0:DM]
        turns = [square[i][:, 0:DM].rearrange("p (c n) -> p c n", c=DC) for i in range(2)]

        w_loaded = [sem(f"ca_w_loaded{s}") for s in range(2)]
        kv_loaded = sem("ca_kv_loaded")
        wo_loaded = sem("ca_wo_loaded")
        k_projected = sem("ca_k_projected")
        v_projected = sem("ca_v_projected")
        k_biased = sem("ca_k_biased")
        k_squared = sem("ca_k_squared")
        k_summed = sem("ca_k_summed")
        k_std = sem("ca_k_std")
        k_rms = sem("ca_k_rms")
        k_normed = sem("ca_k_normed")
        k_turned = sem("ca_k_turned")
        kT_ready = sem("ca_kT_ready")
        vT_ready = sem("ca_vT_ready")
        vw_done = sem("ca_vw_done")
        vw_ready = sem("ca_vw_ready")
        consts_ready = sem("ca_consts_ready")
        q_projected = sem("ca_q_projected")
        q_ready = sem("ca_q_ready")
        qsq_ready = sem("ca_qsq_ready")
        scored = sem("ca_scored")
        qstd_ready = sem("ca_qstd_ready")
        qrms_ready = sem("ca_qrms_ready")
        scaled = sem("ca_scaled")
        masked = sem("ca_masked")

        with nc.Block() as block:
            @block.sync
            def _(sp):
                for dst, src in ((st.ctxT[:], "ctxT"), (wk[:], "ca_wk"), (wv[:], "ca_wv"), (bv[:], "ca_bv"),
                                 (norms[:], "ca_norms"), (bq[:], "ca_bq"), (amask[:], "ca_amask")):
                    sp.dma_start(dst, d[src]).then_inc(kv_loaded, 16)
                sp.dma_start(bk[:], d["ca_bk"].partition_broadcast(P)).then_inc(kv_loaded, 16)
                sp.dma_start(w[0][:], d["ca_wq"][0]).then_inc(w_loaded[0], 16)
                sp.dma_start(w[1][:], d["ca_wq"][1]).then_inc(w_loaded[1], 16)
                sp.dma_start(wo[:], d["ca_wo"]).then_inc(wo_loaded, 16)
                def load(i, u):
                    sp.wait_ge(q_projected, 8 * i + 2 * u + 2)
                    sp.dma_start(w[u % 2][:], d["ca_wq"][4 * i + u + 2]).then_inc(w_loaded[u % 2], 16)
                with sp.Fori(0, KV - 1) as i:
                    for u in range(GROUP):
                        load(i, u)
                load(KV - 1, 0)
                load(KV - 1, 1)

            @block.tensor
            def _(pe):
                pe.wait_ge(kv_loaded, 16 * 8)
                for t in range(2):
                    for j in range(DC):
                        last = pe.matmul(proj[t][:, :], st.ctxT[:, j, tile_cols(t)], wk[:, j, :],
                                         start=j == 0, stop=j == DC - 1)
                    last.then_inc(k_projected, 1)
                for g in range(KV):
                    for j in range(DC):
                        last = pe.matmul(proj[2 + g // 2][:, (g % 2) * CTX:(g % 2 + 1) * CTX],
                                         wv[:, j, g * HD:(g + 1) * HD], st.ctxT[:, j, :],
                                         start=j == 0, stop=j == DC - 1)
                    if g % 2:
                        last.then_inc(v_projected, 1)
                pe.wait_ge(k_normed, 1)
                for g in range(KV):
                    for t in range(2):
                        last = pe.transpose(square[g // 2][:, (g % 2) * CTX + t * P:(g % 2) * CTX + (t + 1) * P],
                                            k[:, t, g * HD:(g + 1) * HD], st.ident[:])
                    if g % 2:
                        last.then_inc(k_turned, 1)
                pe.wait_ge(vT_ready, 2)
                pe.wait_ge(wo_loaded, 16)
                for r in range(2 * PAIRS):
                    pair, half = r // 2, r % 2
                    if r >= 2:
                        pe.wait_ge(vw_ready, r - 1)
                    for b in range(2):
                        for s in range(2):
                            h = 2 * pair + s
                            last = pe.matmul(score[r % 2][s * KEYS:(s + 1) * KEYS, b * DM:(b + 1) * DM],
                                             vT[:, h // GROUP, (2 * half + b) * KEYS:(2 * half + b + 1) * KEYS],
                                             wo[:, h, :], start=True, stop=True)
                    last.then_inc(vw_done, 1)

                def project(h, s, loads):
                    pe.wait_ge(w_loaded[s], 16 * loads)
                    for f in range(2):
                        for j in range(DC):
                            last = pe.matmul(proj[2 * s + f][:, :], w[s][:, j, :],
                                             st.xT[:, j, f * BANK:(f + 1) * BANK],
                                             start=j == 0, stop=j == DC - 1)
                        last.then_inc(q_projected, 1)

                def scores(h, i, s):
                    pe.wait_ge(q_ready, 2 * h + 2)
                    pe.wait_ge(qsq_ready, 2 * h + 2)
                    for t in range(TILES):
                        pe.matmul(square[s][:, t:t + 1], qsq[s][:, tile_cols(t)], ones[:, :], start=True, stop=True)
                    for t in range(TILES):
                        last = pe.matmul(score[s][:, t * KEYS:(t + 1) * KEYS], qT[s][:, tile_cols(t)],
                                         kT[:, bass.ds(i, 1), (t // 2) * KEYS:(t // 2 + 1) * KEYS].squeeze(1),
                                         start=True, stop=True)
                    last.then_inc(scored, 1)

                pe.wait_ge(kT_ready, 2)
                pe.wait_ge(k_biased, 2)
                pe.wait_ge(vw_ready, 2 * PAIRS)
                project(0, 0, 1)
                def early(u):
                    project(u + 1, (u + 1) % 2, (u + 1) // 2 + 1)
                    scores(u, 0, u % 2)
                early(0)
                early(1)
                def later(i, u, more=True):
                    h = 4 * i + u
                    if more:
                        project(h + 1, (u + 1) % 2, 2 * i + (u + 1) // 2 + 1)
                    pe.wait_ge(scaled, h - 1)
                    scores(h, i, u % 2)
                for u in range(2, GROUP):
                    later(0, u)
                with pe.Fori(1, KV - 1) as i:
                    for u in range(GROUP):
                        later(i, u)
                for u in range(GROUP):
                    later(KV - 1, u, u < GROUP - 1)
                pe.wait_ge(scaled, HEADS)
                for t in range(TILES + 2):
                    if t < TILES:
                        cross_turn(pe, st, c, proj[0:2], t)
                    if 0 <= t - 1 < TILES:
                        cross_out(pe, c, n, part, t - 1)
                    if t >= 3:
                        norm_tensor(pe, st, n, turns, t - 3)
                norm_tensor(pe, st, n, turns, TILES - 1)

            @block.scalar
            def _(act):
                act.wait_ge(consts_ready, 1)
                for j in range(2):
                    act.wait_ge(v_projected, j + 1)
                    for g in range(2 * j, 2 * j + 2):
                        last = act.activation(vT[:, g, :], proj[2 + j][:, (g % 2) * CTX:(g % 2 + 1) * CTX],
                                              ACT.Identity, bias=bv[:, g:g + 1])
                    last.then_inc(vT_ready, 1)
                act.wait_ge(k_summed, 1)
                act.activation(kstd[:, :], kss[:, :], ACT.Sqrt, bias=rms_eps[:, :],
                               scale=1.0 / HD).then_inc(k_std, 1)
                for j in range(2):
                    act.wait_ge(k_turned, j + 1)
                    act.activation(kT[:, 2 * j:2 * j + 2, :], square[j][:, :].rearrange("p (g n) -> p g n", g=2),
                                   ACT.Copy, scale=gain[:, :]).then_inc(kT_ready, 1)

                def squares(h, s):
                    for f in range(2):
                        act.wait_ge(q_ready, 2 * h + f + 1)
                        act.activation(qsq[s][:, f * BANK:(f + 1) * BANK], qT[s][:, f * BANK:(f + 1) * BANK],
                                       ACT.Square).then_inc(qsq_ready, 1)

                def q_std(h, s):
                    act.wait_ge(scored, h + 1)
                    act.activation(qstd[:, s, :], square[s][:, 0:TILES], ACT.Sqrt, bias=rms_eps[:, :],
                                   scale=1.0 / HD).then_inc(qstd_ready, 1)

                squares(0, 0)
                def head(i, u, more=True):
                    if more:
                        squares(4 * i + u + 1, (u + 1) % 2)
                    q_std(4 * i + u, u % 2)
                with act.Fori(0, KV - 1) as i:
                    for u in range(GROUP):
                        head(i, u)
                for u in range(GROUP):
                    head(KV - 1, u, u < GROUP - 1)
                for t in range(TILES + 4):
                    if t < TILES:
                        cross_exp(act, c, t)
                    if 0 <= t - 1 < TILES:
                        cross_keep(act, c, proj[0:2], t - 1)
                    if 0 <= t - 2 < TILES:
                        norm_std(act, st, n, t - 2)
                    if 0 <= t - 4:
                        norm_keep(act, st, n, turns, t - 4)

            @block.vector
            def _(dve):
                dve.memset(ones[:], 1.0)
                dve.memset(rms_eps[:], 1e-6)
                dve.wait_ge(kv_loaded, 16 * 8)
                dve.scalar_tensor_tensor(gain[:], norms[:, 0:1], SCALE, norms[:, 1:2],
                                         ALU.mult, ALU.mult).then_inc(consts_ready, 1)
                for t in range(2):
                    dve.wait_ge(k_projected, t + 1)
                    dve.tensor_tensor(k[:, t, :], proj[t][:, :], bk[:, :], ALU.add).then_inc(k_biased, 1)
                dve.wait_ge(k_biased, 2)
                dve.tensor_tensor(ksq[:], k[:], k[:], ALU.mult).then_inc(k_squared, 1)
                dve.wait_ge(k_squared, 1)
                dve.tensor_reduce(kss[:, :], ksq[:].rearrange("p t (g e) -> p (t g) e", g=KV),
                                  X_AXIS, ALU.add).then_inc(k_summed, 1)
                dve.wait_ge(k_std, 1)
                dve.reciprocal(krms[:, :], kstd[:, :]).then_inc(k_rms, 1)
                dve.wait_ge(k_rms, 1)
                kk = k[:].rearrange("p t (g e) -> p (t g) e", g=KV)
                dve.tensor_tensor(kk, kk, krms[:, :].unsqueeze(2).broadcast_to([P, 2 * KV, HD]),
                                  ALU.mult).then_inc(k_normed, 1)
                for r in range(2 * PAIRS):
                    dve.wait_ge(vw_done, r + 1)
                    dve.tensor_copy(c.vw[:, 2 * (r % 2):2 * (r % 2) + 2, r // 2, :],
                                    score[r % 2][:, :].rearrange("p (b n) -> p b n", b=2)).then_inc(vw_ready, 1)

                def keep_q(h, s):
                    for f in range(2):
                        dve.wait_ge(q_projected, 2 * h + f + 1)
                        dve.tensor_scalar(qT[s][:, f * BANK:(f + 1) * BANK], proj[2 * s + f][:, :],
                                          bq[:, bass.ds(h, 1)], None, ALU.add).then_inc(q_ready, 1)

                def scale_scores(h, s):
                    dve.wait_ge(qstd_ready, h + 1)
                    dve.reciprocal(qrms[:, s, :], qstd[:, s, :]).then_inc(qrms_ready, 1)
                    dve.wait_ge(qrms_ready, h + 1)
                    dve.tensor_tensor(c.rows[:, :, bass.ds(h, 1), :].squeeze(2),
                                      score[s][:, :].rearrange("p (t k) -> p t k", t=TILES),
                                      over_keys(qrms[:, s, :]), ALU.mult).then_inc(scaled, 1)

                keep_q(0, 0)
                keep_q(1, 1)
                def head(i, u, more=True):
                    h = 4 * i + u
                    scale_scores(h, u % 2)
                    if more:
                        keep_q(h + 2, u % 2)
                with dve.Fori(0, KV - 1) as i:
                    for u in range(GROUP):
                        head(i, u)
                for u in range(GROUP):
                    head(KV - 1, u, u < 2)
                for t in range(TILES + 3):
                    if t < TILES:
                        dve.wait_ge(masked, t + 1)
                        dve.tensor_reduce(c.max[:, t, :], c.rows[:, t, :, :], X_AXIS,
                                          ALU.max).then_inc(c.max_ready, 1)
                        dve.wait_ge(c.max_ready, t + 1)
                        dve.tensor_tensor(c.rows[:, t, :, :], c.rows[:, t, :, :], over_keys(c.max[:, t, :]),
                                          ALU.subtract).then_inc(c.shifted, 1)
                        cross_normalise_sum(dve, c, t)
                    if 0 <= t - 2 < TILES:
                        norm_sum(dve, st, n, part, t - 2)
                    if 0 <= t - 3:
                        norm_apply(dve, st, n, t - 3)

            @block.gpsimd
            def _(pool):
                pool.wait_ge(scaled, HEADS)
                for t in range(TILES + 1):
                    if t < TILES:
                        pool.tensor_tensor(c.rows[:, t, :, :], c.rows[:, t, :, :],
                                           amask[:, t % 2, :].unsqueeze(1).broadcast_to([P, HEADS, KEYS]),
                                           ALU.add).then_inc(masked, 1)
                    if t > 0:
                        cross_weights(pool, c, t - 1)



VD = DM // HEADS
VCOLS = VD + 1


def recurrent_attention(nc, st, sem, d):
    name = "ra"
    COUNT = HEADS // 2
    with Memory(nc) as mem:
        wq = mem.sb(f"{name}_wq", [P, DC, DM])
        wk = mem.sb(f"{name}_wk", [P, DC, DM])
        wv = mem.sb(f"{name}_wv", [P, DC, DM])
        wo = mem.sb(f"{name}_wo", [P, DC, DM])
        rowmask = mem.sb(f"{name}_rowmask", [P, COUNT])
        qT = mem.sb(f"{name}_qT", [P, 2, TOK])
        kT = mem.sb(f"{name}_kT", [P, 2, TOK])
        qhead = [mem.sb(f"{name}_qhead{s}", [P, TOK]) for s in range(2)]
        v = mem.sb(f"{name}_v", [P, TILES, HEADS, VCOLS])
        shift = mem.sb(f"{name}_shift", [P, 4, 2])
        probs = mem.sb(f"{name}_probs", [P, 4, BANK])
        probsT = mem.sb(f"{name}_probsT", [P, 2, BANK])
        heads_out = mem.sb(f"{name}_heads_out", [P, TILES, 2, COUNT, VCOLS])
        y = mem.sb(f"{name}_y", [P, TILES, DM])
        rinv = mem.sb(f"{name}_rinv", [P, TILES, 2 * COUNT])
        yT = mem.sb(f"{name}_yT", [P, 2, DC, P])
        score = [mem.psum(f"{name}_score{i}", [P, BANK]) for i in range(4)]
        turn = [mem.psum(f"{name}_turn{i}", [P, BANK]) for i in range(2)]
        out = [mem.psum(f"{name}_out{i}", [P, BANK]) for i in range(2)]
        n = norm_tensors(mem, st, name)

        loaded = sem(f"{name}_loaded")
        consts_ready = sem(f"{name}_consts_ready")
        q_projected = sem(f"{name}_q_projected")
        k_projected = sem(f"{name}_k_projected")
        v_projected = sem(f"{name}_v_projected")
        crossed = sem(f"{name}_crossed")
        qk_ready = sem(f"{name}_qk_ready")
        v_ready = sem(f"{name}_v_ready")
        qhead_ready = sem(f"{name}_qhead_ready")
        scored = sem(f"{name}_scored")
        shift_ready = sem(f"{name}_shift_ready")
        exp_ready = sem(f"{name}_exp_ready")
        probs_turned = sem(f"{name}_probs_turned")
        probsT_even = sem(f"{name}_probsT_even")
        probsT_odd = sem(f"{name}_probsT_odd")
        weighed = sem(f"{name}_weighed")
        heads_kept = sem(f"{name}_heads_kept")
        chain = sem(f"{name}_chain")
        y_ready = sem(f"{name}_y_ready")
        y_turned = sem(f"{name}_y_turned")
        yT_ready = sem(f"{name}_yT_ready")

        part = lambda t: score[t % 2][:, 0:DM]
        yturn = [out[i][:, 0:DM].rearrange("p (c n) -> p c n", c=DC) for i in range(2)]
        turns = [turn[i][:, 0:DM].rearrange("p (c n) -> p c n", c=DC) for i in range(2)]
        widths = (P, SEQ)
        block_at = {(0, 0): 0, (0, 1): P, (1, 1): 2 * P}
        turned_cols = P * len(block_at)

        roww = mem.sb(f"{name}_roww", [P, 3, 2])
        rowscale = mem.sb(f"{name}_rowscale", [P, 2])
        swap = mem.sb(f"{name}_swap", [P, 2])
        factors = mem.sb(f"{name}_factors", [P, 4, 2])
        cross = mem.sb(f"{name}_cross", [P, 4, BANK])
        n_loads = 6

        def ahead(i, u, lead):
            return (i, u + lead) if u + lead < 8 else (i + 1, u + lead - 8)

        with nc.Block() as block:
            @block.sync
            def _(sp):
                for dst, src in [(wq, f"{name}_wq"), (wk, f"{name}_wk"), (wv, f"{name}_wv"), (wo, f"{name}_wo"),
                                 (rowmask, f"{name}_rowmask"), (roww, f"{name}_roww")]:
                    sp.dma_start(dst[:], d[src]).then_inc(loaded, 16)

            @block.tensor
            def _(pe):
                pe.wait_ge(loaded, 16 * n_loads)
                for j in range(4):
                    s, f = j // 2, j % 2
                    for w, banks, ready in ((wq, score[0:2], q_projected), (wk, score[2:4], k_projected)):
                        if j >= 2 and w is wq:
                            pe.wait_ge(qk_ready, 2 * (j - 2) + 2)
                        for c in range(DC):
                            last = pe.matmul(banks[j % 2][:, :], w[:, c, tile_cols(s)],
                                             st.xT[:, c, f * BANK:(f + 1) * BANK], start=c == 0, stop=c == DC - 1)
                        last.then_inc(ready, 1)
                for t in range(TILES):
                    if t >= 2:
                        pe.wait_ge(v_ready, t - 1)
                    for c in range(DC):
                        last = pe.matmul(turn[t % 2][:, 0:DM], st.xT[:, c, tile_cols(t)], wv[:, c, :],
                                         start=c == 0, stop=c == DC - 1)
                    last.then_inc(v_projected, 1)

                def scores(i, u):
                    s, b = u // 4, u % 4
                    if b == 0:
                        pe.wait_ge(qhead_ready, 2 * i + s + 1)
                    k0 = b * SEQ
                    for q, width in enumerate(widths):
                        o = score[u % 4][:, q * SEQ:q * SEQ + width]
                        last = pe.matmul(o, qhead[s][:, k0 + q * P:k0 + (q + 1) * P],
                                         kT[:, s, k0:k0 + width], start=True, stop=False)
                        last = pe.matmul(o[:, width - P:width], st.identb[:], st.mask[:], start=False, stop=True)
                    last.then_inc(scored, 1)

                def turn_probs(i, u):
                    unit = 8 * i + u
                    pe.wait_ge(exp_ready, 2 * unit + 2)
                    wait_past(pe, (probsT_even, probsT_odd)[u % 2], 4 * i + u // 2)
                    for (kt, q), at in block_at.items():
                        last = pe.transpose(turn[u % 2][:, at:at + P],
                                            probs[:, u % 4, q * SEQ + kt * P:q * SEQ + (kt + 1) * P], st.ident[:])
                    last.then_inc(probs_turned, 1)

                def weigh(i, u, fresh):
                    s, b = u // 4, u % 4
                    if b == 0 and not fresh:
                        pe.wait_ge(heads_kept, 2 * i + s - 1)
                    pe.wait_ge((probsT_even, probsT_odd)[u % 2], 4 * i + u // 2 + 1)
                    for q in range(2):
                        o = out[s][:, (2 * b + q) * VCOLS:(2 * b + q + 1) * VCOLS]
                        kts = [kt for kt in range(2) if (kt, q) in block_at]
                        for kt in kts:
                            at = block_at[kt, q]
                            values = v[:, 2 * b + kt, bass.ds(s * COUNT + i, 1), :]
                            last = pe.matmul(o, probsT[:, u % 2, at:at + P], values.squeeze(1),
                                             start=kt == 0, stop=kt == kts[-1])
                    if b == 3:
                        last.then_inc(weighed, 1)

                def units(i, first=False, final=False):
                    for u in range(8):
                        if not (final and u + 3 >= 8):
                            scores(*ahead(i, u, 3))
                        turn_probs(i, u)
                        if u > 0:
                            weigh(i, u - 1, first)
                        elif not first:
                            weigh(i - 1, 7, False)

                pe.wait_ge(qk_ready, 8)
                pe.wait_ge(v_ready, TILES)
                for u in range(3):
                    scores(0, u)
                units(0, first=True)
                with pe.Fori(1, COUNT - 1) as i:
                    units(i)
                units(COUNT - 1, final=True)
                weigh(COUNT - 1, 7, False)

                pe.wait_ge(heads_kept, 2 * COUNT)
                for t in range(TILES + 2):
                    if t < TILES:
                        pe.wait_ge(y_ready, t + 1)
                        if t >= 2:
                            pe.wait_ge(yT_ready, t - 1)
                        for c in range(DC):
                            last = pe.transpose(yturn[t % 2][:, c, :], y[:, t, tile_cols(c)], st.ident[:])
                        last.then_inc(y_turned, 1)
                    if 0 <= t - 1 < TILES:
                        r = t - 1
                        pe.wait_ge(yT_ready, r + 1)
                        if r >= 2:
                            pe.wait_ge(n.summed, n.base + r - 1)
                        for c in range(DC):
                            last = pe.matmul(part(r), yT[:, r % 2, c, :], wo[:, c, :], start=c == 0, stop=c == DC - 1)
                        last.then_inc(n.out_ready, 1)
                    if t >= 3:
                        norm_tensor(pe, st, n, turns, t - 3)
                norm_tensor(pe, st, n, turns, TILES - 1)

            @block.scalar
            def _(act):
                act.wait_ge(loaded, 16 * n_loads)
                act.wait_ge(chain, 1)
                act.activation(rowscale[:], roww[:, 0, :], ACT.Sqrt).then_inc(consts_ready, 1)
                act.wait_ge(chain, 7)
                for j in range(4):
                    s = j // 2
                    act.wait_ge(k_projected, j + 1)
                    if j >= 2:
                        act.wait_ge(qk_ready, 2 * (j - 2) + 2)
                    act.activation(cross[:, 2 * (j % 2), :], score[2 + j % 2][:, :], ACT.Copy,
                                   scale=factors[:, 1, s:s + 1]).then_inc(crossed, 1)
                    act.activation(cross[:, 2 * (j % 2) + 1, :], score[j % 2][:, :], ACT.Copy,
                                   scale=factors[:, 3, s:s + 1]).then_inc(crossed, 1)
                for t in range(TILES):
                    act.wait_ge(v_projected, t + 1)
                    act.activation(v[:, t, :, 0:VD], turn[t % 2][:, 0:DM].rearrange("p (h e) -> p h e", h=HEADS),
                                   ACT.Copy).then_inc(v_ready, 1)

                def exps(i, u, fresh=False):
                    unit = 8 * i + u
                    act.wait_ge(shift_ready, 2 * unit + 2)
                    if not fresh:
                        act.wait_ge(probs_turned, unit - 3)
                    for q, width in enumerate(widths):
                        act.activation(probs[:, u % 4, q * SEQ:q * SEQ + width], score[u % 4][:, q * SEQ:q * SEQ + width],
                                       ACT.Exp, bias=shift[:, u % 4, q:q + 1]).then_inc(exp_ready, 1)

                def keep_odd(i, u):
                    act.wait_ge(probs_turned, 8 * i + u + 1)
                    act.activation(probsT[:, 1, 0:turned_cols], turn[1][:, 0:turned_cols],
                                   ACT.Copy).then_inc(probsT_odd, 1)

                def units(i, first=False, final=False):
                    for u in range(8):
                        if not (final and u + 1 >= 8):
                            exps(*ahead(i, u, 1), fresh=first and u + 1 < 4)
                        if u % 2:
                            keep_odd(i, u)

                exps(0, 0, fresh=True)
                units(0, first=True)
                with act.Fori(1, COUNT - 1) as i:
                    units(i)
                units(COUNT - 1, final=True)
                for t in range(TILES + 4):
                    if t < TILES:
                        act.wait_ge(y_turned, t + 1)
                        act.activation(yT[:, t % 2, :, :], yturn[t % 2], ACT.Copy).then_inc(yT_ready, 1)
                    if 0 <= t - 2 < TILES:
                        norm_std(act, st, n, t - 2)
                    if 0 <= t - 4:
                        norm_keep(act, st, n, turns, t - 4)

            @block.vector
            def _(dve):
                links = [0]

                def link(ins):
                    links[0] += 1
                    ins.then_inc(chain, 1)
                    dve.wait_ge(chain, links[0])

                dve.wait_ge(loaded, 16 * n_loads)
                link(dve.tensor_scalar(roww[:, 0, :], roww[:, 0, :], 1e-8, None, ALU.max))
                link(dve.scalar_tensor_tensor(swap[:], roww[:, 1, :], 0.1, roww[:, 2, :], ALU.is_gt, ALU.mult))
                dve.wait_ge(consts_ready, 1)
                link(dve.tensor_tensor(factors[:, 3, :], rowscale[:], swap[:], ALU.mult))
                link(dve.tensor_tensor(factors[:, 2, :], rowscale[:], factors[:, 3, :], ALU.subtract))
                link(dve.tensor_scalar(factors[:, 1, :], factors[:, 3, :], float(VD) ** -0.5, None, ALU.mult))
                link(dve.tensor_scalar(factors[:, 0, :], factors[:, 2, :], float(VD) ** -0.5, None, ALU.mult))
                link(dve.memset(v[:, :, :, VD:VCOLS], 1.0))
                for j in range(4):
                    s, f = j // 2, j % 2
                    cols = slice(f * BANK, (f + 1) * BANK)
                    dve.wait_ge(crossed, 2 * j + 2)
                    dve.scalar_tensor_tensor(qT[:, s, cols], score[j % 2][:, :], factors[:, 0, s:s + 1],
                                             cross[:, 2 * (j % 2), :], ALU.mult, ALU.add).then_inc(qk_ready, 1)
                    dve.scalar_tensor_tensor(kT[:, s, cols], score[2 + j % 2][:, :], factors[:, 2, s:s + 1],
                                             cross[:, 2 * (j % 2) + 1, :], ALU.mult, ALU.add).then_inc(qk_ready, 1)
                dve.wait_ge(qk_ready, 8)

                def mask_q(i, s):
                    dve.tensor_scalar(qhead[s][:, :], qT[:, s, :], rowmask[:, bass.ds(i, 1)], None,
                                      ALU.mult).then_inc(qhead_ready, 1)

                def maxima(i, u, fresh=False):
                    unit = 8 * i + u
                    dve.wait_ge(scored, unit + 1)
                    if not fresh:
                        dve.wait_ge(exp_ready, 2 * unit - 6)
                    for q, width in enumerate(widths):
                        src = score[u % 4][:, q * SEQ:q * SEQ + width]
                        dve.tensor_reduce(shift[:, u % 4, q:q + 1], src, X_AXIS, ALU.max,
                                          negate=True).then_inc(shift_ready, 1)

                def keep_even(i, u):
                    dve.wait_ge(probs_turned, 8 * i + u + 1)
                    dve.tensor_copy(probsT[:, 0, 0:turned_cols], turn[0][:, 0:turned_cols]).then_inc(probsT_even, 1)

                def keep_heads(i, s):
                    dve.wait_ge(weighed, 2 * i + s + 1)
                    dve.tensor_scalar(heads_out[:, :, s, bass.ds(i, 1), :].squeeze(2),
                                      out[s][:, 0:TILES * VCOLS].rearrange("p (t e) -> p t e", t=TILES),
                                      1.0, None, ALU.mult).then_inc(heads_kept, 1)

                def units(i, first=False, final=False):
                    for u in range(8):
                        if not (final and u + 2 >= 8):
                            maxima(*ahead(i, u, 2), fresh=first and u + 2 < 4)
                        if u % 2 == 0:
                            keep_even(i, u)
                        if u == 1 and not first:
                            keep_heads(i - 1, 1)
                        if u in (1, 5) and not final:
                            dve.wait_ge(scored, 8 * i + u + 3)
                            mask_q(i + 1, u // 4)
                        if u == 5:
                            keep_heads(i, 0)

                mask_q(0, 0)
                mask_q(0, 1)
                maxima(0, 0, fresh=True)
                maxima(0, 1, fresh=True)
                units(0, first=True)
                with dve.Fori(1, COUNT - 1) as i:
                    units(i)
                units(COUNT - 1, final=True)
                keep_heads(COUNT - 1, 1)

                dve.wait_ge(heads_kept, 2 * COUNT)
                for t in range(TILES + 3):
                    if t < TILES:
                        o = heads_out[:, t, :, :, :]
                        r = rinv[:, t, :].rearrange("p (s h) -> p s h", s=2)
                        link(dve.reciprocal(r, o[:, :, :, VD]))
                        oo = heads_out[:, t, :, :, 0:VD].rearrange("p s h e -> p (s h) e")
                        dve.tensor_tensor(y[:, t, :].rearrange("p (h e) -> p h e", h=HEADS), oo,
                                          rinv[:, t, :].unsqueeze(2).broadcast_to([P, HEADS, VD]),
                                          ALU.mult).then_inc(y_ready, 1)
                    if 0 <= t - 2 < TILES:
                        norm_sum(dve, st, n, part, t - 2)
                    if 0 <= t - 3:
                        norm_apply(dve, st, n, t - 3)



def fold_tensors(mem, sem):
    class F:
        pass
    f = F()
    f.w = [mem.sb(f"fa_w{s}", [P, 4, DM]) for s in range(2)]
    f.kv = [mem.sb(f"fa_kv{s}", [P, 2, CTX]) for s in range(2)]
    f.folded = mem.sb("fa_folded", [P, DC, BATCH, HEADS, KEYS])
    f.vw = mem.sb("fa_vw", [P, BATCH, PAIRS, DM])
    f.kv_bank = mem.psum("fa_kv_bank", [P, BANK])
    f.fold_bank = mem.psum("fa_fold_bank", [P, BANK])
    f.vw_bank = [mem.psum(f"fa_vw_bank{j}", [P, BANK]) for j in range(2)]
    f.w_loaded = [sem(f"fa_w_loaded{s}") for s in range(2)]
    f.kv_projected = sem("fa_kv_projected")
    f.kv_ready = sem("fa_kv_ready")
    f.fold_done = sem("fa_fold_done")
    f.folded_ready = sem("fa_folded_ready")
    f.vw_done = sem("fa_vw_done")
    f.vw_ready = sem("fa_vw_ready")
    return f


def fold_load(sp, f, d, h):
    if h >= 2:
        sp.wait_ge(f.vw_done, h - 1)
    sp.dma_start(f.w[h % 2][:], d["fa_w"][h]).then_inc(f.w_loaded[h % 2], 16)


def fold_tensor(pe, st, f, h):
    s = h % 2
    pe.wait_ge(f.w_loaded[s], 16 * (h // 2 + 1))
    if h:
        pe.wait_ge(f.kv_ready, h)
    for r in range(2):
        for j in range(DC):
            last = pe.matmul(f.kv_bank[:, r * CTX:(r + 1) * CTX], f.w[s][:, r, j * HD:(j + 1) * HD],
                             st.ctxT[:, j, :], start=j == 0, stop=j == DC - 1)
    last.then_inc(f.kv_projected, 1)
    pe.wait_ge(f.kv_ready, h + 1)
    if h:
        pe.wait_ge(f.folded_ready, h)
    for j in range(DC):
        last = pe.matmul(f.fold_bank[:, j * CTX:(j + 1) * CTX], f.w[s][:, 2, j * P:(j + 1) * P],
                         f.kv[s][:, 0, :], start=True, stop=True)
    last.then_inc(f.fold_done, 1)
    if s == 0 and h:
        pe.wait_ge(f.vw_ready, h)
    for b in range(BATCH):
        last = pe.matmul(f.vw_bank[b // 2][s * KEYS:(s + 1) * KEYS, (b % 2) * DM:(b % 2 + 1) * DM],
                         f.kv[s][:, 1, b * KEYS:(b + 1) * KEYS], f.w[s][:, 3, :], start=True, stop=True)
    last.then_inc(f.vw_done, 1)


def fold_scalar(act, f, h):
    s = h % 2
    act.wait_ge(f.kv_projected, h + 1)
    act.activation(f.kv[s][:].rearrange("p r n -> p (r n)"), f.kv_bank[:, :], ACT.Copy).then_inc(f.kv_ready, 1)
    act.wait_ge(f.fold_done, h + 1)
    act.activation(f.folded[:, :, :, h, :], f.fold_bank[:, :].rearrange("p (c b k) -> p c b k", c=DC, b=BATCH),
                   ACT.Copy, scale=float(HD) ** -0.5).then_inc(f.folded_ready, 1)
    if s:
        act.wait_ge(f.vw_done, h + 1)
        for j in range(2):
            act.activation(f.vw[:, 2 * j:2 * j + 2, h // 2, :],
                           f.vw_bank[j][:, :].rearrange("p (b n) -> p b n", b=2), ACT.Copy).then_inc(f.vw_ready, 1)


def folded_attention(nc, st, sem, d, f):
    with Memory(nc) as mem:
        c = cross_tensors(mem, sem, "fa", f.vw)
        turn_bank = [mem.psum(f"fa_turn{i}", [P, BANK]) for i in range(2)]
        norm_bank = [mem.psum(f"fa_norm{i}", [P, BANK]) for i in range(2)]
        n = norm_tensors(mem, st, "fa")
        score = f.vw_bank
        out_bank = [f.kv_bank, f.fold_bank]
        part = lambda t: out_bank[t % 2][:, 0:DM]
        turns = [norm_bank[i][:, 0:DM].rearrange("p (c n) -> p c n", c=DC) for i in range(2)]
        scored = sem("fa_scored")

        with nc.Block() as block:
            @block.tensor
            def _(pe):
                def scores(t):
                    if t > 0:
                        pe.wait_ge(c.shifted, t)
                    for j in range(2):
                        for k in range(DC):
                            last = pe.matmul(score[j][:, :], st.xT[:, k, tile_cols(t)],
                                             f.folded[:, k, t // 2, 8 * j:8 * j + 8, :].rearrange("p h k -> p (h k)"),
                                             start=k == 0, stop=k == DC - 1)
                        last.then_inc(scored, 1)
                scores(0)
                for t in range(TILES + 2):
                    if t + 1 < TILES:
                        scores(t + 1)
                    if t < TILES:
                        cross_turn(pe, st, c, turn_bank, t)
                    if 0 <= t - 1 < TILES:
                        cross_out(pe, c, n, part, t - 1)
                    if t >= 3:
                        norm_tensor(pe, st, n, turns, t - 3)
                norm_tensor(pe, st, n, turns, TILES - 1)

            @block.scalar
            def _(act):
                for t in range(TILES + 4):
                    if t < TILES:
                        cross_exp(act, c, t)
                    if 0 <= t - 1 < TILES:
                        cross_keep(act, c, turn_bank, t - 1)
                    if 0 <= t - 2 < TILES:
                        norm_std(act, st, n, t - 2)
                    if 0 <= t - 4:
                        norm_keep(act, st, n, turns, t - 4)

            @block.vector
            def _(dve):
                for t in range(TILES + 3):
                    if t < TILES:
                        for j in range(2):
                            dve.wait_ge(scored, 2 * t + j + 1)
                            dve.tensor_reduce(c.max[:, t, 8 * j:8 * j + 8],
                                              score[j][:, :].rearrange("p (h k) -> p h k", h=8),
                                              X_AXIS, ALU.max).then_inc(c.max_ready, 1)
                        dve.wait_ge(c.max_ready, 2 * t + 2)
                        for j in range(2):
                            last = dve.tensor_tensor(c.rows[:, t, 8 * j:8 * j + 8, :],
                                                     score[j][:, :].rearrange("p (h k) -> p h k", h=8),
                                                     over_keys(c.max[:, t, 8 * j:8 * j + 8]), ALU.subtract)
                        last.then_inc(c.shifted, 1)
                        cross_normalise_sum(dve, c, t)
                    if 0 <= t - 2 < TILES:
                        norm_sum(dve, st, n, part, t - 2)
                    if 0 <= t - 3:
                        norm_apply(dve, st, n, t - 3)

            @block.gpsimd
            def _(pool):
                for t in range(TILES):
                    cross_weights(pool, c, t)



def differential_attention(nc, st, sem, d, f):
    HALVES_Q = 2 * HEADS
    D = DM // HALVES_Q
    VD = DM // HEADS
    CHUNKS = 4
    CQ = HALVES_Q // CHUNKS
    with Memory(nc) as mem:
        wqk = mem.sb("da_wqk", [P, DC, 2 * DM])
        wv = mem.sb("da_wv", [P, DC, DM])
        wo = mem.sb("da_wo", [P, DC, DM])
        bo = mem.sb("da_bo", [P, DM])
        lam_in = mem.sb("da_lam_in", [P, 2, 2, D])
        lam_prod = mem.sb("da_lam_prod", [P, 2, D])
        lam_sum = mem.sb("da_lam_sum", [P, 2])
        lam_exp = mem.sb("da_lam_exp", [P, 2])
        neg_lam = mem.sb("da_neg_lam", [P, 1])
        q = mem.sb("da_q", [P, TILES, HALVES_Q, D])
        k = mem.sb("da_k", [P, TILES, HALVES_Q, D])
        v = mem.sb("da_v", [P, TILES, HEADS, VD])
        prod_outer = mem.sb("da_prod_outer", [P, 2, D, CQ, HALVES_Q])
        prod_inner = mem.sb("da_prod_inner", [P, 2, CQ, HALVES_Q, D])
        vprod = mem.sb("da_vprod", [P, 2, HEADS // 2, VD, HEADS])
        att = mem.sb("da_att", [P, 2, HALVES_Q, HALVES_Q])
        above = mem.sb("da_above", [P, HALVES_Q, HALVES_Q])
        below = mem.sb("da_below", [P, HALVES_Q, HALVES_Q])
        rowmax = mem.sb("da_rowmax", [P, HALVES_Q])
        rowsum = mem.sb("da_rowsum", [P, HALVES_Q])
        rinv = mem.sb("da_rinv", [P, HALVES_Q])
        first = mem.sb("da_first", [P, HEADS, HEADS])
        second = mem.sb("da_second", [P, HEADS, HEADS])
        diff = mem.sb("da_diff", [P, 2, HEADS, HEADS])
        mixed = mem.sb("da_mixed", [P, HEADS, VD])
        squares = mem.sb("da_squares", [P, HEADS, VD])
        ssq = mem.sb("da_ssq", [P, HEADS])
        rms = mem.sb("da_rms", [P, HEADS])
        rrms = mem.sb("da_rrms", [P, HEADS])
        y = mem.sb("da_y", [P, 2, DM])
        yT = mem.sb("da_yT", [P, 2, DC, P])
        qk_bank = [mem.psum(f"da_qk_bank{i}", [P, BANK]) for i in range(2)]
        v_bank = [mem.psum(f"da_v_bank{i}", [P, BANK]) for i in range(2)]
        n = norm_tensors(mem, st, "da")
        score_bank = qk_bank[0]
        part = lambda t: qk_bank[1][:, 0:DM]
        yturn = v_bank[0][:, 0:DM].rearrange("p (c n) -> p c n", c=DC)
        turns = [v_bank[1][:, 0:DM].rearrange("p (c n) -> p c n", c=DC)] * 2

        loaded = sem("da_loaded")
        qk_projected = sem("da_qk_projected")
        v_projected = sem("da_v_projected")
        qk_ready = sem("da_qk_ready")
        v_ready = sem("da_v_ready")
        lam_summed = sem("da_lam_summed")
        lam_ready = sem("da_lam_ready")
        pool_prod = sem("da_pool_prod")
        pe_reduced = sem("da_pe_reduced")
        guarded = sem("da_guarded")
        shifted = sem("da_shifted")
        exp_ready = sem("da_exp_ready")
        diff_ready = sem("da_diff_ready")
        pool_vprod = sem("da_pool_vprod")
        vreduced = sem("da_vreduced")
        ssq_ready = sem("da_ssq_ready")
        rms_ready = sem("da_rms_ready")
        y_ready = sem("da_y_ready")
        y_turned = sem("da_y_turned")
        yT_ready = sem("da_yT_ready")
        chain = sem("da_chain")

        def score_product(eng, out, t, j):
            return eng.tensor_tensor(
                out, q[:, t, j * CQ:(j + 1) * CQ, :].unsqueeze(2).broadcast_to([P, CQ, HALVES_Q, D]),
                k[:, t, :, :].unsqueeze(1).broadcast_to([P, CQ, HALVES_Q, D]), ALU.mult)

        with nc.Block() as block:
            @block.sync
            def _(sp):
                for dst, src in ((wqk, "da_wqk"), (wv, "da_wv"), (wo, "da_wo")):
                    sp.dma_start(dst[:], d[src]).then_inc(loaded, 16)
                sp.dma_start(lam_in[:], d["da_lam"].partition_broadcast(P)).then_inc(loaded, 16)
                sp.dma_start(bo[:], d["da_bo"].partition_broadcast(P)).then_inc(loaded, 16)
                for h in range(HEADS):
                    fold_load(sp, f, d, h)

            @block.tensor
            def _(pe):
                pe.wait_ge(loaded, 16 * 5)
                for t in range(TILES):
                    if t >= 2:
                        pe.wait_ge(qk_ready, 2 * (t - 1))
                    for c in range(DC):
                        last = pe.matmul(qk_bank[t % 2][:, :], st.xT[:, c, tile_cols(t)], wqk[:, c, :],
                                         start=c == 0, stop=c == DC - 1)
                    last.then_inc(qk_projected, 1)
                    if t >= 2:
                        pe.wait_ge(v_ready, t - 1)
                    for c in range(DC):
                        last = pe.matmul(v_bank[t % 2][:, 0:DM], st.xT[:, c, tile_cols(t)], wv[:, c, :],
                                         start=c == 0, stop=c == DC - 1)
                    last.then_inc(v_projected, 1)
                pe.wait_ge(qk_ready, 2 * TILES)
                pe.wait_ge(v_ready, TILES)
                for t in range(TILES + 2):
                    if t < TILES:
                        if t:
                            pe.wait_ge(guarded, t)
                        for j in range(2):
                            pe.wait_ge(pool_prod, 2 * t + j + 1)
                            for e in range(D):
                                last = pe.matmul(score_bank[:, j * CQ * HALVES_Q:(j + 1) * CQ * HALVES_Q],
                                                 st.ident[:], prod_outer[:, j, e, :, :].rearrange("p a b -> p (a b)"),
                                                 start=e == 0, stop=e == D - 1)
                            last.then_inc(pe_reduced, 1)
                        fold_tensor(pe, st, f, 2 * t)
                        fold_tensor(pe, st, f, 2 * t + 1)
                    if t >= 2:
                        norm_tensor(pe, st, n, turns, t - 2, depth=1)
                    if 0 <= t - 1 < TILES:
                        r = t - 1
                        pe.wait_ge(y_ready, r + 1)
                        if r:
                            pe.wait_ge(yT_ready, r)
                        for c in range(DC):
                            last = pe.transpose(yturn[:, c, :], y[:, r % 2, tile_cols(c)], st.ident[:])
                        last.then_inc(y_turned, 1)
                        pe.wait_ge(yT_ready, r + 1)
                        if r:
                            pe.wait_ge(n.summed, n.base + r)
                        for c in range(DC):
                            last = pe.matmul(part(r), yT[:, r % 2, c, :], wo[:, c, :], start=c == 0, stop=c == DC - 1)
                        last.then_inc(n.out_ready, 1)

            @block.scalar
            def _(act):
                act.wait_ge(lam_summed, 1)
                act.activation(lam_exp[:], lam_sum[:], ACT.Exp).then_inc(lam_ready, 1)
                for t in range(TILES):
                    act.wait_ge(qk_projected, t + 1)
                    act.activation(q[:, t, :, :].rearrange("p a e -> p (a e)"), qk_bank[t % 2][:, 0:DM], ACT.Copy,
                                   scale=float(D) ** -0.5).then_inc(qk_ready, 1)
                    act.activation(k[:, t, :, :].rearrange("p a e -> p (a e)"), qk_bank[t % 2][:, DM:2 * DM],
                                   ACT.Copy).then_inc(qk_ready, 1)
                    act.wait_ge(v_projected, t + 1)
                    act.activation(v[:, t, :, :].rearrange("p h e -> p (h e)"), v_bank[t % 2][:, 0:DM],
                                   ACT.Copy).then_inc(v_ready, 1)
                for t in range(TILES + 2):
                    if t < TILES:
                        fold_scalar(act, f, 2 * t)
                        fold_scalar(act, f, 2 * t + 1)
                        act.wait_ge(shifted, t + 1)
                        act.activation(att[:, t % 2, :, :], att[:, t % 2, :, :], ACT.Exp).then_inc(exp_ready, 1)
                    if t >= 2:
                        norm_std(act, st, n, t - 2)
                    if 0 <= t - 1 < TILES:
                        act.wait_ge(ssq_ready, t)
                        act.activation(rms[:], ssq[:], ACT.Sqrt, bias=st.eps[:, :],
                                       scale=1.0 / VD).then_inc(rms_ready, 1)
                    if t >= 2:
                        norm_keep(act, st, n, turns, t - 2)
                    if 0 <= t - 1 < TILES:
                        act.wait_ge(y_turned, t)
                        act.activation(yT[:, (t - 1) % 2, :, :], yturn, ACT.Copy).then_inc(yT_ready, 1)

            @block.gpsimd
            def _(pool):
                def score_products(t):
                    pool.wait_ge(qk_ready, 2 * t + 2)
                    for j in range(2):
                        if t > 0:
                            pool.wait_ge(pe_reduced, 2 * (t - 1) + j + 1)
                        score_product(pool, prod_outer[:, j, :, :, :].rearrange("p e a b -> p a b e"),
                                      t, j).then_inc(pool_prod, 1)

                score_products(0)
                for t in range(TILES):
                    if t + 1 < TILES:
                        score_products(t + 1)
                    pool.wait_ge(diff_ready, t + 1)
                    pool.wait_ge(v_ready, t + 1)
                    for j in range(2):
                        if t > 0:
                            pool.wait_ge(vreduced, 2 * (t - 1) + j + 1)
                        HH = HEADS // 2
                        pool.tensor_tensor(
                            vprod[:, j, :, :, :],
                            diff[:, t % 2, j * HH:(j + 1) * HH, :].unsqueeze(2).broadcast_to([P, HH, VD, HEADS]),
                            v[:, t, :, :].rearrange("p h e -> p e h").unsqueeze(1).broadcast_to([P, HH, VD, HEADS]),
                            ALU.mult).then_inc(pool_vprod, 1)

            @block.vector
            def _(dve):
                links = [0]

                def link(ins):
                    links[0] += 1
                    ins.then_inc(chain, 1)
                    dve.wait_ge(chain, links[0])

                def over(a, count):
                    return a.unsqueeze(2).broadcast_to([P, a.shape[1], count])

                dve.wait_ge(loaded, 16 * 5)
                link(dve.tensor_tensor(lam_prod[:], lam_in[:, 0, :, :], lam_in[:, 1, :, :], ALU.mult))
                dve.tensor_reduce(lam_sum[:], lam_prod[:], X_AXIS, ALU.add).then_inc(lam_summed, 1)
                dve.wait_ge(lam_ready, 1)
                link(dve.scalar_tensor_tensor(neg_lam[:], lam_exp[:, 1:2], LAM_INIT, lam_exp[:, 0:1],
                                              ALU.subtract, ALU.subtract))
                for t in range(TILES):
                    link(dve.tensor_tensor(st.x[:, t, :], st.x[:, t, :], bo[:, :], ALU.add))

                def head_maps(t):
                    a = att[:, t % 2, :, :]
                    dve.wait_ge(qk_ready, 2 * t + 2)
                    score_product(dve, prod_inner[:, 0, :, :, :], t, 2)
                    link(score_product(dve, prod_inner[:, 1, :, :, :], t, 3))
                    link(dve.tensor_reduce(a[:, HEADS:, :], prod_inner[:].rearrange("p j a b e -> p (j a) b e"),
                                           X_AXIS, ALU.add))
                    dve.tensor_scalar(above[:, HEADS:, :], a[:, HEADS:, :], 0.0, LARGEST, ALU.max, ALU.min)
                    dve.tensor_scalar(below[:, HEADS:, :], a[:, HEADS:, :], 0.0, -LARGEST, ALU.min, ALU.max)
                    dve.wait_ge(pe_reduced, 2 * t + 2)
                    half = score_bank[:, :].rearrange("p (a b) -> p a b", a=HEADS)
                    dve.tensor_scalar(above[:, 0:HEADS, :], half, 0.0, LARGEST, ALU.max, ALU.min)
                    dve.tensor_scalar(below[:, 0:HEADS, :], half, 0.0, -LARGEST, ALU.min,
                                      ALU.max).then_inc(guarded, 1)
                    dve.wait_ge(guarded, t + 1)
                    link(dve.tensor_tensor(a, above[:], below[:], ALU.add))
                    link(dve.tensor_reduce(rowmax[:], a, X_AXIS, ALU.max))
                    dve.tensor_tensor(a, a, over(rowmax[:], HALVES_Q), ALU.subtract).then_inc(shifted, 1)

                def map_difference(t):
                    a = att[:, t % 2, :, :]
                    dve.wait_ge(exp_ready, t + 1)
                    link(dve.tensor_reduce(rowsum[:], a, X_AXIS, ALU.add))
                    link(dve.reciprocal(rinv[:], rowsum[:]))
                    dve.tensor_tensor(first[:], a[:, 0:HEADS, 0:HEADS], over(rinv[:, 0:HEADS], HEADS), ALU.mult)
                    link(dve.tensor_tensor(second[:], a[:, HEADS:, HEADS:], over(rinv[:, HEADS:], HEADS), ALU.mult))
                    dve.scalar_tensor_tensor(diff[:, t % 2, :, :].rearrange("p a h -> p (a h)"),
                                             second[:].rearrange("p a h -> p (a h)"), neg_lam[:, :],
                                             first[:].rearrange("p a h -> p (a h)"),
                                             ALU.mult, ALU.add).then_inc(diff_ready, 1)

                def mix(t):
                    for j in range(2):
                        dve.wait_ge(pool_vprod, 2 * t + j + 1)
                        dve.tensor_reduce(mixed[:, j * HEADS // 2:(j + 1) * HEADS // 2, :], vprod[:, j, :, :, :],
                                          X_AXIS, ALU.add).then_inc(vreduced, 1)
                    dve.wait_ge(vreduced, 2 * t + 2)
                    link(dve.tensor_tensor(squares[:], mixed[:], mixed[:], ALU.mult))
                    dve.tensor_reduce(ssq[:], squares[:], X_AXIS, ALU.add).then_inc(ssq_ready, 1)

                def mix_norm(t):
                    dve.wait_ge(rms_ready, t + 1)
                    link(dve.reciprocal(rrms[:], rms[:]))
                    dve.scalar_tensor_tensor(y[:, t % 2, :].rearrange("p (h e) -> p h e", h=HEADS), mixed[:],
                                             1.0 - LAM_INIT, over(rrms[:], VD),
                                             ALU.mult, ALU.mult).then_inc(y_ready, 1)

                for t in range(TILES + 2):
                    if t < TILES:
                        head_maps(t)
                    if t >= 2:
                        norm_sum(dve, st, n, part, t - 2)
                    if 0 <= t - 1 < TILES:
                        mix(t - 1)
                    if t < TILES:
                        map_difference(t)
                    if t >= 2:
                        norm_apply(dve, st, n, t - 2)
                    if 0 <= t - 1 < TILES:
                        mix_norm(t - 1)


def differential_and_folded_attention(nc, st, sem, d):
    with Memory(nc) as mem:
        f = fold_tensors(mem, sem)
        differential_attention(nc, st, sem, d, f)
        folded_attention(nc, st, sem, d, f)



def experts(nc, st, sem, d):
    PARTS = 3
    with Memory(nc) as mem:
        w = [mem.sb(f"ex_w{s}", [P, 2, DC, P]) for s in range(2)]
        wd = mem.sb("ex_wd", [P, FTILES, DM])
        router = mem.sb("ex_router", [P, DC, EXPERTS])
        spreadf = mem.sb("ex_spreadf", [PARTS * EXPERTS, FTILES, P])
        spread = mem.sb("ex_spread", [PARTS * EXPERTS, FTILES, P], BF16)
        logits = mem.sb("ex_logits", [P, TILES, EXPERTS])
        top = mem.sb("ex_top", [P, TILES, TOP_K])
        marked = mem.sb("ex_marked", [P, TILES, EXPERTS])
        chosen = mem.sb("ex_chosen", [P, TILES, EXPERTS])
        weights = mem.sb("ex_weights", [P, TILES, EXPERTS])
        wsum = mem.sb("ex_wsum", [P, TILES])
        winv = mem.sb("ex_winv", [P, TILES])
        parts = mem.sb("ex_parts", [P, TILES, PARTS, EXPERTS], BF16)
        partsT = mem.sb("ex_partsT", [PARTS * EXPERTS, TOK], BF16)
        silu = [mem.sb(f"ex_silu{f}", [P, BANK]) for f in range(2)]
        gated = [mem.sb(f"ex_gated{f}", [P, BANK]) for f in range(2)]
        hidden = mem.sb("ex_hidden", [P, FTILES, TOK])
        gate_bank = [mem.psum(f"ex_gate{f}", [P, BANK]) for f in range(2)]
        up_bank = [mem.psum(f"ex_up{f}", [P, BANK]) for f in range(2)]
        route_bank = [mem.psum(f"ex_route{f}", [P, BANK]) for f in range(2)]
        logit_bank = mem.psum("ex_logit", [P, BANK])
        parts_bank = mem.psum("ex_parts_bank", [P, 2 * BANK], BF16)
        n = norm_tensors(mem, st, "ex")
        out_banks = gate_bank + up_bank

        w_loaded = [sem(f"ex_w_loaded{s}") for s in range(2)]
        router_loaded = sem("ex_router_loaded")
        spread_loaded = sem("ex_spread_loaded")
        spread_ready = sem("ex_spread_ready")
        wd_loaded = sem("ex_wd_loaded")
        routed = sem("ex_routed")
        logits_ready = sem("ex_logits_ready")
        top_ready = sem("ex_top_ready")
        chain = sem("ex_chain")
        less_max = sem("ex_less_max")
        exp_ready = sem("ex_exp_ready")
        parts_ready = sem("ex_parts_ready")
        parts_turned = sem("ex_parts_turned")
        partsT_ready = sem("ex_partsT_ready")
        gate_done = sem("ex_gate_done")
        rest_done = sem("ex_rest_done")
        silu_ready = sem("ex_silu_ready")
        gated_ready = sem("ex_gated_ready")
        hidden_ready = sem("ex_hidden_ready")
        stored = sem("ex_stored")

        with nc.Block() as block:
            @block.sync
            def _(sp):
                sp.dma_start(router[:], d["ex_router"]).then_inc(router_loaded, 16)
                sp.dma_start(w[0][:], d["ex_w"][0]).then_inc(w_loaded[0], 16)
                sp.dma_start(w[1][:], d["ex_w"][1]).then_inc(w_loaded[1], 16)
                sp.dma_start(spreadf[:], d["ex_spread"]).then_inc(spread_loaded, 16)
                sp.dma_start(wd[:], d["ex_wd"]).then_inc(wd_loaded, 16)
                with sp.Fori(0, FTILES // 2 - 1) as i:
                    for s in range(2):
                        sp.wait_ge(rest_done, 4 * i + 2 * s + 2)
                        sp.dma_start(w[s][:], d["ex_w"][2 * i + s + 2]).then_inc(w_loaded[s], 16)
                for t in range(TILES):
                    sp.wait_ge(n.x_ready, n.base + t + 1)
                    sp.dma_start(st.out[:, t, :], st.x[:, t, :]).then_inc(stored, 16)
                sp.wait_ge(stored, 16 * TILES)

            @block.tensor
            def _(pe):
                pe.wait_ge(router_loaded, 16)
                for t in range(TILES):
                    for c in range(DC):
                        last = pe.matmul(logit_bank[:, t * EXPERTS:(t + 1) * EXPERTS], st.xT[:, c, tile_cols(t)],
                                         router[:, c, :], start=c == 0, stop=c == DC - 1)
                last.then_inc(routed, 1)

                def gate_up(f, s):
                    for r, bank in ((0, gate_bank[f]), (1, up_bank[f])):
                        for c in range(DC):
                            last = pe.matmul(bank[:, :], w[s][:, r, c, :], st.xT[:, c, f * BANK:(f + 1) * BANK],
                                             start=c == 0, stop=c == DC - 1)
                        if r == 0:
                            last.then_inc(gate_done, 1)

                def route(j, f):
                    pe.matmul(route_bank[f][:, :], spread[:, bass.ds(j, 1), :].squeeze(1),
                              partsT[:, f * BANK:(f + 1) * BANK], start=True, stop=True).then_inc(rest_done, 1)

                pe.wait_ge(w_loaded[0], 16)
                gate_up(0, 0)
                gate_up(1, 0)
                for t in range(TILES):
                    if t == 0:
                        pe.wait_ge(parts_ready, 1)
                    last = pe.transpose(parts_bank[0:PARTS * EXPERTS, tile_cols(t)],
                                        parts[:, t, :, :].rearrange("p r e -> p (r e)"), st.identb[:])
                last.then_inc(parts_turned, 1)
                pe.wait_ge(spread_ready, 1)
                pe.wait_ge(partsT_ready, 1)
                route(0, 0)
                route(0, 1)

                def tile(i, s):
                    j = 2 * i + s
                    pe.wait_ge(w_loaded[s], 16 * (i + 1))
                    for f in range(2):
                        pe.wait_ge(hidden_ready, 2 * j + f - 1)
                        gate_up(f, s)
                        route(j, f)
                tile(0, 1)
                with pe.Fori(1, FTILES // 2) as i:
                    tile(i, 0)
                    tile(i, 1)
                pe.wait_ge(wd_loaded, 16)
                pe.wait_ge(hidden_ready, 2 * FTILES)
                for t in range(TILES):
                    if t >= 4:
                        pe.wait_ge(n.summed, n.base + t - 3)
                    for j in range(FTILES):
                        last = pe.matmul(out_banks[t % 4][:, 0:DM], hidden[:, j, tile_cols(t)], wd[:, j, :],
                                         start=j == 0, stop=j == FTILES - 1)
                    last.then_inc(n.out_ready, 1)

            @block.scalar
            def _(act):
                act.wait_ge(less_max, 1)
                act.activation(weights[:], weights[:], ACT.Exp).then_inc(exp_ready, 1)
                act.wait_ge(parts_turned, 1)
                act.activation(partsT[:, :], parts_bank[0:PARTS * EXPERTS, :], ACT.Copy).then_inc(partsT_ready, 1)

                def unit(j, f):
                    act.wait_ge(gate_done, 2 * j + f + 1)
                    act.activation(silu[f][:, :], gate_bank[f][:, :], ACT.Silu).then_inc(silu_ready, 1)
                with act.Fori(0, FTILES) as j:
                    unit(j, 0)
                    unit(j, 1)
                for t in range(TILES):
                    norm_std(act, st, n, t)

            @block.gpsimd
            def _(pool):
                pool.wait_ge(spread_loaded, 16)
                pool.tensor_copy(spread[:], spreadf[:]).then_inc(spread_ready, 1)

            @block.vector
            def _(dve):
                links = [0]

                def link(ins):
                    links[0] += 1
                    ins.then_inc(chain, 1)
                    dve.wait_ge(chain, links[0])

                def over(a, count):
                    return a.unsqueeze(2).broadcast_to([P, a.shape[1], count])

                dve.wait_ge(routed, 1)
                link(dve.tensor_copy(logits[:].rearrange("p t e -> p (t e)"), logit_bank[:, 0:TILES * EXPERTS]))
                for t in range(TILES):
                    last = dve.max(top[:, t, :], logits[:, t, :])
                link(last)
                for t in range(TILES):
                    last = dve.match_replace(marked[:, t, :], top[:, t, :], logits[:, t, :], -LARGEST)
                dve.tensor_tensor(weights[:], logits[:], over(top[:, :, 0], EXPERTS),
                                  ALU.subtract).then_inc(less_max, 1)
                link(last)
                link(dve.tensor_tensor(chosen[:], logits[:], marked[:], ALU.not_equal))
                dve.wait_ge(exp_ready, 1)
                link(dve.tensor_tensor(weights[:], weights[:], chosen[:], ALU.mult))
                link(dve.tensor_reduce(wsum[:], weights[:], X_AXIS, ALU.add))
                link(dve.reciprocal(winv[:], wsum[:]))
                link(dve.tensor_tensor(weights[:], weights[:], over(winv[:], EXPERTS), ALU.mult))
                for r in range(PARTS - 1):
                    link(dve.tensor_copy(parts[:, :, r, :], weights[:]))
                    link(dve.tensor_tensor(weights[:], weights[:], parts[:, :, r, :], ALU.subtract))
                dve.tensor_copy(parts[:, :, PARTS - 1, :], weights[:]).then_inc(parts_ready, 1)

                def unit(j, f):
                    dve.wait_ge(silu_ready, 2 * j + f + 1)
                    dve.wait_ge(rest_done, 2 * j + f + 1)
                    dve.tensor_tensor(gated[f][:, :], silu[f][:, :], up_bank[f][:, :], ALU.mult).then_inc(gated_ready, 1)
                    dve.wait_ge(gated_ready, 2 * j + f + 1)
                    dve.tensor_tensor(hidden[:, bass.ds(j, 1), f * BANK:(f + 1) * BANK].squeeze(1), gated[f][:, :],
                                      route_bank[f][:, :], ALU.mult).then_inc(hidden_ready, 1)
                with dve.Fori(0, FTILES) as j:
                    unit(j, 0)
                    unit(j, 1)
                norm_vector(dve, st, n, lambda t: out_banks[t % 4][:, 0:DM])


STAGES = [self_attention, context_attention, recurrent_attention, differential_and_folded_attention, experts]


def build(nc, d, out):
    with ExitStack() as stack, Memory(nc) as mem:
        def sem(name):
            return stack.enter_context(nc.semaphore(name))
        st = State()
        st.x = mem.sb("x", [P, TILES, DM])
        st.xT = mem.sb("xT", [P, DC, TOK])
        st.ident = mem.sb("ident", [P, P])
        st.identb = mem.sb("identb", [P, P], BF16)
        st.mask = mem.sb("mask", [P, P], BF16)
        st.eps = mem.sb("eps", [P, 1])
        st.ctxT = mem.sb("ctxT", [P, DC, CTX])
        st.xT_loaded = sem("xT_loaded")
        st.consts_ready = sem("consts_ready")
        st.out = out
        st.norm = norm_signals(sem)
        for stage in STAGES:
            stage(nc, st, sem, d)



def layouts(inp):
    g = {k: np.asarray(v) for k, v in inp.items()}
    o = {}
    rows = lambda a, t: a.reshape(t, P, -1).transpose(1, 0, 2)
    x = g["x"].reshape(TOK, DM)
    o["x"] = rows(x, TILES)
    o["xT"] = rows(x.T, DC)
    o["ident"] = np.eye(P, dtype=np.float32)
    o["mask"] = np.triu(np.full((P, P), MASKED, np.float32), 1)
    qkv = np.stack([g["L0_attn_W_Q"], g["L0_attn_W_K"], g["L0_attn_W_V"]], 1)
    o["sa_w"] = qkv.reshape(HEADS, 3, DC, P, HD).transpose(0, 3, 1, 2, 4)
    o["sa_wo"] = g["L0_attn_W_O"].transpose(1, 0, 2)
    o["sa_bias"] = np.stack([g["L0_attn_b_Q"].T, g["L0_attn_b_K"].T, g["L0_attn_b_V"].T], 1)
    o["sa_bo"] = g["L0_attn_b_O"]
    o["ctxT"] = rows(g["ctx_2048"].reshape(CTX, DM).T, DC)
    o["ca_wq"] = g["L0_xattn_Wq"].reshape(DC, P, HEADS, HD).transpose(2, 1, 0, 3)
    o["ca_wk"] = rows(g["L0_xattn_Wk"], DC)
    o["ca_wv"] = rows(g["L0_xattn_Wv"], DC)
    o["ca_wo"] = g["L0_xattn_Wo"].reshape(HEADS, HD, DM).transpose(1, 0, 2)
    o["ca_bq"] = g["L0_xattn_bq"].reshape(HEADS, HD).T
    o["ca_bk"] = g["L0_xattn_bk"]
    o["ca_bv"] = g["L0_xattn_bv"].reshape(4, HD).T
    o["ca_norms"] = np.stack([g["L0_xattn_qn_w"], g["L0_xattn_kn_w"]], 1)
    o["ca_amask"] = g["mask_1xSxS2_ff0"][0].reshape(2, P, KEYS).transpose(1, 0, 2)
    wa = g["L0_ffn_Wa"]
    q_std, k_std, v, q_low, k_low = np.split(wa, [128, 256, 512, 640], axis=1)
    join = lambda a, b: np.concatenate([a.reshape(DM, HEADS, 8), b.reshape(DM, HEADS, 8)], 2).reshape(DM, DM)
    o["ra_wq"] = rows(join(q_std, q_low), DC)
    o["ra_wk"] = rows(join(k_std, k_low), DC)
    o["ra_wv"] = rows(v, DC)
    o["ra_wo"] = rows(g["L0_ffn_Wp"], DC)
    own = np.repeat(np.eye(8, dtype=np.float32), 16, 0)
    o["ra_rowmask"] = own
    is_low = np.tile(np.repeat(np.array([False, True]), 8), HEADS)
    std_row, rec_row = np.repeat(g["L0_ffn_w_std"], 16), np.repeat(g["L0_ffn_w_rec"], 16)
    w_row = np.where(is_low, rec_row, std_row)
    o["ra_roww"] = np.stack([w_row, rec_row, is_low.astype(np.float32)], 0).reshape(3, 2, P).transpose(2, 0, 1)
    half = lambda a: a.T.reshape(DM, HEADS, 8, 2).transpose(0, 3, 1, 2).reshape(DM, DM)
    o["da_wqk"] = rows(np.concatenate([half(g["L1_attn_Wq"]), half(g["L1_attn_Wk"])], 1), DC)
    o["da_wv"] = rows(g["L1_attn_Wv"].T, DC)
    o["da_wo"] = rows(g["L1_attn_Wo"].T, DC)
    o["da_lam"] = np.stack([np.stack([g["L1_attn_lq1"], g["L1_attn_lq2"]]),
                            np.stack([g["L1_attn_lk1"], g["L1_attn_lk2"]])])
    o["da_bo"] = g["L1_attn_bo"]
    by_head = lambda a: a.reshape(DC, P, HEADS, HD).transpose(2, 1, 0, 3).reshape(HEADS, P, 1, DM)
    o["fa_w"] = np.concatenate([by_head(g["L1_xattn_Wk"]), by_head(g["L1_xattn_Wv"]),
                                g["L1_xattn_Wq"].reshape(DM, HEADS, HD).transpose(1, 2, 0)[:, :, None, :],
                                g["L1_xattn_Wo"].reshape(HEADS, HD, 1, DM)], 2)
    stacked = lambda a: a.reshape(FTILES, P, DC, P).transpose(0, 3, 2, 1)
    o["ex_w"] = np.stack([stacked(g["L1_ffn_w_gate_proj"]), stacked(g["L1_ffn_w_up_proj"])], 2)
    o["ex_wd"] = rows(g["L1_ffn_w_down_proj"].transpose(0, 2, 1).reshape(-1, DM), FTILES)
    o["ex_router"] = rows(g["L1_ffn_gate_w"].T, DC)
    own = np.repeat(np.eye(EXPERTS), INNER, 1).reshape(EXPERTS, FTILES, P)
    o["ex_spread"] = np.concatenate([own] * 3, 0).astype(np.float32)
    return {k: np.ascontiguousarray(v) for k, v in o.items()}


def kernel(**inputs):
    import concourse.bacc as bacc
    from concourse.bass_utils import run_bass_kernel_spmd

    arrays = layouts(inputs)
    nc = bacc.Bacc("TRN2", target_bir_lowering=False, num_devices=1)
    d = {k: nc.dram_tensor(f"in_{k}", a.shape, mybir.dt.from_np(a.dtype), kind="ExternalInput").ap()
         for k, a in arrays.items()}
    out = nc.dram_tensor("out", (P, TILES, DM), F32, kind="ExternalOutput").ap()
    build(nc, d, out)
    r = run_bass_kernel_spmd(nc, [{f"in_{k}": a for k, a in arrays.items()}], core_ids=[0])
    y = r.results[0]["out"]
    return y.transpose(1, 0, 2).reshape(BATCH, SEQ, DM)
```

```python
from contextlib import ExitStack

import numpy as np

import concourse.bass as bass
from concourse import mybir

F32 = mybir.dt.float32
F16 = mybir.dt.float16
F32R = mybir.dt.float32r
BF16 = mybir.dt.bfloat16
ALU = mybir.AluOpType
ACT = mybir.ActivationFunctionType
X_AXIS = mybir.AxisListType.X

P = 128
BATCH = 4
SEQ = 256
KEYS = 64
DM = 256
DC = DM // P
TOK = BATCH * SEQ
TILES = TOK // P
CTX = BATCH * KEYS
HEADS = 16
HD = 128
BANK = 512
HALVES = TOK // BANK
EXPERTS = 32
INNER = 96
FTILES = EXPERTS * INNER // P
TOP_K = 8
LN_EPS = 1e-5
MASKED = -1e30
LARGEST = float(np.finfo(np.float32).max)
LAM_INIT = 0.8 - 0.6 * float(np.exp(-0.3 * 12))


class Memory:

    def __init__(self, nc):
        self.nc = nc
        self.stack = ExitStack()

    def __enter__(self):
        return self

    def __exit__(self, *_):
        self.stack.close()

    def sb(self, name, shape, dt=F32):
        return self.stack.enter_context(self.nc.sbuf_tensor(name, shape, dt))

    def psum(self, name, shape, dt=F32):
        return self.stack.enter_context(self.nc.psum_tensor(name, shape, dt))


class State:
    pass


def wait_past(eng, signal, value):
    if not (isinstance(value, int) and value <= 0):
        eng.wait_ge(signal, value)


def tile_cols(t):
    return slice(t * P, (t + 1) * P)



PASSES = ((0, 0), (0, 1), (1, 0))


def split_on(eng, ones, whole, hi, lo, done, count):
    eng.tensor_tensor(hi, whole, ones, ALU.mult).then_inc(done, 1)
    eng.wait_ge(done, count + 1)
    eng.tensor_tensor(lo, whole, hi, ALU.subtract).then_inc(done, 1)


def ones_like(st, a, b):
    return st.ones[:, :].unsqueeze(2).broadcast_to([P, a, b])


def products():
    steps = [(c, p) for c in range(DC) for p in PASSES]
    return [(c, p, i == 0, i == len(steps) - 1) for i, (c, p) in enumerate(steps)]


class SplitX:
    pass


def split_x_tensors(mem, sem, stage):
    x = SplitX()
    x.parts = mem.sb(f"{stage}_xs", [P, 2, DC, TOK], F32R)
    x.hi_ready = sem(f"{stage}_xhi_ready")
    x.lo_ready = sem(f"{stage}_xlo_ready")
    return x


def split_x_scalar(act, st, x):
    for f in range(HALVES):
        cols = slice(f * BANK, (f + 1) * BANK)
        act.activation(x.parts[:, 0, :, cols], st.xT[:, :, cols], ACT.Copy).then_inc(x.hi_ready, 1)


def split_x_vector(dve, st, x):
    for f in range(HALVES):
        cols = slice(f * BANK, (f + 1) * BANK)
        dve.wait_ge(x.hi_ready, f + 1)
        dve.tensor_tensor(x.parts[:, 1, :, cols], st.xT[:, :, cols], x.parts[:, 0, :, cols],
                          ALU.subtract).then_inc(x.lo_ready, 1)



NORM_SIGNALS = ("out_ready", "summed", "stats_done", "aggregated", "moments_done", "rstd_done",
                "x_ready", "turned", "xT_ready")


class Norm:
    pass


def norm_signals(sem):
    n = Norm()
    n.out_ready, n.summed, n.stats_done, n.aggregated, n.moments_done, n.rstd_done, n.x_ready, n.turned, n.xT_ready = (
        sem(f"norm_{name}") for name in NORM_SIGNALS)
    n.base = -TILES
    return n


def norm_tensors(mem, st, stage):
    n = st.norm
    n.base += TILES
    n.stats = mem.sb(f"{stage}_stats", [P, TILES, 6])
    n.moments = mem.sb(f"{stage}_moments", [P, TILES, 2])
    n.vareps = mem.sb(f"{stage}_vareps", [P, TILES])
    n.rstd = mem.sb(f"{stage}_rstd", [P, TILES])
    return n


def norm_sum(dve, st, n, part, t):
    dve.wait_ge(n.out_ready, n.base + t + 1)
    dve.tensor_tensor(st.x[:, t, :], part(t), st.x[:, t, :], ALU.add).then_inc(n.summed, 1)
    dve.wait_ge(n.summed, n.base + t + 1)
    dve.bn_stats(n.stats[:, t, :], st.x[:, t, :]).then_inc(n.stats_done, 1)
    dve.wait_ge(n.stats_done, n.base + t + 1)
    dve.bn_aggr(n.moments[:, t, :], n.stats[:, t, :]).then_inc(n.aggregated, 1)
    dve.wait_ge(n.aggregated, n.base + t + 1)
    dve.tensor_scalar(n.vareps[:, t:t + 1], n.moments[:, t, 1:2], LN_EPS, None, ALU.add).then_inc(n.moments_done, 1)


def norm_apply(dve, st, n, t):
    dve.wait_ge(n.rstd_done, n.base + t + 1)
    dve.tensor_scalar(st.x[:, t, :], st.x[:, t, :], n.moments[:, t, 0:1], n.rstd[:, t:t + 1],
                      ALU.subtract, ALU.mult).then_inc(n.x_ready, 1)


def norm_vector(dve, st, n, part):
    for t in range(TILES + 1):
        if t < TILES:
            norm_sum(dve, st, n, part, t)
        if t > 0:
            norm_apply(dve, st, n, t - 1)


def norm_rstd(pool, st, n, t):
    pool.wait_ge(n.moments_done, n.base + t + 1)
    pool.tensor_tensor(n.rstd[:, t:t + 1], n.vareps[:, t:t + 1], st.minus_half[:, :], ALU.pow).then_inc(n.rstd_done, 1)


def norm_pool(pool, st, n):
    for t in range(TILES):
        norm_rstd(pool, st, n, t)


def norm_keep(act, st, n, turn, t):
    act.wait_ge(n.turned, n.base + t + 1)
    act.activation(st.xT[:, :, tile_cols(t)], turn[t % 2], ACT.Copy).then_inc(n.xT_ready, 1)


def norm_scalar(act, st, n, turn):
    for t in range(TILES):
        norm_keep(act, st, n, turn, t)


def norm_tensor(pe, st, n, turn, t, depth=2):
    pe.wait_ge(n.x_ready, n.base + t + 1)
    if t >= depth:
        pe.wait_ge(n.xT_ready, n.base + t - depth + 1)
    for c in range(DC):
        last = pe.transpose(turn[t % 2][:, c, :], st.x[:, t, tile_cols(c)], st.ident[:, :])
    last.then_inc(n.turned, 1)



def self_attention(nc, st, sem, d):
    SCALE = float(HD) ** -0.5
    with Memory(nc) as mem:
        w = [mem.sb(f"sa_w{s}", [P, 3, DC, HD]) for s in range(2)]
        ws = [mem.sb(f"sa_ws{s}", [P, 2, 3, DC, HD], F32R) for s in range(2)]
        wo = mem.sb("sa_wo", [P, HEADS, DM])
        bias = mem.sb("sa_bias", [P, 3, HEADS])
        headbias = [mem.sb(f"sa_headbias{s}", [P, 2]) for s in range(2)]
        bo = mem.sb("sa_bo", [P, DM])
        maskf = mem.sb("sa_maskf", [P, P])
        qT = [mem.sb(f"sa_qT{s}", [P, TOK]) for s in range(2)]
        kT = [mem.sb(f"sa_kT{s}", [P, TOK]) for s in range(2)]
        v = [mem.sb(f"sa_v{s}", [P, TILES, HD]) for s in range(2)]
        probs = [mem.sb(f"sa_probs{s}", [P, 3 * BANK]) for s in range(2)]
        probsT = mem.sb("sa_probsT", [P, 2, 3 * P])
        negmax = mem.sb("sa_negmax", [P, 8])
        rowsum = mem.sb("sa_rowsum", [P, 8])
        rinv = mem.sb("sa_rinv", [P, 8])
        zT = mem.sb("sa_zT", [P, HEADS, TOK])
        proj = [mem.psum(f"sa_proj{i}", [P, BANK]) for i in range(2)]
        score = [mem.psum(f"sa_score{i}", [P, BANK]) for i in range(3)]
        turn = [mem.psum(f"sa_turn{i}", [P, BANK]) for i in range(2)]
        zbank = mem.psum("sa_z", [P, BANK])
        zout = [zbank, score[0]]

        w_loaded = [sem(f"sa_w_loaded{s}") for s in range(2)]
        w_split = sem("sa_w_split")
        xs = split_x_tensors(mem, sem, "sa")
        rest_loaded = sem("sa_rest_loaded")
        consts_loaded = sem("sa_consts_loaded")
        bq_scaled = sem("sa_bq_scaled")
        bo_added = sem("sa_bo_added")
        proj_ready = sem("sa_proj_ready")
        qk_ready = sem("sa_qk_ready")
        v_ready = sem("sa_v_ready")
        score_ready = sem("sa_score_ready")
        max_ready = sem("sa_max_ready")
        exp_ready = sem("sa_exp_ready")
        rinv_ready = sem("sa_rinv_ready")
        probs_ready = sem("sa_probs_ready")
        turn_ready = sem("sa_turn_ready")
        probsT_even = sem("sa_probsT_even")
        probsT_odd = sem("sa_probsT_odd")
        hb_ready = sem("sa_headbias_ready")
        z_ready = sem("sa_z_ready")
        zT_ready = sem("sa_zT_ready")
        n = norm_tensors(mem, st, "sa")
        out_part = lambda t: [score[1], score[2], proj[0], proj[1]][t % 4][:, 0:DM]
        turns = [turn[i][:, 0:DM].rearrange("p (c n) -> p c n", c=DC) for i in range(2)]

        def score_cols(b, q):
            return (0, b * P, P) if q == 0 else (1 + b // 2, (b % 2) * SEQ, SEQ)

        with nc.Block() as block:
            @block.sync
            def _(sp):
                sp.dma_start(st.xT[:, :, :], d["xT"]).then_inc(st.xT_loaded, 16)
                sp.dma_start(w[0][:], d["sa_w"][0]).then_inc(w_loaded[0], 16)
                sp.dma_start(bias[:], d["sa_bias"]).then_inc(rest_loaded, 16)
                sp.dma_start(maskf[:], d["mask"]).then_inc(consts_loaded, 16)
                sp.dma_start(st.ident[:], d["ident"]).then_inc(consts_loaded, 16)
                sp.dma_start(w[1][:], d["sa_w"][1]).then_inc(w_loaded[1], 16)
                sp.dma_start(st.x[:], d["x"]).then_inc(rest_loaded, 16)
                sp.dma_start(bo[:], d["sa_bo"].partition_broadcast(P)).then_inc(rest_loaded, 16)
                sp.dma_start(wo[:], d["sa_wo"]).then_inc(rest_loaded, 16)
                with sp.Fori(0, HEADS // 2 - 1) as i:
                    for s in range(2):
                        sp.wait_ge(w_split, 4 * i + 2 * s + 2)
                        sp.dma_start(w[s][:], d["sa_w"][2 * i + 2 + s]).then_inc(w_loaded[s], 16)

            @block.gpsimd
            def _(pool):
                pool.memset(st.minus_half[:, :], -0.5).then_inc(st.consts_ready, 1)
                pool.memset(st.ones[:, :], 1.0).then_inc(st.consts_ready, 1)
                pool.wait_ge(w_loaded[0], 16)
                pool.tensor_copy(ws[0][:, 0], w[0][:]).then_inc(w_split, 1)
                pool.wait_ge(consts_loaded, 32)
                pool.tensor_copy(st.identb[:], st.ident[:]).then_inc(st.consts_ready, 1)
                pool.tensor_copy(st.mask[:], maskf[:]).then_inc(st.consts_ready, 1)

                def split_w(h, s, loads):
                    pool.wait_ge(w_loaded[s], 16 * loads)
                    if not isinstance(h, int) or h >= 2:
                        pool.wait_ge(proj_ready, 6 * h - 6)
                    flat = [a.rearrange("p m c e -> p (m c) e") for a in (w[s][:], ws[s][:, 0], ws[s][:, 1])]
                    split_on(pool, ones_like(st, 3 * DC, HD), *flat, w_split, 2 * h)
                pool.wait_ge(st.consts_ready, 4)
                pool.wait_ge(w_split, 2)
                split_w(1, 1, 1)
                with pool.Fori(1, HEADS // 2) as i:
                    split_w(2 * i, 0, i + 1)
                    split_w(2 * i + 1, 1, i + 1)
                norm_pool(pool, st, n)

            @block.tensor
            def _(pe):
                def project(h, s, f):
                    if f == 0:
                        pe.wait_ge(w_split, 2 * h + 2)
                    if f < 2:
                        wait_past(pe, v_ready, 2 * h + f - 1)
                    else:
                        pe.wait_ge(qk_ready, 4 * h + f - 1)
                    if isinstance(h, int) and h == 0 and f < 2:
                        pe.wait_ge(xs.lo_ready, f + 1)
                    for c, (k, m), first, end in products() if f < 4 else ():
                        last = pe.matmul(proj[f % 2][:, :], ws[s][:, k, f // 2, c, :],
                                         xs.parts[:, m, c, (f % 2) * BANK:(f % 2 + 1) * BANK],
                                         start=first, stop=end)
                    for j in range(4) if f >= 4 else ():
                        for c, (k, m), first, end in products():
                            last = pe.matmul(proj[f % 2][:, j * HD:(j + 1) * HD],
                                             xs.parts[:, k, c, tile_cols((f - 4) * 4 + j)], ws[s][:, m, 2, c, :],
                                             start=first, stop=end)
                    last.then_inc(proj_ready, 1)

                def scores(h, s):
                    pe.wait_ge(qk_ready, 4 * h + 4)
                    wait_past(pe, zT_ready, 2 * h - 2)
                    wait_past(pe, exp_ready, 8 * h)
                    for bank in range(3):
                        for b in range(BATCH):
                            for q in range(2):
                                at, c0, width = score_cols(b, q)
                                if at != bank:
                                    continue
                                k0 = b * SEQ
                                pe.matmul(score[at][:, c0:c0 + width], qT[s][:, k0 + q * P:k0 + q * P + P],
                                          kT[s][:, k0:k0 + width], start=True, stop=False)
                                last = pe.matmul(score[at][:, c0 + width - P:c0 + width], st.identb[:], st.mask[:],
                                                 start=False, stop=True)
                        last.then_inc(score_ready, 1)

                def turn_probs(h, s, b):
                    pe.wait_ge(probs_ready, 8 * h + 5 + b)
                    o = turn[b % 2]
                    pe.transpose(o[:, 0:P], probs[s][:, b * P:(b + 1) * P], st.ident[:])
                    c0 = BANK + b * SEQ
                    pe.transpose(o[:, P:2 * P], probs[s][:, c0:c0 + P], st.ident[:])
                    pe.transpose(o[:, 2 * P:3 * P], probs[s][:, c0 + P:c0 + 2 * P], st.ident[:]).then_inc(turn_ready, 1)

                def weigh(h, s, b):
                    if b == 0:
                        pe.wait_ge(v_ready, 2 * h + 2)
                        wait_past(pe, zT_ready, 2 * h)
                    pe.wait_ge((probsT_even, probsT_odd)[b % 2], 2 * h + b // 2 + 1)
                    z = zout[b // 2][:, (b % 2) * SEQ:(b % 2 + 1) * SEQ]
                    pe.matmul(z, v[s][:, 2 * b, :], probsT[:, b % 2, 0:2 * P], start=True, stop=False)
                    last = pe.matmul(z[:, P:2 * P], v[s][:, 2 * b + 1, :], probsT[:, b % 2, 2 * P:3 * P],
                                     start=False, stop=True)
                    if b % 2:
                        last.then_inc(z_ready, 1)

                def step(h, s, attend=True, more=True):
                    if more is not None:
                        scores(h, s)
                    if attend:
                        turn_probs(h - 1, 1 - s, 0)
                        turn_probs(h - 1, 1 - s, 1)
                    if more:
                        project(h + 1, 1 - s, 0)
                    if attend:
                        weigh(h - 1, 1 - s, 0)
                        weigh(h - 1, 1 - s, 1)
                        turn_probs(h - 1, 1 - s, 2)
                        turn_probs(h - 1, 1 - s, 3)
                    if more:
                        project(h + 1, 1 - s, 1)
                    if attend:
                        if more is not None:
                            pe.wait_ge(exp_ready, 8 * h + 4)
                        weigh(h - 1, 1 - s, 2)
                        weigh(h - 1, 1 - s, 3)
                    if more:
                        for f in range(2, 6):
                            project(h + 1, 1 - s, f)

                pe.wait_ge(w_split, 2)
                for f in range(6):
                    project(0, 0, f)
                pe.wait_ge(rest_loaded, 16 * 4)
                pe.wait_ge(consts_loaded, 32)
                pe.wait_ge(st.consts_ready, 4)
                step(0, 0, attend=False)
                step(1, 1)
                step(2, 0)
                with pe.Fori(1, HEADS // 2 - 1) as i:
                    step(2 * i + 1, 1)
                    step(2 * i + 2, 0)
                step(HEADS - 1, 1, more=False)
                step(HEADS, 0, more=None)
                pe.wait_ge(zT_ready, 2 * HEADS)
                for t in range(TILES):
                    if t >= 4:
                        pe.wait_ge(n.summed, n.base + t - 3)
                    for g in range(HEADS):
                        last = pe.matmul(out_part(t), zT[:, g, tile_cols(t)], wo[:, g, :],
                                         start=g == 0, stop=g == HEADS - 1)
                    last.then_inc(n.out_ready, 1)
                    if t >= 2:
                        norm_tensor(pe, st, n, turns, t - 2)
                norm_tensor(pe, st, n, turns, TILES - 2)
                norm_tensor(pe, st, n, turns, TILES - 1)

            @block.scalar
            def _(act):
                def keep_qk(h, s, f):
                    act.wait_ge(proj_ready, 6 * h + f + 1)
                    act.wait_ge(hb_ready, h + 1)
                    dst = (qT if f < 2 else kT)[s][:, (f % 2) * BANK:(f % 2 + 1) * BANK]
                    act.activation(dst, proj[f % 2][:, :], ACT.Identity, bias=headbias[s][:, f // 2:f // 2 + 1],
                                   scale=SCALE if f < 2 else 1.0).then_inc(qk_ready, 1)

                def exps(h, s, bank):
                    act.wait_ge(max_ready, 3 * h + bank + 1)
                    wait_past(act, turn_ready, 4 * h - 4)
                    for j in range(4) if bank == 0 else range(2 * bank + 2, 2 * bank + 4):
                        width = P if bank == 0 else SEQ
                        c0 = j * P if bank == 0 else (j % 2) * SEQ
                        act.activation(probs[s][:, bank * BANK + c0:bank * BANK + c0 + width],
                                       score[bank][:, c0:c0 + width], ACT.Exp, bias=negmax[:, j:j + 1],
                                       accum_out=rowsum[:, j:j + 1]).then_inc(exp_ready, 1)

                def keep_turned(h, b):
                    act.wait_ge(turn_ready, 4 * h + b + 1)
                    act.activation(probsT[:, b % 2, :], turn[b % 2][:, 0:3 * P], ACT.Copy).then_inc(probsT_odd, 1)

                act.wait_ge(st.xT_loaded, 16)
                split_x_scalar(act, st, xs)
                for f in range(4):
                    keep_qk(0, 0, f)

                def step(h, s, attend=True, more=True):
                    if more is not None:
                        exps(h, s, 0)
                    if attend:
                        keep_turned(h - 1, 1)
                    if more is not None:
                        exps(h, s, 1)
                    if more:
                        keep_qk(h + 1, 1 - s, 0)
                    if attend:
                        keep_turned(h - 1, 3)
                    if more is not None:
                        exps(h, s, 2)
                    if more:
                        for f in range(1, 4):
                            keep_qk(h + 1, 1 - s, f)

                step(0, 0, attend=False)
                with act.Fori(0, HEADS // 2 - 1) as i:
                    step(2 * i + 1, 1)
                    step(2 * i + 2, 0)
                step(HEADS - 1, 1, more=False)
                step(HEADS, 0, more=None)
                norm_scalar(act, st, n, turns)

            @block.vector
            def _(dve):
                dve.wait_ge(w_split, 1)
                dve.tensor_tensor(ws[0][:, 1], w[0][:], ws[0][:, 0], ALU.subtract).then_inc(w_split, 1)
                split_x_vector(dve, st, xs)
                dve.wait_ge(rest_loaded, 16 * 4)
                dve.tensor_scalar(bias[:, 0, :], bias[:, 0, :], SCALE, None, ALU.mult).then_inc(bq_scaled, 1)

                def keep_v(h, s, j):
                    dve.wait_ge(proj_ready, 6 * h + 5 + j)
                    dve.tensor_copy(v[s][:, 4 * j:4 * j + 4, :].rearrange("p t e -> p (t e)"),
                                    proj[j][:, :]).then_inc(v_ready, 1)

                def head_bias(h, s):
                    dve.tensor_copy(headbias[s][:, :].unsqueeze(2), bias[:, 0:2, bass.ds(h, 1)]).then_inc(hb_ready, 1)

                def maxima(h):
                    for bank in range(3):
                        groups, first = (4, 0) if bank == 0 else (2, 2 * bank + 2)
                        dve.wait_ge(score_ready, 3 * h + bank + 1)
                        dve.tensor_reduce(negmax[:, first:first + groups],
                                          score[bank][:, :].rearrange("p (g k) -> p g k", g=groups),
                                          X_AXIS, ALU.max, negate=True).then_inc(max_ready, 1)

                def normalise(h, s, bank):
                    groups, first = (4, 0) if bank == 0 else (2, 2 * bank + 2)
                    width = BANK // groups
                    dve.wait_ge(exp_ready, 8 * h + first + groups)
                    dve.reciprocal(rinv[:, first:first + groups],
                                   rowsum[:, first:first + groups]).then_inc(rinv_ready, 1)
                    dve.wait_ge(rinv_ready, 3 * h + bank + 1)
                    for g in range(groups):
                        part = probs[s][:, bank * BANK + g * width:bank * BANK + (g + 1) * width]
                        dve.tensor_scalar(part, part, rinv[:, first + g:first + g + 1], None,
                                          ALU.mult).then_inc(probs_ready, 1)

                def keep_turned(h, b):
                    dve.wait_ge(turn_ready, 4 * h + b + 1)
                    dve.tensor_copy(probsT[:, 0, :], turn[0][:, 0:3 * P]).then_inc(probsT_even, 1)

                def keep_z(h, p):
                    dve.wait_ge(z_ready, 2 * h + p + 1)
                    dve.tensor_scalar(zT[:, bass.ds(h, 1), p * BANK:(p + 1) * BANK], zout[p][:, :].unsqueeze(1),
                                      bias[:, 2, bass.ds(h, 1)], None, ALU.add).then_inc(zT_ready, 1)

                def step(h, s, attend=True, more=True):
                    if more:
                        head_bias(h + 1, 1 - s)
                    if more is not None:
                        maxima(h)
                    if attend:
                        keep_turned(h - 1, 0)
                    if more is not None:
                        normalise(h, s, 0)
                    if attend:
                        keep_turned(h - 1, 2)
                    if more is not None:
                        normalise(h, s, 1)
                    if attend:
                        keep_z(h - 1, 0)
                    if more is not None:
                        normalise(h, s, 2)
                    if attend:
                        keep_z(h - 1, 1)
                    if more:
                        keep_v(h + 1, 1 - s, 0)
                        keep_v(h + 1, 1 - s, 1)

                dve.wait_ge(bq_scaled, 1)
                head_bias(0, 0)
                keep_v(0, 0, 0)
                keep_v(0, 0, 1)
                step(0, 0, attend=False)
                with dve.Fori(0, HEADS // 2 - 1) as i:
                    step(2 * i + 1, 1)
                    step(2 * i + 2, 0)
                step(HEADS - 1, 1, more=False)
                step(HEADS, 0, more=None)
                for t in range(TILES):
                    last = dve.tensor_tensor(st.x[:, t, :], st.x[:, t, :], bo[:, :], ALU.add)
                last.then_inc(bo_added, 1)
                dve.wait_ge(bo_added, 1)
                norm_vector(dve, st, n, out_part)



PAIRS = HEADS // 2


def cross_tensors(mem, sem, name, vw=None):
    class C:
        pass
    c = C()
    c.rows = mem.sb(f"{name}_rows", [P, TILES, HEADS, KEYS])
    c.vw = vw if vw is not None else mem.sb(f"{name}_vw", [P, BATCH, PAIRS, DM])
    c.max = mem.sb(f"{name}_max", [P, TILES, HEADS])
    c.sum = mem.sb(f"{name}_sum", [P, TILES, HEADS])
    c.inv = mem.sb(f"{name}_inv", [P, TILES, HEADS])
    c.rowsT = mem.sb(f"{name}_rowsT", [P, 2, PAIRS, P])
    c.max_ready = sem(f"{name}_max_ready")
    c.shifted = sem(f"{name}_shifted")
    c.exp_ready = sem(f"{name}_exp_ready")
    c.sum_ready = sem(f"{name}_sum_ready")
    c.inv_ready = sem(f"{name}_inv_ready")
    c.probs_ready = sem(f"{name}_probs_ready")
    c.turned = sem(f"{name}_rows_turned")
    c.rowsT_ready = sem(f"{name}_rowsT_ready")
    return c


def over_keys(a):
    return a.unsqueeze(2).broadcast_to([P, a.shape[1], KEYS])


def cross_normalise_sum(dve, c, t):
    dve.wait_ge(c.exp_ready, t + 1)
    dve.tensor_reduce(c.sum[:, t, :], c.rows[:, t, :, :], X_AXIS, ALU.add).then_inc(c.sum_ready, 1)
    dve.wait_ge(c.sum_ready, t + 1)
    dve.reciprocal(c.inv[:, t, :], c.sum[:, t, :]).then_inc(c.inv_ready, 1)


def cross_exp(act, c, t):
    act.wait_ge(c.shifted, t + 1)
    act.activation(c.rows[:, t, :, :], c.rows[:, t, :, :], ACT.Exp).then_inc(c.exp_ready, 1)


def cross_weights(pool, c, t):
    pool.wait_ge(c.inv_ready, t + 1)
    pool.tensor_tensor(c.rows[:, t, :, :], c.rows[:, t, :, :], over_keys(c.inv[:, t, :]),
                       ALU.mult).then_inc(c.probs_ready, 1)


def cross_turn(pe, st, c, turn, t, probs=None):
    pe.wait_ge(c.probs_ready, probs or t + 1)
    if t >= 1:
        pe.wait_ge(c.rowsT_ready, 2 * t)
    for g in range(PAIRS):
        last = pe.transpose(turn[g // 4][:, (g % 4) * P:(g % 4 + 1) * P],
                            c.rows[:, t, 2 * g:2 * g + 2, :].rearrange("p h k -> p (h k)"), st.ident[:])
        if g % 4 == 3:
            last.then_inc(c.turned, 1)


def cross_keep(act, c, turn, t):
    for j in range(2):
        act.wait_ge(c.turned, 2 * t + j + 1)
        act.activation(c.rowsT[:, t % 2, 4 * j:4 * j + 4, :],
                       turn[j][:, :].rearrange("p (g n) -> p g n", g=4), ACT.Copy).then_inc(c.rowsT_ready, 1)


def cross_out(pe, c, n, part, t):
    pe.wait_ge(c.rowsT_ready, 2 * t + 2)
    if t >= 2:
        pe.wait_ge(n.summed, n.base + t - 1)
    for g in range(PAIRS):
        last = pe.matmul(part(t), c.rowsT[:, t % 2, g, :], c.vw[:, t // 2, g, :],
                         start=g == 0, stop=g == PAIRS - 1)
    last.then_inc(n.out_ready, 1)



def context_attention(nc, st, sem, d):
    SCALE = float(HD) ** -0.5
    RMS_EPS = 1e-6
    KV = 4
    GROUP = HEADS // KV
    with Memory(nc) as mem:
        c = cross_tensors(mem, sem, "ca")
        xs = split_x_tensors(mem, sem, "ca")
        w = [mem.sb(f"ca_w{s}", [P, DC, HD]) for s in range(2)]
        ws = [mem.sb(f"ca_ws{s}", [P, 2, DC, HD], F32R) for s in range(2)]
        wo = mem.sb("ca_wo", [P, HEADS, DM])
        wk = mem.sb("ca_wk", [P, DC, KV * HD])
        wv = mem.sb("ca_wv", [P, DC, KV * HD])
        bk = mem.sb("ca_bk", [P, KV * HD])
        bq = mem.sb("ca_bq", [P, HEADS])
        headbias = mem.sb("ca_headbias", [P, 4])
        bv = mem.sb("ca_bv", [P, KV])
        norms = mem.sb("ca_norms", [P, 2])
        gain = mem.sb("ca_gain", [P, 1])
        amask = mem.sb("ca_amask", [P, 2, KEYS])
        ones = mem.sb("ca_ones", [P, KEYS])
        rms_eps = mem.sb("ca_rms_eps", [P, 1])
        k = mem.sb("ca_k", [P, 2, KV * HD])
        ksq = mem.sb("ca_ksq", [P, 2, KV * HD])
        kss = mem.sb("ca_kss", [P, 2 * KV])
        kstd = mem.sb("ca_kstd", [P, 2 * KV])
        krms = mem.sb("ca_krms", [P, 2 * KV])
        kT = mem.sb("ca_kT", [P, KV, CTX])
        vT = mem.sb("ca_vT", [P, KV, CTX])
        qT = [mem.sb(f"ca_qT{s}", [P, TOK]) for s in range(2)]
        qsq = [mem.sb(f"ca_qsq{s}", [P, TOK]) for s in range(2)]
        qmean = mem.sb("ca_qmean", [P, 4, TILES])
        qrms = mem.sb("ca_qrms", [P, 4, TILES])
        cells = mem.sb("ca_cells", [P, 4, TILES, KEYS])
        rowmax = mem.sb("ca_rowmax", [P, 4, TILES])
        rowsum = mem.sb("ca_rowsum", [P, 4, TILES])
        rowinv = mem.sb("ca_rowinv", [P, 4, TILES])
        proj = [mem.psum(f"ca_proj{i}", [P, BANK]) for i in range(4)]
        score = [mem.psum(f"ca_score{i}", [P, BANK]) for i in range(2)]
        square = [mem.psum(f"ca_square{i}", [P, BANK]) for i in range(2)]
        n = norm_tensors(mem, st, "ca")
        part = lambda t: score[t % 2][:, 0:DM]
        turns = [square[i][:, 0:DM].rearrange("p (c n) -> p c n", c=DC) for i in range(2)]

        w_loaded = [sem(f"ca_w_loaded{s}") for s in range(2)]
        w_split = sem("ca_w_split")
        kv_loaded = sem("ca_kv_loaded")
        wo_loaded = sem("ca_wo_loaded")
        k_projected = sem("ca_k_projected")
        v_projected = sem("ca_v_projected")
        k_biased = sem("ca_k_biased")
        k_squared = sem("ca_k_squared")
        k_summed = sem("ca_k_summed")
        k_std = sem("ca_k_std")
        k_rms = sem("ca_k_rms")
        k_normed = sem("ca_k_normed")
        k_turned = sem("ca_k_turned")
        kT_ready = sem("ca_kT_ready")
        vT_ready = sem("ca_vT_ready")
        vw_done = sem("ca_vw_done")
        vw_ready = sem("ca_vw_ready")
        consts_ready = sem("ca_consts_ready")
        q_projected = sem("ca_q_projected")
        q_ready = sem("ca_q_ready")
        qsq_ready = sem("ca_qsq_ready")
        scored = sem("ca_scored")
        headbias_ready = sem("ca_headbias_ready")
        qmean_ready = sem("ca_qmean_ready")
        qrms_ready = sem("ca_qrms_ready")
        scaled = sem("ca_scaled")
        masked = sem("ca_masked")

        with nc.Block() as block:
            @block.sync
            def _(sp):
                for dst, src in ((st.ctxT[:], "ctxT"), (wk[:], "ca_wk"), (wv[:], "ca_wv"), (bv[:], "ca_bv"),
                                 (norms[:], "ca_norms"), (bq[:], "ca_bq"), (amask[:], "ca_amask")):
                    sp.dma_start(dst, d[src]).then_inc(kv_loaded, 16)
                sp.dma_start(bk[:], d["ca_bk"].partition_broadcast(P)).then_inc(kv_loaded, 16)
                sp.dma_start(w[0][:], d["ca_wq"][0]).then_inc(w_loaded[0], 16)
                sp.dma_start(w[1][:], d["ca_wq"][1]).then_inc(w_loaded[1], 16)
                sp.dma_start(wo[:], d["ca_wo"]).then_inc(wo_loaded, 16)
                def load(i, u):
                    sp.wait_ge(w_split, 8 * i + 2 * u + 2)
                    sp.dma_start(w[u % 2][:], d["ca_wq"][4 * i + u + 2]).then_inc(w_loaded[u % 2], 16)
                with sp.Fori(0, KV - 1) as i:
                    for u in range(GROUP):
                        load(i, u)
                load(KV - 1, 0)
                load(KV - 1, 1)

            @block.tensor
            def _(pe):
                pe.wait_ge(kv_loaded, 16 * 8)
                for t in range(2):
                    for j in range(DC):
                        last = pe.matmul(proj[t][:, :], st.ctxT[:, j, tile_cols(t)], wk[:, j, :],
                                         start=j == 0, stop=j == DC - 1)
                    last.then_inc(k_projected, 1)
                for g in range(KV):
                    for j in range(DC):
                        last = pe.matmul(proj[2 + g // 2][:, (g % 2) * CTX:(g % 2 + 1) * CTX],
                                         wv[:, j, g * HD:(g + 1) * HD], st.ctxT[:, j, :],
                                         start=j == 0, stop=j == DC - 1)
                    if g % 2:
                        last.then_inc(v_projected, 1)
                pe.wait_ge(k_normed, 1)
                for g in range(KV):
                    for t in range(2):
                        last = pe.transpose(square[g // 2][:, (g % 2) * CTX + t * P:(g % 2) * CTX + (t + 1) * P],
                                            k[:, t, g * HD:(g + 1) * HD], st.ident[:])
                    if g % 2:
                        last.then_inc(k_turned, 1)
                pe.wait_ge(vT_ready, 2)
                pe.wait_ge(wo_loaded, 16)
                for r in range(2 * PAIRS):
                    pair, half = r // 2, r % 2
                    if r >= 2:
                        pe.wait_ge(vw_ready, r - 1)
                    for b in range(2):
                        for s in range(2):
                            h = 2 * pair + s
                            last = pe.matmul(score[r % 2][s * KEYS:(s + 1) * KEYS, b * DM:(b + 1) * DM],
                                             vT[:, h // GROUP, (2 * half + b) * KEYS:(2 * half + b + 1) * KEYS],
                                             wo[:, h, :], start=True, stop=True)
                    last.then_inc(vw_done, 1)

                def project(h, s):
                    pe.wait_ge(w_split, 2 * h + 2)
                    for f in range(2):
                        wait_past(pe, q_ready, 2 * h + f - 3)
                        for j, (k, m), first, end in products():
                            last = pe.matmul(proj[2 * s + f][:, :], ws[s][:, k, j, :],
                                             xs.parts[:, m, j, f * BANK:(f + 1) * BANK], start=first, stop=end)
                        last.then_inc(q_projected, 1)

                def scores(h, i, s):
                    pe.wait_ge(qsq_ready, 2 * h + 2)
                    wait_past(pe, qmean_ready, h - 1)
                    for t in range(TILES):
                        pe.matmul(square[s][:, t * KEYS:(t + 1) * KEYS], qsq[s][:, tile_cols(t)], ones[:, :], start=True, stop=True)
                    wait_past(pe, scaled, h - 1)
                    for t in range(TILES):
                        last = pe.matmul(score[s][:, t * KEYS:(t + 1) * KEYS], qT[s][:, tile_cols(t)],
                                         kT[:, bass.ds(i, 1), (t // 2) * KEYS:(t // 2 + 1) * KEYS].squeeze(1),
                                         start=True, stop=True)
                    last.then_inc(scored, 1)

                pe.wait_ge(xs.lo_ready, HALVES)
                pe.wait_ge(kT_ready, 2)
                pe.wait_ge(k_biased, 2)
                pe.wait_ge(vw_ready, 2 * PAIRS)
                project(0, 0)

                def step(i, u, more=True):
                    h = GROUP * i + u
                    if more:
                        project(h + 1, (u + 1) % 2)
                    scores(h, i, u % 2)
                for u in range(GROUP):
                    step(0, u)
                with pe.Fori(1, KV - 1) as i:
                    for u in range(GROUP):
                        step(i, u)
                for u in range(GROUP):
                    step(KV - 1, u, u < GROUP - 1)
                pe.wait_ge(scaled, HEADS)
                for t in range(TILES + 2):
                    if t < TILES:
                        cross_turn(pe, st, c, proj[0:2], t, HEADS)
                    if 0 <= t - 1 < TILES:
                        cross_out(pe, c, n, part, t - 1)
                    if t >= 3:
                        norm_tensor(pe, st, n, turns, t - 3)
                norm_tensor(pe, st, n, turns, TILES - 1)

            @block.scalar
            def _(act):
                split_x_scalar(act, st, xs)
                act.wait_ge(consts_ready, 1)
                for j in range(2):
                    act.wait_ge(v_projected, j + 1)
                    for g in range(2 * j, 2 * j + 2):
                        last = act.activation(vT[:, g, :], proj[2 + j][:, (g % 2) * CTX:(g % 2 + 1) * CTX],
                                              ACT.Identity, bias=bv[:, g:g + 1])
                    last.then_inc(vT_ready, 1)
                act.wait_ge(k_summed, 1)
                act.activation(kstd[:, :], kss[:, :], ACT.Sqrt, bias=rms_eps[:, :],
                               scale=1.0 / HD).then_inc(k_std, 1)
                for j in range(2):
                    act.wait_ge(k_turned, j + 1)
                    act.activation(kT[:, 2 * j:2 * j + 2, :], square[j][:, :].rearrange("p (g n) -> p g n", g=2),
                                   ACT.Copy, scale=gain[:, :]).then_inc(kT_ready, 1)

                def keep_q(h, s, slot):
                    act.wait_ge(headbias_ready, h + 1)
                    wait_past(act, scored, h - 1)
                    for f in range(2):
                        cols = slice(f * BANK, (f + 1) * BANK)
                        act.wait_ge(q_projected, 2 * h + f + 1)
                        act.activation(qT[s][:, cols], proj[2 * s + f][:, :], ACT.Identity,
                                       bias=headbias[:, slot:slot + 1]).then_inc(q_ready, 1)
                    for f in range(2):
                        cols = slice(f * BANK, (f + 1) * BANK)
                        act.wait_ge(q_ready, 2 * h + f + 1)
                        act.activation(qsq[s][:, cols], qT[s][:, cols], ACT.Square).then_inc(qsq_ready, 1)

                def exps(h, slot):
                    act.wait_ge(c.shifted, h + 1)
                    act.activation(cells[:, slot, :, :], cells[:, slot, :, :], ACT.Exp).then_inc(c.exp_ready, 1)

                keep_q(0, 0, 0)

                def step(h, u):
                    if not isinstance(h, int) or h + 1 < HEADS:
                        keep_q(h + 1, (u + 1) % 2, (u + 1) % 4)
                    if not isinstance(h, int) or h >= 2:
                        exps(h - 2, (u - 2) % 4)
                for h in range(GROUP):
                    step(h, h)
                with act.Fori(1, KV - 1) as i:
                    for u in range(GROUP):
                        step(GROUP * i + u, u)
                for h in range(HEADS - GROUP, HEADS + 2):
                    step(h, h % 4)
                for t in range(TILES + 4):
                    if 0 <= t - 1 < TILES:
                        cross_keep(act, c, proj[0:2], t - 1)
                    if 0 <= t - 4:
                        norm_keep(act, st, n, turns, t - 4)

            @block.vector
            def _(dve):
                dve.memset(ones[:], 1.0)
                dve.memset(rms_eps[:], RMS_EPS)
                split_x_vector(dve, st, xs)
                dve.wait_ge(kv_loaded, 16 * 8)
                dve.scalar_tensor_tensor(gain[:], norms[:, 0:1], SCALE, norms[:, 1:2],
                                         ALU.mult, ALU.mult).then_inc(consts_ready, 1)
                for t in range(2):
                    dve.wait_ge(k_projected, t + 1)
                    dve.tensor_tensor(k[:, t, :], proj[t][:, :], bk[:, :], ALU.add).then_inc(k_biased, 1)
                dve.wait_ge(k_biased, 2)
                dve.tensor_tensor(ksq[:], k[:], k[:], ALU.mult).then_inc(k_squared, 1)
                dve.wait_ge(k_squared, 1)
                dve.tensor_reduce(kss[:, :], ksq[:].rearrange("p t (g e) -> p (t g) e", g=KV),
                                  X_AXIS, ALU.add).then_inc(k_summed, 1)
                dve.wait_ge(k_std, 1)
                dve.reciprocal(krms[:, :], kstd[:, :]).then_inc(k_rms, 1)
                dve.wait_ge(k_rms, 1)
                kk = k[:].rearrange("p t (g e) -> p (t g) e", g=KV)
                dve.tensor_tensor(kk, kk, krms[:, :].unsqueeze(2).broadcast_to([P, 2 * KV, HD]),
                                  ALU.mult).then_inc(k_normed, 1)
                for r in range(2 * PAIRS):
                    dve.wait_ge(vw_done, r + 1)
                    dve.tensor_copy(c.vw[:, 2 * (r % 2):2 * (r % 2) + 2, r // 2, :],
                                    score[r % 2][:, :].rearrange("p (b n) -> p b n", b=2)).then_inc(vw_ready, 1)

                def head_bias(h, slot):
                    dve.tensor_copy(headbias[:, slot:slot + 1], bq[:, bass.ds(h, 1)]).then_inc(headbias_ready, 1)

                def mean_squares(h, s, slot):
                    dve.wait_ge(scored, h + 1)
                    sums = square[s][:, :].rearrange("p (t k) -> p t k", t=TILES)[:, :, 0]
                    dve.tensor_scalar(qmean[:, slot, :], sums, 1.0 / HD, RMS_EPS,
                                      ALU.mult, ALU.add).then_inc(qmean_ready, 1)

                def scale_scores(h, s, slot):
                    dve.wait_ge(qrms_ready, h + 1)
                    wait_past(dve, c.probs_ready, h - 3)
                    dve.tensor_tensor(cells[:, slot, :, :], score[s][:, :].rearrange("p (t k) -> p t k", t=TILES),
                                      over_keys(qrms[:, slot, :]), ALU.mult).then_inc(scaled, 1)

                def shift(h, slot):
                    dve.wait_ge(masked, h + 1)
                    dve.tensor_reduce(rowmax[:, slot, :], cells[:, slot, :, :], X_AXIS, ALU.max).then_inc(c.max_ready, 1)
                    dve.wait_ge(c.max_ready, h + 1)
                    dve.tensor_tensor(cells[:, slot, :, :], cells[:, slot, :, :], over_keys(rowmax[:, slot, :]),
                                      ALU.subtract).then_inc(c.shifted, 1)

                def normalise(h, slot):
                    dve.wait_ge(c.exp_ready, h + 1)
                    dve.tensor_reduce(rowsum[:, slot, :], cells[:, slot, :, :], X_AXIS, ALU.add).then_inc(c.sum_ready, 1)
                    dve.wait_ge(c.sum_ready, h + 1)
                    dve.reciprocal(rowinv[:, slot, :], rowsum[:, slot, :]).then_inc(c.inv_ready, 1)
                    dve.wait_ge(c.inv_ready, h + 1)
                    dve.tensor_tensor(c.rows[:, :, bass.ds(h, 1), :].squeeze(2), cells[:, slot, :, :],
                                      over_keys(rowinv[:, slot, :]), ALU.mult).then_inc(c.probs_ready, 1)

                head_bias(0, 0)
                head_bias(1, 1)

                def step(h, u):
                    inside = not isinstance(h, int)
                    if inside or h < HEADS:
                        mean_squares(h, u % 2, u)
                    if inside or h + 2 < HEADS:
                        head_bias(h + 2, (u + 2) % 4)
                    if inside or 0 <= h - 1 < HEADS:
                        scale_scores(h - 1, (u - 1) % 2, (u - 1) % 4)
                    if inside or 0 <= h - 2 < HEADS:
                        shift(h - 2, (u - 2) % 4)
                    if inside or 0 <= h - 3 < HEADS:
                        normalise(h - 3, (u - 3) % 4)
                for h in range(GROUP):
                    step(h, h)
                with dve.Fori(1, KV - 1) as i:
                    for u in range(GROUP):
                        step(GROUP * i + u, u)
                for h in range(HEADS - GROUP, HEADS + 3):
                    step(h, h % 4)
                for t in range(TILES + 3):
                    if 0 <= t - 2 < TILES:
                        norm_sum(dve, st, n, part, t - 2)
                    if 0 <= t - 3:
                        norm_apply(dve, st, n, t - 3)

            @block.gpsimd
            def _(pool):
                def split_w(h, s, loads):
                    pool.wait_ge(w_loaded[s], 16 * loads)
                    wait_past(pool, q_projected, 2 * h - 2)
                    split_on(pool, ones_like(st, DC, HD), w[s][:], ws[s][:, 0], ws[s][:, 1], w_split, 2 * h)
                split_w(0, 0, 1)
                split_w(1, 1, 1)

                def q_rms(h, slot):
                    pool.wait_ge(qmean_ready, h + 1)
                    pool.tensor_tensor(qrms[:, slot, :], qmean[:, slot, :], st.minus_half[:, :].broadcast_to([P, TILES]),
                                       ALU.pow).then_inc(qrms_ready, 1)

                def add_mask(h, slot):
                    pool.wait_ge(scaled, h + 1)
                    cell = cells[:, slot, :, :].rearrange("p (b q) k -> p b (q k)", q=2)
                    pool.tensor_tensor(cell, cell, amask[:].rearrange("p q k -> p (q k)").unsqueeze(1).broadcast_to(
                        [P, BATCH, 2 * KEYS]), ALU.add).then_inc(masked, 1)

                def step(h, u, loads):
                    inside = not isinstance(h, int)
                    if inside or h + 2 < HEADS:
                        split_w(h + 2, u % 2, loads)
                    if inside or h < HEADS:
                        q_rms(h, u)
                    if inside or 0 <= h - 1:
                        add_mask(h - 1, (u - 1) % 4)
                for h in range(GROUP):
                    step(h, h, 2 + h // 2)
                with pool.Fori(1, KV - 1) as i:
                    for u in range(GROUP):
                        step(GROUP * i + u, u, 2 * i + 2 + u // 2)
                for h in range(HEADS - GROUP, HEADS + 1):
                    step(h, h % 4, 2 + h // 2)
                norm_pool(pool, st, n)



VD = DM // HEADS
VCOLS = VD + 1


def recurrent_attention(nc, st, sem, d):
    name = "ra"
    COUNT = HEADS // 2
    with Memory(nc) as mem:
        wq = mem.sb(f"{name}_wq", [P, DC, DM])
        wk = mem.sb(f"{name}_wk", [P, DC, DM])
        wv = mem.sb(f"{name}_wv", [P, DC, DM])
        wo = mem.sb(f"{name}_wo", [P, DC, DM])
        rowmask = mem.sb(f"{name}_rowmask", [P, COUNT])
        qT = mem.sb(f"{name}_qT", [P, 2, TOK])
        kT = mem.sb(f"{name}_kT", [P, 2, TOK])
        qhead = [mem.sb(f"{name}_qhead{s}", [P, TOK]) for s in range(2)]
        v = mem.sb(f"{name}_v", [P, TILES, HEADS, VCOLS])
        shift = mem.sb(f"{name}_shift", [P, 4, 2])
        probs = mem.sb(f"{name}_probs", [P, 4, BANK])
        probsT = mem.sb(f"{name}_probsT", [P, 2, BANK])
        heads_out = mem.sb(f"{name}_heads_out", [P, TILES, 2, COUNT, VCOLS])
        y = mem.sb(f"{name}_y", [P, TILES, DM])
        rinv = mem.sb(f"{name}_rinv", [P, TILES, 2 * COUNT])
        yT = mem.sb(f"{name}_yT", [P, 2, DC, P])
        score = [mem.psum(f"{name}_score{i}", [P, BANK]) for i in range(4)]
        turn = [mem.psum(f"{name}_turn{i}", [P, BANK]) for i in range(2)]
        out = [mem.psum(f"{name}_out{i}", [P, BANK]) for i in range(2)]
        n = norm_tensors(mem, st, name)

        loaded = sem(f"{name}_loaded")
        consts_ready = sem(f"{name}_consts_ready")
        q_projected = sem(f"{name}_q_projected")
        k_projected = sem(f"{name}_k_projected")
        v_projected = sem(f"{name}_v_projected")
        crossed = sem(f"{name}_crossed")
        qk_ready = sem(f"{name}_qk_ready")
        v_ready = sem(f"{name}_v_ready")
        qhead_ready = sem(f"{name}_qhead_ready")
        scored = sem(f"{name}_scored")
        shift_ready = sem(f"{name}_shift_ready")
        exp_ready = sem(f"{name}_exp_ready")
        probs_turned = sem(f"{name}_probs_turned")
        probsT_even = sem(f"{name}_probsT_even")
        probsT_odd = sem(f"{name}_probsT_odd")
        weighed = sem(f"{name}_weighed")
        heads_kept = sem(f"{name}_heads_kept")
        chain = sem(f"{name}_chain")
        y_ready = sem(f"{name}_y_ready")
        y_turned = sem(f"{name}_y_turned")
        yT_ready = sem(f"{name}_yT_ready")

        part = lambda t: score[t % 2][:, 0:DM]
        yturn = [out[i][:, 0:DM].rearrange("p (c n) -> p c n", c=DC) for i in range(2)]
        turns = [turn[i][:, 0:DM].rearrange("p (c n) -> p c n", c=DC) for i in range(2)]
        widths = (P, SEQ)
        block_at = {(0, 0): 0, (0, 1): P, (1, 1): 2 * P}
        turned_cols = P * len(block_at)

        roww = mem.sb(f"{name}_roww", [P, 3, 2])
        rowscale = mem.sb(f"{name}_rowscale", [P, 2])
        swap = mem.sb(f"{name}_swap", [P, 2])
        factors = mem.sb(f"{name}_factors", [P, 4, 2])
        cross = mem.sb(f"{name}_cross", [P, 4, BANK])
        n_loads = 6

        def ahead(i, u, lead):
            return (i, u + lead) if u + lead < 8 else (i + 1, u + lead - 8)

        with nc.Block() as block:
            @block.sync
            def _(sp):
                for dst, src in [(wq, f"{name}_wq"), (wk, f"{name}_wk"), (wv, f"{name}_wv"), (wo, f"{name}_wo"),
                                 (rowmask, f"{name}_rowmask"), (roww, f"{name}_roww")]:
                    sp.dma_start(dst[:], d[src]).then_inc(loaded, 16)

            @block.tensor
            def _(pe):
                pe.wait_ge(loaded, 16 * n_loads)
                for j in range(4):
                    s, f = j // 2, j % 2
                    for w, banks, ready in ((wq, score[0:2], q_projected), (wk, score[2:4], k_projected)):
                        if j >= 2 and w is wq:
                            pe.wait_ge(qk_ready, 2 * (j - 2) + 2)
                        for c in range(DC):
                            last = pe.matmul(banks[j % 2][:, :], w[:, c, tile_cols(s)],
                                             st.xT[:, c, f * BANK:(f + 1) * BANK], start=c == 0, stop=c == DC - 1)
                        last.then_inc(ready, 1)
                for t in range(TILES):
                    if t >= 2:
                        pe.wait_ge(v_ready, t - 1)
                    for c in range(DC):
                        last = pe.matmul(turn[t % 2][:, 0:DM], st.xT[:, c, tile_cols(t)], wv[:, c, :],
                                         start=c == 0, stop=c == DC - 1)
                    last.then_inc(v_projected, 1)

                def scores(i, u):
                    s, b = u // 4, u % 4
                    if b == 0:
                        pe.wait_ge(qhead_ready, 2 * i + s + 1)
                    k0 = b * SEQ
                    for q, width in enumerate(widths):
                        o = score[u % 4][:, q * SEQ:q * SEQ + width]
                        last = pe.matmul(o, qhead[s][:, k0 + q * P:k0 + (q + 1) * P],
                                         kT[:, s, k0:k0 + width], start=True, stop=False)
                        last = pe.matmul(o[:, width - P:width], st.identb[:], st.mask[:], start=False, stop=True)
                    last.then_inc(scored, 1)

                def turn_probs(i, u):
                    unit = 8 * i + u
                    pe.wait_ge(exp_ready, 2 * unit + 2)
                    wait_past(pe, (probsT_even, probsT_odd)[u % 2], 4 * i + u // 2)
                    for (kt, q), at in block_at.items():
                        last = pe.transpose(turn[u % 2][:, at:at + P],
                                            probs[:, u % 4, q * SEQ + kt * P:q * SEQ + (kt + 1) * P], st.ident[:])
                    last.then_inc(probs_turned, 1)

                def weigh(i, u, fresh):
                    s, b = u // 4, u % 4
                    if b == 0 and not fresh:
                        pe.wait_ge(heads_kept, 2 * i + s - 1)
                    pe.wait_ge((probsT_even, probsT_odd)[u % 2], 4 * i + u // 2 + 1)
                    for q in range(2):
                        o = out[s][:, (2 * b + q) * VCOLS:(2 * b + q + 1) * VCOLS]
                        kts = [kt for kt in range(2) if (kt, q) in block_at]
                        for kt in kts:
                            at = block_at[kt, q]
                            values = v[:, 2 * b + kt, bass.ds(s * COUNT + i, 1), :]
                            last = pe.matmul(o, probsT[:, u % 2, at:at + P], values.squeeze(1),
                                             start=kt == 0, stop=kt == kts[-1])
                    if b == 3:
                        last.then_inc(weighed, 1)

                def units(i, first=False, final=False):
                    for u in range(8):
                        if not (final and u + 3 >= 8):
                            scores(*ahead(i, u, 3))
                        turn_probs(i, u)
                        if u > 0:
                            weigh(i, u - 1, first)
                        elif not first:
                            weigh(i - 1, 7, False)

                pe.wait_ge(qk_ready, 8)
                pe.wait_ge(v_ready, TILES)
                for u in range(3):
                    scores(0, u)
                units(0, first=True)
                with pe.Fori(1, COUNT - 1) as i:
                    units(i)
                units(COUNT - 1, final=True)
                weigh(COUNT - 1, 7, False)

                pe.wait_ge(heads_kept, 2 * COUNT)
                for t in range(TILES + 2):
                    if t < TILES:
                        pe.wait_ge(y_ready, t + 1)
                        if t >= 2:
                            pe.wait_ge(yT_ready, t - 1)
                        for c in range(DC):
                            last = pe.transpose(yturn[t % 2][:, c, :], y[:, t, tile_cols(c)], st.ident[:])
                        last.then_inc(y_turned, 1)
                    if 0 <= t - 1 < TILES:
                        r = t - 1
                        pe.wait_ge(yT_ready, r + 1)
                        if r >= 2:
                            pe.wait_ge(n.summed, n.base + r - 1)
                        for c in range(DC):
                            last = pe.matmul(part(r), yT[:, r % 2, c, :], wo[:, c, :], start=c == 0, stop=c == DC - 1)
                        last.then_inc(n.out_ready, 1)
                    if t >= 3:
                        norm_tensor(pe, st, n, turns, t - 3)
                norm_tensor(pe, st, n, turns, TILES - 1)

            @block.scalar
            def _(act):
                act.wait_ge(loaded, 16 * n_loads)
                act.wait_ge(chain, 1)
                act.activation(rowscale[:], roww[:, 0, :], ACT.Sqrt).then_inc(consts_ready, 1)
                act.wait_ge(chain, 7)
                for j in range(4):
                    s = j // 2
                    act.wait_ge(k_projected, j + 1)
                    if j >= 2:
                        act.wait_ge(qk_ready, 2 * (j - 2) + 2)
                    act.activation(cross[:, 2 * (j % 2), :], score[2 + j % 2][:, :], ACT.Copy,
                                   scale=factors[:, 1, s:s + 1]).then_inc(crossed, 1)
                    act.activation(cross[:, 2 * (j % 2) + 1, :], score[j % 2][:, :], ACT.Copy,
                                   scale=factors[:, 3, s:s + 1]).then_inc(crossed, 1)
                for t in range(TILES):
                    act.wait_ge(v_projected, t + 1)
                    act.activation(v[:, t, :, 0:VD], turn[t % 2][:, 0:DM].rearrange("p (h e) -> p h e", h=HEADS),
                                   ACT.Copy).then_inc(v_ready, 1)

                def exps(i, u, fresh=False):
                    unit = 8 * i + u
                    act.wait_ge(shift_ready, 2 * unit + 2)
                    if not fresh:
                        act.wait_ge(probs_turned, unit - 3)
                    for q, width in enumerate(widths):
                        act.activation(probs[:, u % 4, q * SEQ:q * SEQ + width], score[u % 4][:, q * SEQ:q * SEQ + width],
                                       ACT.Exp, bias=shift[:, u % 4, q:q + 1]).then_inc(exp_ready, 1)

                def keep_odd(i, u):
                    act.wait_ge(probs_turned, 8 * i + u + 1)
                    act.activation(probsT[:, 1, 0:turned_cols], turn[1][:, 0:turned_cols],
                                   ACT.Copy).then_inc(probsT_odd, 1)

                def units(i, first=False, final=False):
                    for u in range(8):
                        if not (final and u + 1 >= 8):
                            exps(*ahead(i, u, 1), fresh=first and u + 1 < 4)
                        if u % 2:
                            keep_odd(i, u)

                exps(0, 0, fresh=True)
                units(0, first=True)
                with act.Fori(1, COUNT - 1) as i:
                    units(i)
                units(COUNT - 1, final=True)
                for t in range(TILES + 4):
                    if t < TILES:
                        act.wait_ge(y_turned, t + 1)
                        act.activation(yT[:, t % 2, :, :], yturn[t % 2], ACT.Copy).then_inc(yT_ready, 1)
                    if 0 <= t - 4:
                        norm_keep(act, st, n, turns, t - 4)

            @block.vector
            def _(dve):
                links = [0]

                def link(ins):
                    links[0] += 1
                    ins.then_inc(chain, 1)
                    dve.wait_ge(chain, links[0])

                dve.wait_ge(loaded, 16 * n_loads)
                link(dve.tensor_scalar(roww[:, 0, :], roww[:, 0, :], 1e-8, None, ALU.max))
                link(dve.scalar_tensor_tensor(swap[:], roww[:, 1, :], 0.1, roww[:, 2, :], ALU.is_gt, ALU.mult))
                dve.wait_ge(consts_ready, 1)
                link(dve.tensor_tensor(factors[:, 3, :], rowscale[:], swap[:], ALU.mult))
                link(dve.tensor_tensor(factors[:, 2, :], rowscale[:], factors[:, 3, :], ALU.subtract))
                link(dve.tensor_scalar(factors[:, 1, :], factors[:, 3, :], float(VD) ** -0.5, None, ALU.mult))
                link(dve.tensor_scalar(factors[:, 0, :], factors[:, 2, :], float(VD) ** -0.5, None, ALU.mult))
                link(dve.memset(v[:, :, :, VD:VCOLS], 1.0))
                for j in range(4):
                    s, f = j // 2, j % 2
                    cols = slice(f * BANK, (f + 1) * BANK)
                    dve.wait_ge(crossed, 2 * j + 2)
                    dve.scalar_tensor_tensor(qT[:, s, cols], score[j % 2][:, :], factors[:, 0, s:s + 1],
                                             cross[:, 2 * (j % 2), :], ALU.mult, ALU.add).then_inc(qk_ready, 1)
                    dve.scalar_tensor_tensor(kT[:, s, cols], score[2 + j % 2][:, :], factors[:, 2, s:s + 1],
                                             cross[:, 2 * (j % 2) + 1, :], ALU.mult, ALU.add).then_inc(qk_ready, 1)
                dve.wait_ge(qk_ready, 8)

                def mask_q(i, s):
                    dve.tensor_scalar(qhead[s][:, :], qT[:, s, :], rowmask[:, bass.ds(i, 1)], None,
                                      ALU.mult).then_inc(qhead_ready, 1)

                def maxima(i, u, fresh=False):
                    unit = 8 * i + u
                    dve.wait_ge(scored, unit + 1)
                    if not fresh:
                        dve.wait_ge(exp_ready, 2 * unit - 6)
                    for q, width in enumerate(widths):
                        src = score[u % 4][:, q * SEQ:q * SEQ + width]
                        dve.tensor_reduce(shift[:, u % 4, q:q + 1], src, X_AXIS, ALU.max,
                                          negate=True).then_inc(shift_ready, 1)

                def keep_even(i, u):
                    dve.wait_ge(probs_turned, 8 * i + u + 1)
                    dve.tensor_copy(probsT[:, 0, 0:turned_cols], turn[0][:, 0:turned_cols]).then_inc(probsT_even, 1)

                def keep_heads(i, s):
                    dve.wait_ge(weighed, 2 * i + s + 1)
                    dve.tensor_scalar(heads_out[:, :, s, bass.ds(i, 1), :].squeeze(2),
                                      out[s][:, 0:TILES * VCOLS].rearrange("p (t e) -> p t e", t=TILES),
                                      1.0, None, ALU.mult).then_inc(heads_kept, 1)

                def units(i, first=False, final=False):
                    for u in range(8):
                        if not (final and u + 2 >= 8):
                            maxima(*ahead(i, u, 2), fresh=first and u + 2 < 4)
                        if u % 2 == 0:
                            keep_even(i, u)
                        if u == 1 and not first:
                            keep_heads(i - 1, 1)
                        if u in (1, 5) and not final:
                            dve.wait_ge(scored, 8 * i + u + 3)
                            mask_q(i + 1, u // 4)
                        if u == 5:
                            keep_heads(i, 0)

                mask_q(0, 0)
                mask_q(0, 1)
                maxima(0, 0, fresh=True)
                maxima(0, 1, fresh=True)
                units(0, first=True)
                with dve.Fori(1, COUNT - 1) as i:
                    units(i)
                units(COUNT - 1, final=True)
                keep_heads(COUNT - 1, 1)

                dve.wait_ge(heads_kept, 2 * COUNT)
                for t in range(TILES + 3):
                    if t < TILES:
                        o = heads_out[:, t, :, :, :]
                        r = rinv[:, t, :].rearrange("p (s h) -> p s h", s=2)
                        link(dve.reciprocal(r, o[:, :, :, VD]))
                        oo = heads_out[:, t, :, :, 0:VD].rearrange("p s h e -> p (s h) e")
                        dve.tensor_tensor(y[:, t, :].rearrange("p (h e) -> p h e", h=HEADS), oo,
                                          rinv[:, t, :].unsqueeze(2).broadcast_to([P, HEADS, VD]),
                                          ALU.mult).then_inc(y_ready, 1)
                    if 0 <= t - 2 < TILES:
                        norm_sum(dve, st, n, part, t - 2)
                    if 0 <= t - 3:
                        norm_apply(dve, st, n, t - 3)

            @block.gpsimd
            def _(pool):
                norm_pool(pool, st, n)



def fold_tensors(mem, sem):
    class F:
        pass
    f = F()
    f.w = [mem.sb(f"fa_w{s}", [P, 4, DM]) for s in range(2)]
    f.kv = [mem.sb(f"fa_kv{s}", [P, 2, CTX]) for s in range(2)]
    f.folded = mem.sb("fa_folded", [P, DC, BATCH, HEADS, KEYS])
    f.vw = mem.sb("fa_vw", [P, BATCH, PAIRS, DM])
    f.kv_bank = mem.psum("fa_kv_bank", [P, BANK])
    f.fold_bank = mem.psum("fa_fold_bank", [P, BANK])
    f.vw_bank = [mem.psum(f"fa_vw_bank{j}", [P, BANK]) for j in range(2)]
    f.w_loaded = [sem(f"fa_w_loaded{s}") for s in range(2)]
    f.kv_projected = sem("fa_kv_projected")
    f.kv_ready = sem("fa_kv_ready")
    f.fold_done = sem("fa_fold_done")
    f.folded_ready = sem("fa_folded_ready")
    f.vw_done = sem("fa_vw_done")
    f.vw_ready = sem("fa_vw_ready")
    return f


def fold_load(sp, f, d, h):
    if h >= 2:
        sp.wait_ge(f.vw_done, h - 1)
    sp.dma_start(f.w[h % 2][:], d["fa_w"][h]).then_inc(f.w_loaded[h % 2], 16)


def fold_tensor(pe, st, f, h):
    s = h % 2
    pe.wait_ge(f.w_loaded[s], 16 * (h // 2 + 1))
    if h:
        pe.wait_ge(f.kv_ready, h)
    for r in range(2):
        for j in range(DC):
            last = pe.matmul(f.kv_bank[:, r * CTX:(r + 1) * CTX], f.w[s][:, r, j * HD:(j + 1) * HD],
                             st.ctxT[:, j, :], start=j == 0, stop=j == DC - 1)
    last.then_inc(f.kv_projected, 1)
    pe.wait_ge(f.kv_ready, h + 1)
    if h:
        pe.wait_ge(f.folded_ready, h)
    for j in range(DC):
        last = pe.matmul(f.fold_bank[:, j * CTX:(j + 1) * CTX], f.w[s][:, 2, j * P:(j + 1) * P],
                         f.kv[s][:, 0, :], start=True, stop=True)
    last.then_inc(f.fold_done, 1)
    if s == 0 and h:
        pe.wait_ge(f.vw_ready, h)
    for b in range(BATCH):
        last = pe.matmul(f.vw_bank[b // 2][s * KEYS:(s + 1) * KEYS, (b % 2) * DM:(b % 2 + 1) * DM],
                         f.kv[s][:, 1, b * KEYS:(b + 1) * KEYS], f.w[s][:, 3, :], start=True, stop=True)
    last.then_inc(f.vw_done, 1)


def fold_scalar(act, f, h):
    s = h % 2
    act.wait_ge(f.kv_projected, h + 1)
    act.activation(f.kv[s][:].rearrange("p r n -> p (r n)"), f.kv_bank[:, :], ACT.Copy).then_inc(f.kv_ready, 1)
    act.wait_ge(f.fold_done, h + 1)
    act.activation(f.folded[:, :, :, h, :], f.fold_bank[:, :].rearrange("p (c b k) -> p c b k", c=DC, b=BATCH),
                   ACT.Copy, scale=float(HD) ** -0.5).then_inc(f.folded_ready, 1)
    if s:
        act.wait_ge(f.vw_done, h + 1)
        for j in range(2):
            act.activation(f.vw[:, 2 * j:2 * j + 2, h // 2, :],
                           f.vw_bank[j][:, :].rearrange("p (b n) -> p b n", b=2), ACT.Copy).then_inc(f.vw_ready, 1)


def folded_attention(nc, st, sem, d, f):
    with Memory(nc) as mem:
        c = cross_tensors(mem, sem, "fa", f.vw)
        turn_bank = [mem.psum(f"fa_turn{i}", [P, BANK]) for i in range(2)]
        norm_bank = [mem.psum(f"fa_norm{i}", [P, BANK]) for i in range(2)]
        n = norm_tensors(mem, st, "fa")
        score = f.vw_bank
        out_bank = [f.kv_bank, f.fold_bank]
        part = lambda t: out_bank[t % 2][:, 0:DM]
        turns = [norm_bank[i][:, 0:DM].rearrange("p (c n) -> p c n", c=DC) for i in range(2)]
        scored = sem("fa_scored")

        with nc.Block() as block:
            @block.tensor
            def _(pe):
                def scores(t):
                    if t > 0:
                        pe.wait_ge(c.shifted, t)
                    for j in range(2):
                        for k in range(DC):
                            last = pe.matmul(score[j][:, :], st.xT[:, k, tile_cols(t)],
                                             f.folded[:, k, t // 2, 8 * j:8 * j + 8, :].rearrange("p h k -> p (h k)"),
                                             start=k == 0, stop=k == DC - 1)
                        last.then_inc(scored, 1)
                scores(0)
                for t in range(TILES + 2):
                    if t + 1 < TILES:
                        scores(t + 1)
                    if t < TILES:
                        cross_turn(pe, st, c, turn_bank, t)
                    if 0 <= t - 1 < TILES:
                        cross_out(pe, c, n, part, t - 1)
                    if t >= 3:
                        norm_tensor(pe, st, n, turns, t - 3)
                norm_tensor(pe, st, n, turns, TILES - 1)

            @block.scalar
            def _(act):
                for t in range(TILES + 4):
                    if t < TILES:
                        cross_exp(act, c, t)
                    if 0 <= t - 1 < TILES:
                        cross_keep(act, c, turn_bank, t - 1)
                    if 0 <= t - 4:
                        norm_keep(act, st, n, turns, t - 4)

            @block.vector
            def _(dve):
                for t in range(TILES + 3):
                    if t < TILES:
                        for j in range(2):
                            dve.wait_ge(scored, 2 * t + j + 1)
                            dve.tensor_reduce(c.max[:, t, 8 * j:8 * j + 8],
                                              score[j][:, :].rearrange("p (h k) -> p h k", h=8),
                                              X_AXIS, ALU.max).then_inc(c.max_ready, 1)
                        dve.wait_ge(c.max_ready, 2 * t + 2)
                        for j in range(2):
                            last = dve.tensor_tensor(c.rows[:, t, 8 * j:8 * j + 8, :],
                                                     score[j][:, :].rearrange("p (h k) -> p h k", h=8),
                                                     over_keys(c.max[:, t, 8 * j:8 * j + 8]), ALU.subtract)
                        last.then_inc(c.shifted, 1)
                        cross_normalise_sum(dve, c, t)
                    if 0 <= t - 2 < TILES:
                        norm_sum(dve, st, n, part, t - 2)
                    if 0 <= t - 3:
                        norm_apply(dve, st, n, t - 3)

            @block.gpsimd
            def _(pool):
                for t in range(TILES + 2):
                    if t < TILES:
                        cross_weights(pool, c, t)
                    if t >= 2:
                        norm_rstd(pool, st, n, t - 2)



def differential_attention(nc, st, sem, d, f):
    HALVES_Q = 2 * HEADS
    D = DM // HALVES_Q
    VD = DM // HEADS
    CHUNKS = 4
    CQ = HALVES_Q // CHUNKS
    with Memory(nc) as mem:
        wqk = mem.sb("da_wqk", [P, DC, 2 * DM])
        wv = mem.sb("da_wv", [P, DC, DM])
        wo = mem.sb("da_wo", [P, DC, DM])
        bo = mem.sb("da_bo", [P, DM])
        lam_in = mem.sb("da_lam_in", [P, 2, 2, D])
        lam_prod = mem.sb("da_lam_prod", [P, 2, D])
        lam_sum = mem.sb("da_lam_sum", [P, 2])
        lam_exp = mem.sb("da_lam_exp", [P, 2])
        neg_lam = mem.sb("da_neg_lam", [P, 1])
        q = mem.sb("da_q", [P, TILES, HALVES_Q, D])
        k = mem.sb("da_k", [P, TILES, HALVES_Q, D])
        v = mem.sb("da_v", [P, TILES, HEADS, VD])
        prod_outer = mem.sb("da_prod_outer", [P, 2, D, CQ, HALVES_Q])
        prod_inner = mem.sb("da_prod_inner", [P, 2, CQ, HALVES_Q, D])
        vprod = mem.sb("da_vprod", [P, 2, HEADS // 2, VD, HEADS])
        att = mem.sb("da_att", [P, 2, HALVES_Q, HALVES_Q])
        above = mem.sb("da_above", [P, HALVES_Q, HALVES_Q])
        below = mem.sb("da_below", [P, HALVES_Q, HALVES_Q])
        rowmax = mem.sb("da_rowmax", [P, HALVES_Q])
        rowsum = mem.sb("da_rowsum", [P, HALVES_Q])
        rinv = mem.sb("da_rinv", [P, HALVES_Q])
        first = mem.sb("da_first", [P, HEADS, HEADS])
        second = mem.sb("da_second", [P, HEADS, HEADS])
        diff = mem.sb("da_diff", [P, 2, HEADS, HEADS])
        mixed = mem.sb("da_mixed", [P, HEADS, VD])
        squares = mem.sb("da_squares", [P, HEADS, VD])
        ssq = mem.sb("da_ssq", [P, HEADS])
        meansq = mem.sb("da_meansq", [P, HEADS])
        rrms = mem.sb("da_rrms", [P, HEADS])
        y = mem.sb("da_y", [P, 2, DM])
        yT = mem.sb("da_yT", [P, 2, DC, P])
        qk_bank = [mem.psum(f"da_qk_bank{i}", [P, BANK]) for i in range(2)]
        v_bank = [mem.psum(f"da_v_bank{i}", [P, BANK]) for i in range(2)]
        n = norm_tensors(mem, st, "da")
        score_bank = qk_bank[0]
        part = lambda t: qk_bank[1][:, 0:DM]
        yturn = v_bank[0][:, 0:DM].rearrange("p (c n) -> p c n", c=DC)
        turns = [v_bank[1][:, 0:DM].rearrange("p (c n) -> p c n", c=DC)] * 2

        loaded = sem("da_loaded")
        qk_projected = sem("da_qk_projected")
        v_projected = sem("da_v_projected")
        qk_ready = sem("da_qk_ready")
        v_ready = sem("da_v_ready")
        lam_summed = sem("da_lam_summed")
        lam_ready = sem("da_lam_ready")
        pool_prod = sem("da_pool_prod")
        pe_reduced = sem("da_pe_reduced")
        guarded = sem("da_guarded")
        shifted = sem("da_shifted")
        exp_ready = sem("da_exp_ready")
        diff_ready = sem("da_diff_ready")
        pool_vprod = sem("da_pool_vprod")
        vreduced = sem("da_vreduced")
        ssq_ready = sem("da_ssq_ready")
        rms_ready = sem("da_rms_ready")
        y_ready = sem("da_y_ready")
        y_turned = sem("da_y_turned")
        yT_ready = sem("da_yT_ready")
        chain = sem("da_chain")

        def score_product(eng, out, t, j):
            return eng.tensor_tensor(
                out, q[:, t, j * CQ:(j + 1) * CQ, :].unsqueeze(2).broadcast_to([P, CQ, HALVES_Q, D]),
                k[:, t, :, :].unsqueeze(1).broadcast_to([P, CQ, HALVES_Q, D]), ALU.mult)

        with nc.Block() as block:
            @block.sync
            def _(sp):
                for dst, src in ((wqk, "da_wqk"), (wv, "da_wv"), (wo, "da_wo")):
                    sp.dma_start(dst[:], d[src]).then_inc(loaded, 16)
                sp.dma_start(lam_in[:], d["da_lam"].partition_broadcast(P)).then_inc(loaded, 16)
                sp.dma_start(bo[:], d["da_bo"].partition_broadcast(P)).then_inc(loaded, 16)
                for h in range(HEADS):
                    fold_load(sp, f, d, h)

            @block.tensor
            def _(pe):
                pe.wait_ge(loaded, 16 * 5)
                for t in range(TILES):
                    if t >= 2:
                        pe.wait_ge(qk_ready, 2 * (t - 1))
                    for c in range(DC):
                        last = pe.matmul(qk_bank[t % 2][:, :], st.xT[:, c, tile_cols(t)], wqk[:, c, :],
                                         start=c == 0, stop=c == DC - 1)
                    last.then_inc(qk_projected, 1)
                    if t >= 2:
                        pe.wait_ge(v_ready, t - 1)
                    for c in range(DC):
                        last = pe.matmul(v_bank[t % 2][:, 0:DM], st.xT[:, c, tile_cols(t)], wv[:, c, :],
                                         start=c == 0, stop=c == DC - 1)
                    last.then_inc(v_projected, 1)
                pe.wait_ge(qk_ready, 2 * TILES)
                pe.wait_ge(v_ready, TILES)
                for t in range(TILES + 2):
                    if t < TILES:
                        if t:
                            pe.wait_ge(guarded, t)
                        for j in range(2):
                            pe.wait_ge(pool_prod, 2 * t + j + 1)
                            for e in range(D):
                                last = pe.matmul(score_bank[:, j * CQ * HALVES_Q:(j + 1) * CQ * HALVES_Q],
                                                 st.ident[:], prod_outer[:, j, e, :, :].rearrange("p a b -> p (a b)"),
                                                 start=e == 0, stop=e == D - 1)
                            last.then_inc(pe_reduced, 1)
                        fold_tensor(pe, st, f, 2 * t)
                        fold_tensor(pe, st, f, 2 * t + 1)
                    if t >= 2:
                        norm_tensor(pe, st, n, turns, t - 2, depth=1)
                    if 0 <= t - 1 < TILES:
                        r = t - 1
                        pe.wait_ge(y_ready, r + 1)
                        if r:
                            pe.wait_ge(yT_ready, r)
                        for c in range(DC):
                            last = pe.transpose(yturn[:, c, :], y[:, r % 2, tile_cols(c)], st.ident[:])
                        last.then_inc(y_turned, 1)
                        pe.wait_ge(yT_ready, r + 1)
                        if r:
                            pe.wait_ge(n.summed, n.base + r)
                        for c in range(DC):
                            last = pe.matmul(part(r), yT[:, r % 2, c, :], wo[:, c, :], start=c == 0, stop=c == DC - 1)
                        last.then_inc(n.out_ready, 1)

            @block.scalar
            def _(act):
                act.wait_ge(lam_summed, 1)
                act.activation(lam_exp[:], lam_sum[:], ACT.Exp).then_inc(lam_ready, 1)
                for t in range(TILES):
                    act.wait_ge(qk_projected, t + 1)
                    act.activation(q[:, t, :, :].rearrange("p a e -> p (a e)"), qk_bank[t % 2][:, 0:DM], ACT.Copy,
                                   scale=float(D) ** -0.5).then_inc(qk_ready, 1)
                    act.activation(k[:, t, :, :].rearrange("p a e -> p (a e)"), qk_bank[t % 2][:, DM:2 * DM],
                                   ACT.Copy).then_inc(qk_ready, 1)
                    act.wait_ge(v_projected, t + 1)
                    act.activation(v[:, t, :, :].rearrange("p h e -> p (h e)"), v_bank[t % 2][:, 0:DM],
                                   ACT.Copy).then_inc(v_ready, 1)
                for t in range(TILES + 2):
                    if t < TILES:
                        fold_scalar(act, f, 2 * t)
                        fold_scalar(act, f, 2 * t + 1)
                        act.wait_ge(shifted, t + 1)
                        act.activation(att[:, t % 2, :, :], att[:, t % 2, :, :], ACT.Exp).then_inc(exp_ready, 1)
                    if t >= 2:
                        norm_keep(act, st, n, turns, t - 2)
                    if 0 <= t - 1 < TILES:
                        act.wait_ge(y_turned, t)
                        act.activation(yT[:, (t - 1) % 2, :, :], yturn, ACT.Copy).then_inc(yT_ready, 1)

            @block.gpsimd
            def _(pool):
                def score_products(t):
                    pool.wait_ge(qk_ready, 2 * t + 2)
                    for j in range(2):
                        if t > 0:
                            pool.wait_ge(pe_reduced, 2 * (t - 1) + j + 1)
                        score_product(pool, prod_outer[:, j, :, :, :].rearrange("p e a b -> p a b e"),
                                      t, j).then_inc(pool_prod, 1)

                score_products(0)
                for t in range(TILES + 2):
                    if t + 1 < TILES:
                        score_products(t + 1)
                    if t >= 2:
                        norm_rstd(pool, st, n, t - 2)
                    if 1 <= t <= TILES:
                        pool.wait_ge(ssq_ready, t)
                        pool.tensor_tensor(rrms[:], meansq[:], st.minus_half[:, :].broadcast_to([P, HEADS]),
                                           ALU.pow).then_inc(rms_ready, 1)
                    if t >= TILES:
                        continue
                    pool.wait_ge(diff_ready, t + 1)
                    pool.wait_ge(v_ready, t + 1)
                    for j in range(2):
                        if t > 0:
                            pool.wait_ge(vreduced, 2 * (t - 1) + j + 1)
                        HH = HEADS // 2
                        pool.tensor_tensor(
                            vprod[:, j, :, :, :],
                            diff[:, t % 2, j * HH:(j + 1) * HH, :].unsqueeze(2).broadcast_to([P, HH, VD, HEADS]),
                            v[:, t, :, :].rearrange("p h e -> p e h").unsqueeze(1).broadcast_to([P, HH, VD, HEADS]),
                            ALU.mult).then_inc(pool_vprod, 1)

            @block.vector
            def _(dve):
                links = [0]

                def link(ins):
                    links[0] += 1
                    ins.then_inc(chain, 1)
                    dve.wait_ge(chain, links[0])

                def over(a, count):
                    return a.unsqueeze(2).broadcast_to([P, a.shape[1], count])

                dve.wait_ge(loaded, 16 * 5)
                link(dve.tensor_tensor(lam_prod[:], lam_in[:, 0, :, :], lam_in[:, 1, :, :], ALU.mult))
                dve.tensor_reduce(lam_sum[:], lam_prod[:], X_AXIS, ALU.add).then_inc(lam_summed, 1)
                dve.wait_ge(lam_ready, 1)
                link(dve.scalar_tensor_tensor(neg_lam[:], lam_exp[:, 1:2], LAM_INIT, lam_exp[:, 0:1],
                                              ALU.subtract, ALU.subtract))
                for t in range(TILES):
                    link(dve.tensor_tensor(st.x[:, t, :], st.x[:, t, :], bo[:, :], ALU.add))

                def head_maps(t):
                    a = att[:, t % 2, :, :]
                    dve.wait_ge(qk_ready, 2 * t + 2)
                    score_product(dve, prod_inner[:, 0, :, :, :], t, 2)
                    link(score_product(dve, prod_inner[:, 1, :, :, :], t, 3))
                    link(dve.tensor_reduce(a[:, HEADS:, :], prod_inner[:].rearrange("p j a b e -> p (j a) b e"),
                                           X_AXIS, ALU.add))
                    dve.tensor_scalar(above[:, HEADS:, :], a[:, HEADS:, :], 0.0, LARGEST, ALU.max, ALU.min)
                    dve.tensor_scalar(below[:, HEADS:, :], a[:, HEADS:, :], 0.0, -LARGEST, ALU.min, ALU.max)
                    dve.wait_ge(pe_reduced, 2 * t + 2)
                    half = score_bank[:, :].rearrange("p (a b) -> p a b", a=HEADS)
                    dve.tensor_scalar(above[:, 0:HEADS, :], half, 0.0, LARGEST, ALU.max, ALU.min)
                    dve.tensor_scalar(below[:, 0:HEADS, :], half, 0.0, -LARGEST, ALU.min,
                                      ALU.max).then_inc(guarded, 1)
                    dve.wait_ge(guarded, t + 1)
                    link(dve.tensor_tensor(a, above[:], below[:], ALU.add))
                    link(dve.tensor_reduce(rowmax[:], a, X_AXIS, ALU.max))
                    dve.tensor_tensor(a, a, over(rowmax[:], HALVES_Q), ALU.subtract).then_inc(shifted, 1)

                def map_difference(t):
                    a = att[:, t % 2, :, :]
                    dve.wait_ge(exp_ready, t + 1)
                    link(dve.tensor_reduce(rowsum[:], a, X_AXIS, ALU.add))
                    link(dve.reciprocal(rinv[:], rowsum[:]))
                    dve.tensor_tensor(first[:], a[:, 0:HEADS, 0:HEADS], over(rinv[:, 0:HEADS], HEADS), ALU.mult)
                    link(dve.tensor_tensor(second[:], a[:, HEADS:, HEADS:], over(rinv[:, HEADS:], HEADS), ALU.mult))
                    dve.scalar_tensor_tensor(diff[:, t % 2, :, :].rearrange("p a h -> p (a h)"),
                                             second[:].rearrange("p a h -> p (a h)"), neg_lam[:, :],
                                             first[:].rearrange("p a h -> p (a h)"),
                                             ALU.mult, ALU.add).then_inc(diff_ready, 1)

                def mix(t):
                    for j in range(2):
                        dve.wait_ge(pool_vprod, 2 * t + j + 1)
                        dve.tensor_reduce(mixed[:, j * HEADS // 2:(j + 1) * HEADS // 2, :], vprod[:, j, :, :, :],
                                          X_AXIS, ALU.add).then_inc(vreduced, 1)
                    dve.wait_ge(vreduced, 2 * t + 2)
                    link(dve.tensor_tensor(squares[:], mixed[:], mixed[:], ALU.mult))
                    link(dve.tensor_reduce(ssq[:], squares[:], X_AXIS, ALU.add))
                    dve.tensor_scalar(meansq[:], ssq[:], 1.0 / VD, LN_EPS, ALU.mult, ALU.add).then_inc(ssq_ready, 1)

                def mix_norm(t):
                    dve.wait_ge(rms_ready, t + 1)
                    dve.scalar_tensor_tensor(y[:, t % 2, :].rearrange("p (h e) -> p h e", h=HEADS), mixed[:],
                                             1.0 - LAM_INIT, over(rrms[:], VD),
                                             ALU.mult, ALU.mult).then_inc(y_ready, 1)

                for t in range(TILES + 2):
                    if t < TILES:
                        head_maps(t)
                    if t >= 2:
                        norm_sum(dve, st, n, part, t - 2)
                    if 0 <= t - 1 < TILES:
                        mix(t - 1)
                    if t < TILES:
                        map_difference(t)
                    if t >= 2:
                        norm_apply(dve, st, n, t - 2)
                    if 0 <= t - 1 < TILES:
                        mix_norm(t - 1)


def differential_and_folded_attention(nc, st, sem, d):
    with Memory(nc) as mem:
        f = fold_tensors(mem, sem)
        differential_attention(nc, st, sem, d, f)
        folded_attention(nc, st, sem, d, f)



def experts(nc, st, sem, d):
    PARTS = 3
    with Memory(nc) as mem:
        w = [mem.sb(f"ex_w{s}", [P, 2, DC, P]) for s in range(2)]
        xs = split_x_tensors(mem, sem, "ex")
        ws = [mem.sb(f"ex_ws{s}", [P, 2, 2, DC, P], F32R) for s in range(2)]
        wd = mem.sb("ex_wd", [P, FTILES, DM])
        router = mem.sb("ex_router", [P, DC, EXPERTS])
        spreadf = mem.sb("ex_spreadf", [PARTS * EXPERTS, FTILES, P])
        spread = mem.sb("ex_spread", [PARTS * EXPERTS, FTILES, P], BF16)
        logits = mem.sb("ex_logits", [P, TILES, EXPERTS])
        top = mem.sb("ex_top", [P, TILES, TOP_K])
        marked = mem.sb("ex_marked", [P, TILES, EXPERTS])
        chosen = mem.sb("ex_chosen", [P, TILES, EXPERTS])
        weights = mem.sb("ex_weights", [P, TILES, EXPERTS])
        wsum = mem.sb("ex_wsum", [P, TILES])
        winv = mem.sb("ex_winv", [P, TILES])
        parts = mem.sb("ex_parts", [P, TILES, PARTS, EXPERTS], BF16)
        partsT = mem.sb("ex_partsT", [PARTS * EXPERTS, TOK], BF16)
        silu = [mem.sb(f"ex_silu{f}", [P, BANK]) for f in range(2)]
        gated = [mem.sb(f"ex_gated{f}", [P, BANK]) for f in range(2)]
        hidden = mem.sb("ex_hidden", [P, FTILES, TOK])
        gate_bank = [mem.psum(f"ex_gate{f}", [P, BANK]) for f in range(2)]
        up_bank = [mem.psum(f"ex_up{f}", [P, BANK]) for f in range(2)]
        route_bank = [mem.psum(f"ex_route{f}", [P, BANK]) for f in range(2)]
        logit_bank = mem.psum("ex_logit", [P, BANK])
        parts_bank = mem.psum("ex_parts_bank", [P, 2 * BANK], BF16)
        n = norm_tensors(mem, st, "ex")
        out_banks = gate_bank + up_bank

        w_loaded = [sem(f"ex_w_loaded{s}") for s in range(2)]
        w_split = sem("ex_w_split")
        router_loaded = sem("ex_router_loaded")
        spread_loaded = sem("ex_spread_loaded")
        spread_ready = sem("ex_spread_ready")
        wd_loaded = sem("ex_wd_loaded")
        routed = sem("ex_routed")
        logits_ready = sem("ex_logits_ready")
        top_ready = sem("ex_top_ready")
        chain = sem("ex_chain")
        less_max = sem("ex_less_max")
        exp_ready = sem("ex_exp_ready")
        parts_ready = sem("ex_parts_ready")
        parts_turned = sem("ex_parts_turned")
        partsT_ready = sem("ex_partsT_ready")
        gate_done = sem("ex_gate_done")
        rest_done = sem("ex_rest_done")
        silu_ready = sem("ex_silu_ready")
        gated_ready = sem("ex_gated_ready")
        hidden_ready = sem("ex_hidden_ready")
        stored = sem("ex_stored")

        with nc.Block() as block:
            @block.sync
            def _(sp):
                sp.dma_start(router[:], d["ex_router"]).then_inc(router_loaded, 16)
                sp.dma_start(w[0][:], d["ex_w"][0]).then_inc(w_loaded[0], 16)
                sp.dma_start(w[1][:], d["ex_w"][1]).then_inc(w_loaded[1], 16)
                sp.dma_start(spreadf[:], d["ex_spread"]).then_inc(spread_loaded, 16)
                sp.dma_start(wd[:], d["ex_wd"]).then_inc(wd_loaded, 16)
                with sp.Fori(0, FTILES // 2 - 1) as i:
                    for s in range(2):
                        sp.wait_ge(w_split, 4 * i + 2 * s + 2)
                        sp.dma_start(w[s][:], d["ex_w"][2 * i + s + 2]).then_inc(w_loaded[s], 16)
                for t in range(TILES):
                    sp.wait_ge(n.x_ready, n.base + t + 1)
                    sp.dma_start(st.out[:, t, :], st.x[:, t, :]).then_inc(stored, 16)
                sp.wait_ge(stored, 16 * TILES)

            @block.tensor
            def _(pe):
                pe.wait_ge(router_loaded, 16)
                for t in range(TILES):
                    for c in range(DC):
                        last = pe.matmul(logit_bank[:, t * EXPERTS:(t + 1) * EXPERTS], st.xT[:, c, tile_cols(t)],
                                         router[:, c, :], start=c == 0, stop=c == DC - 1)
                last.then_inc(routed, 1)

                def gate_up(f, s):
                    for r, bank in ((0, gate_bank[f]), (1, up_bank[f])):
                        for c, (k, m), first, end in products():
                            last = pe.matmul(bank[:, :], ws[s][:, k, r, c, :],
                                             xs.parts[:, m, c, f * BANK:(f + 1) * BANK], start=first, stop=end)
                        if r == 0:
                            last.then_inc(gate_done, 1)

                def route(j, f):
                    pe.matmul(route_bank[f][:, :], spread[:, bass.ds(j, 1), :].squeeze(1),
                              partsT[:, f * BANK:(f + 1) * BANK], start=True, stop=True).then_inc(rest_done, 1)

                pe.wait_ge(xs.lo_ready, HALVES)
                pe.wait_ge(w_split, 2)
                gate_up(0, 0)
                gate_up(1, 0)
                for t in range(TILES):
                    if t == 0:
                        pe.wait_ge(parts_ready, 1)
                    last = pe.transpose(parts_bank[0:PARTS * EXPERTS, tile_cols(t)],
                                        parts[:, t, :, :].rearrange("p r e -> p (r e)"), st.identb[:])
                last.then_inc(parts_turned, 1)
                pe.wait_ge(spread_ready, 1)
                pe.wait_ge(partsT_ready, 1)
                route(0, 0)
                route(0, 1)

                def tile(i, s):
                    j = 2 * i + s
                    pe.wait_ge(w_split, 2 * j + 2)
                    for f in range(2):
                        pe.wait_ge(hidden_ready, 2 * j + f - 1)
                        gate_up(f, s)
                        route(j, f)
                tile(0, 1)
                with pe.Fori(1, FTILES // 2) as i:
                    tile(i, 0)
                    tile(i, 1)
                pe.wait_ge(wd_loaded, 16)
                pe.wait_ge(hidden_ready, 2 * FTILES)
                for t in range(TILES):
                    if t >= 4:
                        pe.wait_ge(n.summed, n.base + t - 3)
                    for j in range(FTILES):
                        last = pe.matmul(out_banks[t % 4][:, 0:DM], hidden[:, j, tile_cols(t)], wd[:, j, :],
                                         start=j == 0, stop=j == FTILES - 1)
                    last.then_inc(n.out_ready, 1)

            @block.scalar
            def _(act):
                split_x_scalar(act, st, xs)
                act.wait_ge(less_max, 1)
                act.activation(weights[:], weights[:], ACT.Exp).then_inc(exp_ready, 1)
                act.wait_ge(parts_turned, 1)
                act.activation(partsT[:, :], parts_bank[0:PARTS * EXPERTS, :], ACT.Copy).then_inc(partsT_ready, 1)

                def unit(j, f):
                    act.wait_ge(gate_done, 2 * j + f + 1)
                    act.activation(silu[f][:, :], gate_bank[f][:, :], ACT.Silu).then_inc(silu_ready, 1)
                with act.Fori(0, FTILES) as j:
                    unit(j, 0)
                    unit(j, 1)

            @block.gpsimd
            def _(pool):
                def split_w(j, s, loads):
                    pool.wait_ge(w_loaded[s], 16 * loads)
                    if not isinstance(j, int):
                        pool.wait_ge(rest_done, 2 * j - 2)
                    flat = [a.rearrange("p r c n -> p (r c) n") for a in (w[s][:], ws[s][:, 0], ws[s][:, 1])]
                    split_on(pool, ones_like(st, 2 * DC, P), *flat, w_split, 2 * j)
                split_w(0, 0, 1)
                pool.wait_ge(spread_loaded, 16)
                pool.tensor_copy(spread[:], spreadf[:]).then_inc(spread_ready, 1)
                split_w(1, 1, 1)
                with pool.Fori(1, FTILES // 2) as i:
                    split_w(2 * i, 0, i + 1)
                    split_w(2 * i + 1, 1, i + 1)
                norm_pool(pool, st, n)

            @block.vector
            def _(dve):
                links = [0]

                def link(ins):
                    links[0] += 1
                    ins.then_inc(chain, 1)
                    dve.wait_ge(chain, links[0])

                def over(a, count):
                    return a.unsqueeze(2).broadcast_to([P, a.shape[1], count])

                split_x_vector(dve, st, xs)
                dve.wait_ge(routed, 1)
                link(dve.tensor_copy(logits[:].rearrange("p t e -> p (t e)"), logit_bank[:, 0:TILES * EXPERTS]))
                for t in range(TILES):
                    last = dve.max(top[:, t, :], logits[:, t, :])
                link(last)
                for t in range(TILES):
                    last = dve.match_replace(marked[:, t, :], top[:, t, :], logits[:, t, :], -LARGEST)
                dve.tensor_tensor(weights[:], logits[:], over(top[:, :, 0], EXPERTS),
                                  ALU.subtract).then_inc(less_max, 1)
                link(last)
                link(dve.tensor_tensor(chosen[:], logits[:], marked[:], ALU.not_equal))
                dve.wait_ge(exp_ready, 1)
                link(dve.tensor_tensor(weights[:], weights[:], chosen[:], ALU.mult))
                link(dve.tensor_reduce(wsum[:], weights[:], X_AXIS, ALU.add))
                link(dve.reciprocal(winv[:], wsum[:]))
                link(dve.tensor_tensor(weights[:], weights[:], over(winv[:], EXPERTS), ALU.mult))
                for r in range(PARTS - 1):
                    link(dve.tensor_copy(parts[:, :, r, :], weights[:]))
                    link(dve.tensor_tensor(weights[:], weights[:], parts[:, :, r, :], ALU.subtract))
                dve.tensor_copy(parts[:, :, PARTS - 1, :], weights[:]).then_inc(parts_ready, 1)

                def unit(j, f):
                    dve.wait_ge(silu_ready, 2 * j + f + 1)
                    dve.wait_ge(rest_done, 2 * j + f + 1)
                    dve.tensor_tensor(gated[f][:, :], silu[f][:, :], up_bank[f][:, :], ALU.mult).then_inc(gated_ready, 1)
                    dve.wait_ge(gated_ready, 2 * j + f + 1)
                    dve.tensor_tensor(hidden[:, bass.ds(j, 1), f * BANK:(f + 1) * BANK].squeeze(1), gated[f][:, :],
                                      route_bank[f][:, :], ALU.mult).then_inc(hidden_ready, 1)
                with dve.Fori(0, FTILES) as j:
                    unit(j, 0)
                    unit(j, 1)
                norm_vector(dve, st, n, lambda t: out_banks[t % 4][:, 0:DM])


STAGES = [self_attention, context_attention, recurrent_attention, differential_and_folded_attention, experts]


def build(nc, d, out):
    with ExitStack() as stack, Memory(nc) as mem:
        def sem(name):
            return stack.enter_context(nc.semaphore(name))
        st = State()
        st.x = mem.sb("x", [P, TILES, DM])
        st.xT = mem.sb("xT", [P, DC, TOK])
        st.ident = mem.sb("ident", [P, P])
        st.identb = mem.sb("identb", [P, P], BF16)
        st.mask = mem.sb("mask", [P, P], BF16)
        st.minus_half = mem.sb("minus_half", [P, 1])
        st.ones = mem.sb("ones", [P, 1])
        st.ctxT = mem.sb("ctxT", [P, DC, CTX])
        st.xT_loaded = sem("xT_loaded")
        st.consts_ready = sem("consts_ready")
        st.out = out
        st.norm = norm_signals(sem)
        for stage in STAGES:
            stage(nc, st, sem, d)



def layouts(inp):
    g = {k: np.asarray(v) for k, v in inp.items()}
    o = {}
    rows = lambda a, t: a.reshape(t, P, -1).transpose(1, 0, 2)
    x = g["x"].reshape(TOK, DM)
    o["x"] = rows(x, TILES)
    o["xT"] = rows(x.T, DC)
    o["ident"] = np.eye(P, dtype=np.float32)
    o["mask"] = np.triu(np.full((P, P), MASKED, np.float32), 1)
    qkv = np.stack([g["L0_attn_W_Q"], g["L0_attn_W_K"], g["L0_attn_W_V"]], 1)
    o["sa_w"] = qkv.reshape(HEADS, 3, DC, P, HD).transpose(0, 3, 1, 2, 4)
    o["sa_wo"] = g["L0_attn_W_O"].transpose(1, 0, 2)
    o["sa_bias"] = np.stack([g["L0_attn_b_Q"].T, g["L0_attn_b_K"].T, g["L0_attn_b_V"].T], 1)
    o["sa_bo"] = g["L0_attn_b_O"]
    o["ctxT"] = rows(g["ctx_2048"].reshape(CTX, DM).T, DC)
    o["ca_wq"] = g["L0_xattn_Wq"].reshape(DC, P, HEADS, HD).transpose(2, 1, 0, 3)
    o["ca_wk"] = rows(g["L0_xattn_Wk"], DC)
    o["ca_wv"] = rows(g["L0_xattn_Wv"], DC)
    o["ca_wo"] = g["L0_xattn_Wo"].reshape(HEADS, HD, DM).transpose(1, 0, 2)
    o["ca_bq"] = g["L0_xattn_bq"].reshape(HEADS, HD).T
    o["ca_bk"] = g["L0_xattn_bk"]
    o["ca_bv"] = g["L0_xattn_bv"].reshape(4, HD).T
    o["ca_norms"] = np.stack([g["L0_xattn_qn_w"], g["L0_xattn_kn_w"]], 1)
    o["ca_amask"] = g["mask_1xSxS2_ff0"][0].reshape(2, P, KEYS).transpose(1, 0, 2)
    wa = g["L0_ffn_Wa"]
    q_std, k_std, v, q_low, k_low = np.split(wa, [128, 256, 512, 640], axis=1)
    join = lambda a, b: np.concatenate([a.reshape(DM, HEADS, 8), b.reshape(DM, HEADS, 8)], 2).reshape(DM, DM)
    o["ra_wq"] = rows(join(q_std, q_low), DC)
    o["ra_wk"] = rows(join(k_std, k_low), DC)
    o["ra_wv"] = rows(v, DC)
    o["ra_wo"] = rows(g["L0_ffn_Wp"], DC)
    own = np.repeat(np.eye(8, dtype=np.float32), 16, 0)
    o["ra_rowmask"] = own
    is_low = np.tile(np.repeat(np.array([False, True]), 8), HEADS)
    std_row, rec_row = np.repeat(g["L0_ffn_w_std"], 16), np.repeat(g["L0_ffn_w_rec"], 16)
    w_row = np.where(is_low, rec_row, std_row)
    o["ra_roww"] = np.stack([w_row, rec_row, is_low.astype(np.float32)], 0).reshape(3, 2, P).transpose(2, 0, 1)
    half = lambda a: a.T.reshape(DM, HEADS, 8, 2).transpose(0, 3, 1, 2).reshape(DM, DM)
    o["da_wqk"] = rows(np.concatenate([half(g["L1_attn_Wq"]), half(g["L1_attn_Wk"])], 1), DC)
    o["da_wv"] = rows(g["L1_attn_Wv"].T, DC)
    o["da_wo"] = rows(g["L1_attn_Wo"].T, DC)
    o["da_lam"] = np.stack([np.stack([g["L1_attn_lq1"], g["L1_attn_lq2"]]),
                            np.stack([g["L1_attn_lk1"], g["L1_attn_lk2"]])])
    o["da_bo"] = g["L1_attn_bo"]
    by_head = lambda a: a.reshape(DC, P, HEADS, HD).transpose(2, 1, 0, 3).reshape(HEADS, P, 1, DM)
    o["fa_w"] = np.concatenate([by_head(g["L1_xattn_Wk"]), by_head(g["L1_xattn_Wv"]),
                                g["L1_xattn_Wq"].reshape(DM, HEADS, HD).transpose(1, 2, 0)[:, :, None, :],
                                g["L1_xattn_Wo"].reshape(HEADS, HD, 1, DM)], 2)
    stacked = lambda a: a.reshape(FTILES, P, DC, P).transpose(0, 3, 2, 1)
    o["ex_w"] = np.stack([stacked(g["L1_ffn_w_gate_proj"]), stacked(g["L1_ffn_w_up_proj"])], 2)
    o["ex_wd"] = rows(g["L1_ffn_w_down_proj"].transpose(0, 2, 1).reshape(-1, DM), FTILES)
    o["ex_router"] = rows(g["L1_ffn_gate_w"].T, DC)
    own = np.repeat(np.eye(EXPERTS), INNER, 1).reshape(EXPERTS, FTILES, P)
    o["ex_spread"] = np.concatenate([own] * 3, 0).astype(np.float32)
    return {k: np.ascontiguousarray(v) for k, v in o.items()}


def kernel(**inputs):
    import concourse.bacc as bacc
    from concourse.bass_utils import run_bass_kernel_spmd

    arrays = layouts(inputs)
    nc = bacc.Bacc("TRN2", target_bir_lowering=False, num_devices=1)
    d = {k: nc.dram_tensor(f"in_{k}", a.shape, mybir.dt.from_np(a.dtype), kind="ExternalInput").ap()
         for k, a in arrays.items()}
    out = nc.dram_tensor("out", (P, TILES, DM), F32, kind="ExternalOutput").ap()
    build(nc, d, out)
    r = run_bass_kernel_spmd(nc, [{f"in_{k}": a for k, a in arrays.items()}], core_ids=[0])
    y = r.results[0]["out"]
    return y.transpose(1, 0, 2).reshape(BATCH, SEQ, DM)
```

```python
from contextlib import ExitStack

import numpy as np

import concourse.bass as bass
from concourse import mybir

F32 = mybir.dt.float32
F32R = mybir.dt.float32r
BF16 = mybir.dt.bfloat16
ALU = mybir.AluOpType
ACT = mybir.ActivationFunctionType
X_AXIS = mybir.AxisListType.X

P = 128
BATCH = 4
SEQ = 256
KEYS = 64
DM = 256
DC = DM // P
TOK = BATCH * SEQ
TILES = TOK // P
CTX = BATCH * KEYS
HEADS = 16
HD = 128
BANK = 512
HALVES = TOK // BANK
EXPERTS = 32
INNER = 96
FTILES = EXPERTS * INNER // P
TOP_K = 8
LN_EPS = 1e-5
MASKED = -1e30
LARGEST = float(np.finfo(np.float32).max)
LAM_INIT = 0.8 - 0.6 * float(np.exp(-0.3 * 12))


class Memory:

    def __init__(self, nc):
        self.nc = nc
        self.stack = ExitStack()

    def __enter__(self):
        return self

    def __exit__(self, *_):
        self.stack.close()

    def sb(self, name, shape, dt=F32):
        return self.stack.enter_context(self.nc.sbuf_tensor(name, shape, dt))

    def psum(self, name, shape, dt=F32):
        return self.stack.enter_context(self.nc.psum_tensor(name, shape, dt))


class State:
    pass


def wait_past(eng, signal, value):
    if not (isinstance(value, int) and value <= 0):
        eng.wait_ge(signal, value)


def tile_cols(t):
    return slice(t * P, (t + 1) * P)



class Early:

    def __init__(self, area, sem, stage, **shapes):
        at = 0
        self.names = {}
        for name, shape in shapes.items():
            size = int(np.prod(shape))
            part = area[:, at:at + size]
            axes = "abc"[:len(shape)]
            if len(shape) > 1:
                part = part.rearrange(f"p ({' '.join(axes)}) -> p {' '.join(axes)}",
                                      **{a: n for a, n in zip(axes, shape)})
            self.names[name] = part
            at += size
        self.loaded = sem(f"{stage}_first_loaded")
        self.loads = 16 * len(shapes)

    def __getitem__(self, name):
        return self.names[name]



PASSES = ((0, 0), (0, 1), (1, 0))


def split_on(eng, ones, whole, hi, lo, done, count):
    eng.tensor_tensor(hi, whole, ones, ALU.mult).then_inc(done, 1)
    eng.wait_ge(done, count + 1)
    eng.tensor_tensor(lo, whole, hi, ALU.subtract).then_inc(done, 1)


def ones_like(st, a, b):
    return st.ones[:, :].unsqueeze(2).broadcast_to([P, a, b])


def products():
    steps = [(c, p) for c in range(DC) for p in PASSES]
    return [(c, p, i == 0, i == len(steps) - 1) for i, (c, p) in enumerate(steps)]


class SplitX:
    pass


def split_x_signals(sem):
    x = SplitX()
    x.hi_ready = sem("x_hi_ready")
    x.lo_ready = sem("x_lo_ready")
    x.base = -HALVES
    return x


def split_x_tensors(mem, st, stage):
    x = st.split
    x.base += HALVES
    x.parts = mem.sb(f"{stage}_xs", [P, 2, DC, TOK], F32R)
    return x


def split_x_scalar(act, st, x):
    for f in range(HALVES):
        cols = slice(f * BANK, (f + 1) * BANK)
        act.activation(x.parts[:, 0, :, cols], st.xT[:, :, cols], ACT.Copy).then_inc(x.hi_ready, 1)


def split_x_vector(dve, st, x):
    for f in range(HALVES):
        cols = slice(f * BANK, (f + 1) * BANK)
        dve.wait_ge(x.hi_ready, x.base + f + 1)
        dve.tensor_tensor(x.parts[:, 1, :, cols], st.xT[:, :, cols], x.parts[:, 0, :, cols],
                          ALU.subtract).then_inc(x.lo_ready, 1)



NORM_SIGNALS = ("out_ready", "summed", "stats_done", "aggregated", "moments_done", "rstd_done",
                "x_ready", "turned", "xT_ready")


class Norm:
    pass


def norm_signals(sem):
    n = Norm()
    n.out_ready, n.summed, n.stats_done, n.aggregated, n.moments_done, n.rstd_done, n.x_ready, n.turned, n.xT_ready = (
        sem(f"norm_{name}") for name in NORM_SIGNALS)
    n.base = -TILES
    return n


def norm_tensors(mem, st, stage):
    n = st.norm
    n.base += TILES
    n.stats = mem.sb(f"{stage}_stats", [P, TILES, 6])
    n.moments = mem.sb(f"{stage}_moments", [P, TILES, 2])
    n.vareps = mem.sb(f"{stage}_vareps", [P, TILES])
    n.rstd = mem.sb(f"{stage}_rstd", [P, TILES])
    return n


def norm_sum(dve, st, n, part, t):
    dve.wait_ge(n.out_ready, n.base + t + 1)
    dve.tensor_tensor(st.x[:, t, :], part(t), st.x[:, t, :], ALU.add).then_inc(n.summed, 1)
    dve.wait_ge(n.summed, n.base + t + 1)
    dve.bn_stats(n.stats[:, t, :], st.x[:, t, :]).then_inc(n.stats_done, 1)
    dve.wait_ge(n.stats_done, n.base + t + 1)
    dve.bn_aggr(n.moments[:, t, :], n.stats[:, t, :]).then_inc(n.aggregated, 1)
    dve.wait_ge(n.aggregated, n.base + t + 1)
    dve.tensor_scalar(n.vareps[:, t:t + 1], n.moments[:, t, 1:2], LN_EPS, None, ALU.add).then_inc(n.moments_done, 1)


def norm_apply(dve, st, n, t):
    dve.wait_ge(n.rstd_done, n.base + t + 1)
    dve.tensor_scalar(st.x[:, t, :], st.x[:, t, :], n.moments[:, t, 0:1], n.rstd[:, t:t + 1],
                      ALU.subtract, ALU.mult).then_inc(n.x_ready, 1)


def norm_vector(dve, st, n, part):
    for t in range(TILES + 1):
        if t < TILES:
            norm_sum(dve, st, n, part, t)
        if t > 0:
            norm_apply(dve, st, n, t - 1)


def norm_rstd(pool, st, n, t):
    pool.wait_ge(n.moments_done, n.base + t + 1)
    pool.tensor_tensor(n.rstd[:, t:t + 1], n.vareps[:, t:t + 1], st.minus_half[:, :], ALU.pow).then_inc(n.rstd_done, 1)


def norm_pool(pool, st, n):
    for t in range(TILES):
        norm_rstd(pool, st, n, t)


def norm_keep(act, st, n, turn, t):
    act.wait_ge(n.turned, n.base + t + 1)
    act.activation(st.xT[:, :, tile_cols(t)], turn[t % 2], ACT.Copy).then_inc(n.xT_ready, 1)


def norm_tensor(pe, st, n, turn, t, depth=2):
    pe.wait_ge(n.x_ready, n.base + t + 1)
    if t >= depth:
        pe.wait_ge(n.xT_ready, n.base + t - depth + 1)
    for c in range(DC):
        last = pe.transpose(turn[t % 2][:, c, :], st.x[:, t, tile_cols(c)], st.ident[:, :])
    last.then_inc(n.turned, 1)



def self_attention(nc, st, sem, d):
    with Memory(nc) as outer:
        wo = outer.sb("sa_wo", [P, HEADS, DM])
        zT = outer.sb("sa_zT", [P, HEADS, TOK])
        bo = outer.sb("sa_bo", [P, DM])
        proj = [outer.psum(f"sa_proj{i}", [P, BANK]) for i in range(2)]
        score = [outer.psum(f"sa_score{i}", [P, BANK]) for i in range(3)]
        turn = [outer.psum(f"sa_turn{i}", [P, BANK]) for i in range(2)]
        zbank = outer.psum("sa_z", [P, BANK])
        self_attention_heads(nc, st, sem, d, wo, zT, bo, proj, score, turn, zbank)
        self_attention_output(nc, st, wo, zT, proj, score, turn)


def self_attention_heads(nc, st, sem, d, wo, zT, bo, proj, score, turn, zbank):
    SCALE = float(HD) ** -0.5
    with Memory(nc) as mem:
        w = [mem.sb(f"sa_w{s}", [P, 2, DC, HD]) for s in range(2)]
        ws = [mem.sb(f"sa_ws{s}", [P, 2, 2, DC, HD], F32R) for s in range(2)]
        wv = mem.sb("sa_wv", [P, DC, 2, HD])
        wvs = [mem.sb(f"sa_wvs{g}", [P, 2, DC, 2, HD], F32R) for g in range(2)]
        bias = mem.sb("sa_bias", [P, 3, HEADS])
        headbias = [mem.sb(f"sa_headbias{s}", [P, 2]) for s in range(2)]
        maskf = mem.sb("sa_maskf", [P, P])
        qT = [mem.sb(f"sa_qT{s}", [P, TOK]) for s in range(2)]
        kT = [mem.sb(f"sa_kT{s}", [P, TOK]) for s in range(2)]
        v = [mem.sb(f"sa_v{g}", [P, TILES, 2, HD]) for g in range(2)]
        probs = [mem.sb(f"sa_probs{s}", [P, 3 * BANK]) for s in range(2)]
        probsT = mem.sb("sa_probsT", [P, 2, 3 * P])
        negmax = mem.sb("sa_negmax", [P, 8])
        rowsum = mem.sb("sa_rowsum", [P, 8])
        rinv = mem.sb("sa_rinv", [P, 8])
        zout = [zbank, score[0]]

        w_loaded = [sem(f"sa_w_loaded{s}") for s in range(2)]
        wv_loaded = sem("sa_wv_loaded")
        w_split = sem("sa_w_split")
        wv_split = sem("sa_wv_split")
        xs = split_x_tensors(mem, st, "sa")
        rest_loaded = sem("sa_rest_loaded")
        consts_loaded = sem("sa_consts_loaded")
        bq_scaled = sem("sa_bq_scaled")
        proj_ready = sem("sa_proj_ready")
        qk_ready = sem("sa_qk_ready")
        v_ready = sem("sa_v_ready")
        score_ready = sem("sa_score_ready")
        max_ready = sem("sa_max_ready")
        exp_ready = sem("sa_exp_ready")
        rinv_ready = sem("sa_rinv_ready")
        probs_ready = sem("sa_probs_ready")
        turn_ready = sem("sa_turn_ready")
        probsT_even = sem("sa_probsT_even")
        probsT_odd = sem("sa_probsT_odd")
        hb_ready = sem("sa_headbias_ready")
        z_ready = sem("sa_z_ready")
        zT_ready = sem("sa_zT_ready")

        def score_cols(b, q):
            return (0, b * P, P) if q == 0 else (1 + b // 2, (b % 2) * SEQ, SEQ)

        with nc.Block() as block:
            @block.sync
            def _(sp):
                sp.dma_start(st.xT[:, :, :], d["xT"]).then_inc(st.xT_loaded, 16)
                sp.dma_start(w[0][:], d["sa_w"][0]).then_inc(w_loaded[0], 16)
                sp.dma_start(wv[:], d["sa_wv"][0]).then_inc(wv_loaded, 16)
                sp.dma_start(bias[:], d["sa_bias"]).then_inc(rest_loaded, 16)
                sp.dma_start(maskf[:], d["mask"]).then_inc(consts_loaded, 16)
                sp.dma_start(st.ident[:], d["ident"]).then_inc(consts_loaded, 16)
                sp.dma_start(w[1][:], d["sa_w"][1]).then_inc(w_loaded[1], 16)
                sp.dma_start(st.x[:], d["x"]).then_inc(rest_loaded, 16)
                sp.dma_start(bo[:], d["sa_bo"].partition_broadcast(P)).then_inc(rest_loaded, 16)
                sp.dma_start(wo[:], d["sa_wo"]).then_inc(rest_loaded, 16)
                context_loads(sp, st, d)
                with sp.Fori(0, HEADS // 2 - 1) as i:
                    for s in range(2):
                        sp.wait_ge(w_split, 4 * i + 2 * s + 2)
                        sp.dma_start(w[s][:], d["sa_w"][2 * i + 2 + s]).then_inc(w_loaded[s], 16)
                        if s == 0:
                            sp.wait_ge(wv_split, 2 * i + 2)
                            sp.dma_start(wv[:], d["sa_wv"][i + 1]).then_inc(wv_loaded, 16)

            @block.gpsimd
            def _(pool):
                pool.memset(st.minus_half[:, :], -0.5).then_inc(st.consts_ready, 1)
                pool.memset(st.ones[:, :], 1.0).then_inc(st.consts_ready, 1)
                pool.wait_ge(w_loaded[0], 16)
                pool.tensor_copy(ws[0][:, 0], w[0][:]).then_inc(w_split, 1)
                pool.wait_ge(wv_loaded, 16)
                pool.tensor_copy(wvs[0][:, 0], wv[:]).then_inc(wv_split, 1)
                pool.wait_ge(consts_loaded, 32)
                pool.tensor_copy(st.identb[:], st.ident[:]).then_inc(st.consts_ready, 1)
                pool.tensor_copy(st.mask[:], maskf[:]).then_inc(st.consts_ready, 1)

                def split_w(h, s, loads):
                    pool.wait_ge(w_loaded[s], 16 * loads)
                    wait_past(pool, proj_ready, 6 * h - 6)
                    flat = [a.rearrange("p m c e -> p (m c) e") for a in (w[s][:], ws[s][:, 0], ws[s][:, 1])]
                    split_on(pool, ones_like(st, 2 * DC, HD), *flat, w_split, 2 * h)

                def split_wv(pair, g):
                    pool.wait_ge(wv_loaded, 16 * pair + 16)
                    wait_past(pool, proj_ready, 12 * pair - 12)
                    flat = [a.rearrange("p c r e -> p (c r) e") for a in (wv[:], wvs[g][:, 0], wvs[g][:, 1])]
                    split_on(pool, ones_like(st, 2 * DC, HD), *flat, wv_split, 2 * pair)

                pool.wait_ge(st.consts_ready, 4)
                pool.wait_ge(w_split, 2)
                pool.wait_ge(wv_split, 2)
                split_w(1, 1, 1)
                split_w(2, 0, 2)
                split_wv(1, 1)
                split_w(3, 1, 2)
                with pool.Fori(1, HEADS // 4) as i:
                    for g in range(2):
                        split_w(4 * i + 2 * g, 0, 2 * i + g + 1)
                        split_wv(2 * i + g, g)
                        split_w(4 * i + 2 * g + 1, 1, 2 * i + g + 1)

            @block.tensor
            def _(pe):
                def project(h, u, f):
                    s, g = u % 2, u // 2
                    if f == 0:
                        pe.wait_ge(w_split, 2 * h + 2)
                    if f == 4 and s == 0:
                        pe.wait_ge(wv_split, h + 2)
                    if f < 2:
                        wait_past(pe, v_ready, 2 * h + f - 1)
                    else:
                        pe.wait_ge(qk_ready, 4 * h + f - 1)
                    if isinstance(h, int) and h == 0 and f < 2:
                        pe.wait_ge(xs.lo_ready, xs.base + f + 1)
                    for c, (k, m), first, end in products() if f < 4 else ():
                        last = pe.matmul(proj[f % 2][:, :], ws[s][:, k, f // 2, c, :],
                                         xs.parts[:, m, c, (f % 2) * BANK:(f % 2 + 1) * BANK],
                                         start=first, stop=end)
                    for j in range(2) if f >= 4 else ():
                        t = 4 * s + 2 * (f - 4) + j
                        for c, (k, m), first, end in products():
                            last = pe.matmul(proj[f % 2][:, j * 2 * HD:(j + 1) * 2 * HD], xs.parts[:, k, c, tile_cols(t)],
                                             wvs[g][:, m, c, :, :].rearrange("p r e -> p (r e)"), start=first, stop=end)
                    last.then_inc(proj_ready, 1)

                def scores(h, s):
                    pe.wait_ge(qk_ready, 4 * h + 4)
                    wait_past(pe, zT_ready, 2 * h - 2)
                    wait_past(pe, exp_ready, 8 * h)
                    for bank in range(3):
                        for b in range(BATCH):
                            for q in range(2):
                                at, c0, width = score_cols(b, q)
                                if at != bank:
                                    continue
                                k0 = b * SEQ
                                pe.matmul(score[at][:, c0:c0 + width], qT[s][:, k0 + q * P:k0 + q * P + P],
                                          kT[s][:, k0:k0 + width], start=True, stop=False)
                                last = pe.matmul(score[at][:, c0 + width - P:c0 + width], st.identb[:], st.mask[:],
                                                 start=False, stop=True)
                        last.then_inc(score_ready, 1)

                def turn_probs(h, s, b):
                    pe.wait_ge(probs_ready, 8 * h + 5 + b)
                    o = turn[b % 2]
                    pe.transpose(o[:, 0:P], probs[s][:, b * P:(b + 1) * P], st.ident[:])
                    c0 = BANK + b * SEQ
                    pe.transpose(o[:, P:2 * P], probs[s][:, c0:c0 + P], st.ident[:])
                    pe.transpose(o[:, 2 * P:3 * P], probs[s][:, c0 + P:c0 + 2 * P], st.ident[:]).then_inc(turn_ready, 1)

                def weigh(h, u, b):
                    s, g = u % 2, u // 2
                    if b == 0:
                        pe.wait_ge(v_ready, 2 * h + 4 - 2 * s)
                        wait_past(pe, zT_ready, 2 * h)
                    pe.wait_ge((probsT_even, probsT_odd)[b % 2], 2 * h + b // 2 + 1)
                    z = zout[b // 2][:, (b % 2) * SEQ:(b % 2 + 1) * SEQ]
                    pe.matmul(z, v[g][:, 2 * b, s, :], probsT[:, b % 2, 0:2 * P], start=True, stop=False)
                    last = pe.matmul(z[:, P:2 * P], v[g][:, 2 * b + 1, s, :], probsT[:, b % 2, 2 * P:3 * P],
                                     start=False, stop=True)
                    if b % 2:
                        last.then_inc(z_ready, 1)

                def step(h, u, attend=True, more=True):
                    before, after = (u - 1) % 4, (u + 1) % 4
                    if more is not None:
                        scores(h, u % 2)
                    if attend:
                        turn_probs(h - 1, before % 2, 0)
                        turn_probs(h - 1, before % 2, 1)
                    if more:
                        project(h + 1, after, 0)
                    if attend:
                        weigh(h - 1, before, 0)
                        weigh(h - 1, before, 1)
                        turn_probs(h - 1, before % 2, 2)
                        turn_probs(h - 1, before % 2, 3)
                    if more:
                        project(h + 1, after, 1)
                    if attend:
                        if more is not None:
                            pe.wait_ge(exp_ready, 8 * h + 4)
                        weigh(h - 1, before, 2)
                        weigh(h - 1, before, 3)
                    if more:
                        for f in range(2, 6):
                            project(h + 1, after, f)

                pe.wait_ge(w_split, 2)
                for f in range(6):
                    project(0, 0, f)
                pe.wait_ge(rest_loaded, 16 * 4)
                pe.wait_ge(consts_loaded, 32)
                pe.wait_ge(st.consts_ready, 4)
                step(0, 0, attend=False)
                step(1, 1)
                step(2, 2)
                with pe.Fori(0, HEADS // 4 - 1) as i:
                    for k in range(3, 7):
                        step(4 * i + k, k % 4)
                step(HEADS - 1, 3, more=False)
                step(HEADS, 0, more=None)

            @block.scalar
            def _(act):
                def keep_qk(h, s, f):
                    act.wait_ge(proj_ready, 6 * h + f + 1)
                    act.wait_ge(hb_ready, h + 1)
                    dst = (qT if f < 2 else kT)[s][:, (f % 2) * BANK:(f % 2 + 1) * BANK]
                    act.activation(dst, proj[f % 2][:, :], ACT.Identity, bias=headbias[s][:, f // 2:f // 2 + 1],
                                   scale=SCALE if f < 2 else 1.0).then_inc(qk_ready, 1)

                def exps(h, s, bank):
                    act.wait_ge(max_ready, 3 * h + bank + 1)
                    wait_past(act, turn_ready, 4 * h - 4)
                    for j in range(4) if bank == 0 else range(2 * bank + 2, 2 * bank + 4):
                        width = P if bank == 0 else SEQ
                        c0 = j * P if bank == 0 else (j % 2) * SEQ
                        act.activation(probs[s][:, bank * BANK + c0:bank * BANK + c0 + width],
                                       score[bank][:, c0:c0 + width], ACT.Exp, bias=negmax[:, j:j + 1],
                                       accum_out=rowsum[:, j:j + 1]).then_inc(exp_ready, 1)

                def keep_turned(h, b):
                    act.wait_ge(turn_ready, 4 * h + b + 1)
                    act.activation(probsT[:, b % 2, :], turn[b % 2][:, 0:3 * P], ACT.Copy).then_inc(probsT_odd, 1)

                act.wait_ge(st.xT_loaded, 16)
                split_x_scalar(act, st, xs)
                for f in range(4):
                    keep_qk(0, 0, f)

                def step(h, s, attend=True, more=True):
                    if more is not None:
                        exps(h, s, 0)
                    if attend:
                        keep_turned(h - 1, 1)
                    if more is not None:
                        exps(h, s, 1)
                    if more:
                        keep_qk(h + 1, 1 - s, 0)
                    if attend:
                        keep_turned(h - 1, 3)
                    if more is not None:
                        exps(h, s, 2)
                    if more:
                        for f in range(1, 4):
                            keep_qk(h + 1, 1 - s, f)

                step(0, 0, attend=False)
                with act.Fori(0, HEADS // 2 - 1) as i:
                    step(2 * i + 1, 1)
                    step(2 * i + 2, 0)
                step(HEADS - 1, 1, more=False)
                step(HEADS, 0, more=None)

            @block.vector
            def _(dve):
                dve.wait_ge(w_split, 1)
                dve.tensor_tensor(ws[0][:, 1], w[0][:], ws[0][:, 0], ALU.subtract).then_inc(w_split, 1)
                split_x_vector(dve, st, xs)
                dve.wait_ge(wv_split, 1)
                dve.tensor_tensor(wvs[0][:, 1], wv[:], wvs[0][:, 0], ALU.subtract).then_inc(wv_split, 1)
                dve.wait_ge(rest_loaded, 16 * 4)
                dve.tensor_scalar(bias[:, 0, :], bias[:, 0, :], SCALE, None, ALU.mult).then_inc(bq_scaled, 1)

                def keep_v(h, u, j):
                    s, g = u % 2, u // 2
                    t = 4 * s + 2 * j
                    dve.wait_ge(proj_ready, 6 * h + 5 + j)
                    dve.tensor_copy(v[g][:, t:t + 2, :, :].rearrange("p t r e -> p (t r e)"),
                                    proj[j][:, :]).then_inc(v_ready, 1)

                def head_bias(h, s):
                    dve.tensor_copy(headbias[s][:, :].unsqueeze(2), bias[:, 0:2, bass.ds(h, 1)]).then_inc(hb_ready, 1)

                def maxima(h):
                    for bank in range(3):
                        groups, first = (4, 0) if bank == 0 else (2, 2 * bank + 2)
                        dve.wait_ge(score_ready, 3 * h + bank + 1)
                        dve.tensor_reduce(negmax[:, first:first + groups],
                                          score[bank][:, :].rearrange("p (g k) -> p g k", g=groups),
                                          X_AXIS, ALU.max, negate=True).then_inc(max_ready, 1)

                def normalise(h, s, bank):
                    groups, first = (4, 0) if bank == 0 else (2, 2 * bank + 2)
                    width = BANK // groups
                    dve.wait_ge(exp_ready, 8 * h + first + groups)
                    dve.reciprocal(rinv[:, first:first + groups],
                                   rowsum[:, first:first + groups]).then_inc(rinv_ready, 1)
                    dve.wait_ge(rinv_ready, 3 * h + bank + 1)
                    for g in range(groups):
                        part = probs[s][:, bank * BANK + g * width:bank * BANK + (g + 1) * width]
                        dve.tensor_scalar(part, part, rinv[:, first + g:first + g + 1], None,
                                          ALU.mult).then_inc(probs_ready, 1)

                def keep_turned(h, b):
                    dve.wait_ge(turn_ready, 4 * h + b + 1)
                    dve.tensor_copy(probsT[:, 0, :], turn[0][:, 0:3 * P]).then_inc(probsT_even, 1)

                def keep_z(h, p):
                    dve.wait_ge(z_ready, 2 * h + p + 1)
                    dve.tensor_scalar(zT[:, bass.ds(h, 1), p * BANK:(p + 1) * BANK], zout[p][:, :].unsqueeze(1),
                                      bias[:, 2, bass.ds(h, 1)], None, ALU.add).then_inc(zT_ready, 1)

                def step(h, u, attend=True, more=True):
                    s, after = u % 2, (u + 1) % 4
                    if more:
                        head_bias(h + 1, 1 - s)
                    if more is not None:
                        maxima(h)
                    if attend:
                        keep_turned(h - 1, 0)
                    if more is not None:
                        normalise(h, s, 0)
                    if attend:
                        keep_turned(h - 1, 2)
                    if more is not None:
                        normalise(h, s, 1)
                    if attend:
                        keep_z(h - 1, 0)
                    if more is not None:
                        normalise(h, s, 2)
                    if attend:
                        keep_z(h - 1, 1)
                    if more:
                        keep_v(h + 1, after, 0)
                        keep_v(h + 1, after, 1)

                dve.wait_ge(bq_scaled, 1)
                head_bias(0, 0)
                keep_v(0, 0, 0)
                keep_v(0, 0, 1)
                step(0, 0, attend=False)
                step(1, 1)
                step(2, 2)
                with dve.Fori(0, HEADS // 4 - 1) as i:
                    for k in range(3, 7):
                        step(4 * i + k, k % 4)
                for t in range(TILES):
                    dve.tensor_tensor(st.x[:, t, :], st.x[:, t, :], bo[:, :], ALU.add)
                step(HEADS - 1, 3, more=False)
                step(HEADS, 0, more=None)


def self_attention_output(nc, st, wo, zT, proj, score, turn):
    WO_PARTS = 4
    GROUP = HEADS // WO_PARTS
    with Memory(nc) as mem:
        wos = mem.sb("so_wos", [P, 2, HEADS, DM], F32R)
        zs = [mem.sb(f"so_zs{i}", [P, 2, HEADS, P], F32R) for i in range(3)]
        n = norm_tensors(mem, st, "so")
        out_part = lambda t: [score[1], score[2], proj[0], proj[1]][t % 4][:, 0:DM]
        turns = [turn[i][:, 0:DM].rearrange("p (c n) -> p c n", c=DC) for i in range(2)]
        split = st.split
        base = split.base + HALVES
        split.base += WO_PARTS + TILES
        z_count = lambda t: base + (1 if t == 0 else t + 1 + WO_PARTS)

        with nc.Block() as block:
            @block.tensor
            def _(pe):
                for t in range(TILES):
                    if t >= 1:
                        pe.wait_ge(split.lo_ready, z_count(t))
                    if t >= 4:
                        pe.wait_ge(n.summed, n.base + t - 3)
                    for g in range(HEADS):
                        if t == 0 and g % GROUP == 0:
                            pe.wait_ge(split.lo_ready, base + 2 + g // GROUP)
                        for k, m in PASSES:
                            last = pe.matmul(out_part(t), zs[t % 3][:, k, g, :], wos[:, m, g, :],
                                             start=g == 0 and (k, m) == PASSES[0],
                                             stop=g == HEADS - 1 and (k, m) == PASSES[-1])
                    last.then_inc(n.out_ready, 1)
                    if t >= 2:
                        norm_tensor(pe, st, n, turns, t - 2)
                norm_tensor(pe, st, n, turns, TILES - 2)
                norm_tensor(pe, st, n, turns, TILES - 1)

            @block.scalar
            def _(act):
                def high_z(t):
                    if t >= 3:
                        act.wait_ge(n.out_ready, n.base + t - 2)
                    act.activation(zs[t % 3][:, 0, :, :], zT[:, :, tile_cols(t)], ACT.Copy).then_inc(split.hi_ready, 1)

                high_z(0)
                for r in range(WO_PARTS):
                    heads = slice(r * GROUP, (r + 1) * GROUP)
                    act.activation(wos[:, 0, heads, :], wo[:, heads, :], ACT.Copy).then_inc(split.hi_ready, 1)
                for t in range(1, TILES + 3):
                    if t < TILES:
                        high_z(t)
                    if t >= 3:
                        norm_keep(act, st, n, turns, t - 3)

            @block.vector
            def _(dve):
                def low_z(t):
                    dve.wait_ge(split.hi_ready, z_count(t))
                    dve.tensor_tensor(zs[t % 3][:, 1, :, :], zT[:, :, tile_cols(t)], zs[t % 3][:, 0, :, :],
                                      ALU.subtract).then_inc(split.lo_ready, 1)

                low_z(0)
                for r in range(WO_PARTS):
                    heads = slice(r * GROUP, (r + 1) * GROUP)
                    dve.wait_ge(split.hi_ready, base + 2 + r)
                    dve.tensor_tensor(wos[:, 1, heads, :], wo[:, heads, :], wos[:, 0, heads, :],
                                      ALU.subtract).then_inc(split.lo_ready, 1)
                for t in range(1, TILES + 2):
                    if t < TILES:
                        low_z(t)
                    if t - 1 < TILES:
                        norm_sum(dve, st, n, out_part, t - 1)
                    if t >= 2:
                        norm_apply(dve, st, n, t - 2)

            @block.gpsimd
            def _(pool):
                norm_pool(pool, st, n)



PAIRS = HEADS // 2


def cross_tensors(mem, sem, name, vw=None):
    class C:
        pass
    c = C()
    c.rows = mem.sb(f"{name}_rows", [P, TILES, HEADS, KEYS])
    c.vw = vw if vw is not None else mem.sb(f"{name}_vw", [P, BATCH, PAIRS, DM])
    c.max = mem.sb(f"{name}_max", [P, TILES, HEADS])
    c.sum = mem.sb(f"{name}_sum", [P, TILES, HEADS])
    c.inv = mem.sb(f"{name}_inv", [P, TILES, HEADS])
    c.rowsT = mem.sb(f"{name}_rowsT", [P, 2, PAIRS, P])
    c.max_ready = sem(f"{name}_max_ready")
    c.shifted = sem(f"{name}_shifted")
    c.exp_ready = sem(f"{name}_exp_ready")
    c.sum_ready = sem(f"{name}_sum_ready")
    c.inv_ready = sem(f"{name}_inv_ready")
    c.probs_ready = sem(f"{name}_probs_ready")
    c.turned = sem(f"{name}_rows_turned")
    c.rowsT_ready = sem(f"{name}_rowsT_ready")
    return c


def over_keys(a):
    return a.unsqueeze(2).broadcast_to([P, a.shape[1], KEYS])


def cross_normalise_sum(dve, c, t):
    dve.wait_ge(c.exp_ready, t + 1)
    dve.tensor_reduce(c.sum[:, t, :], c.rows[:, t, :, :], X_AXIS, ALU.add).then_inc(c.sum_ready, 1)
    dve.wait_ge(c.sum_ready, t + 1)
    dve.reciprocal(c.inv[:, t, :], c.sum[:, t, :]).then_inc(c.inv_ready, 1)


def cross_exp(act, c, t):
    act.wait_ge(c.shifted, t + 1)
    act.activation(c.rows[:, t, :, :], c.rows[:, t, :, :], ACT.Exp).then_inc(c.exp_ready, 1)


def cross_weights(pool, c, t):
    pool.wait_ge(c.inv_ready, t + 1)
    pool.tensor_tensor(c.rows[:, t, :, :], c.rows[:, t, :, :], over_keys(c.inv[:, t, :]),
                       ALU.mult).then_inc(c.probs_ready, 1)


def cross_turn(pe, st, c, turn, t, probs=None):
    pe.wait_ge(c.probs_ready, probs or t + 1)
    if t >= 1:
        pe.wait_ge(c.rowsT_ready, 2 * t)
    for g in range(PAIRS):
        last = pe.transpose(turn[g // 4][:, (g % 4) * P:(g % 4 + 1) * P],
                            c.rows[:, t, 2 * g:2 * g + 2, :].rearrange("p h k -> p (h k)"), st.ident[:])
        if g % 4 == 3:
            last.then_inc(c.turned, 1)


def cross_keep(act, c, turn, t):
    for j in range(2):
        act.wait_ge(c.turned, 2 * t + j + 1)
        act.activation(c.rowsT[:, t % 2, 4 * j:4 * j + 4, :],
                       turn[j][:, :].rearrange("p (g n) -> p g n", g=4), ACT.Copy).then_inc(c.rowsT_ready, 1)


def cross_out(pe, c, n, part, t):
    pe.wait_ge(c.rowsT_ready, 2 * t + 2)
    if t >= 2:
        pe.wait_ge(n.summed, n.base + t - 1)
    for g in range(PAIRS):
        last = pe.matmul(part(t), c.rowsT[:, t % 2, g, :], c.vw[:, t // 2, g, :],
                         start=g == 0, stop=g == PAIRS - 1)
    last.then_inc(n.out_ready, 1)



KV = 4
GROUP = HEADS // KV
CONTEXT_FIRST = dict(wk=(DC, KV * HD), wv=(DC, KV * HD), bv=(KV,), norms=(2,), bq=(HEADS,), amask=(2, KEYS),
                     bk=(KV * HD,))


def context_loads(sp, st, d):
    e = st.first2
    sp.dma_start(st.ctxT[:], d["ctxT"]).then_inc(st.ctxT_loaded, 16)
    for name in CONTEXT_FIRST:
        src = d[f"ca_{name}"]
        sp.dma_start(e[name], src.partition_broadcast(P) if name == "bk" else src).then_inc(e.loaded, 16)


def context_attention(nc, st, sem, d):
    SCALE = float(HD) ** -0.5
    RMS_EPS = 1e-6
    e = st.first2
    wk, wv, bv, norms, bq, amask, bk = (e[name] for name in CONTEXT_FIRST)
    with Memory(nc) as mem:
        c = cross_tensors(mem, sem, "ca")
        xs = split_x_tensors(mem, st, "ca")
        w = [mem.sb(f"ca_w{s}", [P, DC, HD]) for s in range(2)]
        ws = [mem.sb(f"ca_ws{s}", [P, 2, DC, HD], F32R) for s in range(2)]
        wo = mem.sb("ca_wo", [P, HEADS, DM])
        headbias = mem.sb("ca_headbias", [P, 4])
        gain = mem.sb("ca_gain", [P, 1])
        ones = mem.sb("ca_ones", [P, KEYS])
        rms_eps = mem.sb("ca_rms_eps", [P, 1])
        k = mem.sb("ca_k", [P, 2, KV * HD])
        ksq = mem.sb("ca_ksq", [P, 2, KV * HD])
        kss = mem.sb("ca_kss", [P, 2 * KV])
        kstd = mem.sb("ca_kstd", [P, 2 * KV])
        krms = mem.sb("ca_krms", [P, 2 * KV])
        kT = mem.sb("ca_kT", [P, KV, CTX])
        vT = mem.sb("ca_vT", [P, KV, CTX])
        qT = [mem.sb(f"ca_qT{s}", [P, TOK]) for s in range(2)]
        qsq = [mem.sb(f"ca_qsq{s}", [P, TOK]) for s in range(2)]
        qmean = mem.sb("ca_qmean", [P, 4, TILES])
        qrms = mem.sb("ca_qrms", [P, 4, TILES])
        cells = mem.sb("ca_cells", [P, 4, TILES, KEYS])
        rowmax = mem.sb("ca_rowmax", [P, 4, TILES])
        rowsum = mem.sb("ca_rowsum", [P, 4, TILES])
        rowinv = mem.sb("ca_rowinv", [P, 4, TILES])
        proj = [mem.psum(f"ca_proj{i}", [P, BANK]) for i in range(4)]
        score = [mem.psum(f"ca_score{i}", [P, BANK]) for i in range(2)]
        square = [mem.psum(f"ca_square{i}", [P, BANK]) for i in range(2)]
        n = norm_tensors(mem, st, "ca")
        part = lambda t: score[t % 2][:, 0:DM]
        turns = [square[i][:, 0:DM].rearrange("p (c n) -> p c n", c=DC) for i in range(2)]

        w_loaded = [sem(f"ca_w_loaded{s}") for s in range(2)]
        w_split = sem("ca_w_split")
        wo_loaded = sem("ca_wo_loaded")
        k_projected = sem("ca_k_projected")
        v_projected = sem("ca_v_projected")
        k_biased = sem("ca_k_biased")
        k_squared = sem("ca_k_squared")
        k_summed = sem("ca_k_summed")
        k_std = sem("ca_k_std")
        k_rms = sem("ca_k_rms")
        k_normed = sem("ca_k_normed")
        k_turned = sem("ca_k_turned")
        kT_ready = sem("ca_kT_ready")
        vT_ready = sem("ca_vT_ready")
        vw_done = sem("ca_vw_done")
        vw_ready = sem("ca_vw_ready")
        consts_ready = sem("ca_consts_ready")
        q_projected = sem("ca_q_projected")
        q_ready = sem("ca_q_ready")
        qsq_ready = sem("ca_qsq_ready")
        scored = sem("ca_scored")
        headbias_ready = sem("ca_headbias_ready")
        qmean_ready = sem("ca_qmean_ready")
        qrms_ready = sem("ca_qrms_ready")
        scaled = sem("ca_scaled")
        masked = sem("ca_masked")

        with nc.Block() as block:
            @block.sync
            def _(sp):
                sp.dma_start(w[0][:], d["ca_wq"][0]).then_inc(w_loaded[0], 16)
                sp.dma_start(w[1][:], d["ca_wq"][1]).then_inc(w_loaded[1], 16)
                sp.dma_start(wo[:], d["ca_wo"]).then_inc(wo_loaded, 16)
                recurrent_loads(sp, st, d)
                def load(i, u):
                    sp.wait_ge(w_split, 8 * i + 2 * u + 2)
                    sp.dma_start(w[u % 2][:], d["ca_wq"][4 * i + u + 2]).then_inc(w_loaded[u % 2], 16)
                with sp.Fori(0, KV - 1) as i:
                    for u in range(GROUP):
                        load(i, u)
                load(KV - 1, 0)
                load(KV - 1, 1)

            @block.tensor
            def _(pe):
                pe.wait_ge(st.ctxT_loaded, 16)
                pe.wait_ge(e.loaded, e.loads)
                for t in range(2):
                    for j in range(DC):
                        last = pe.matmul(proj[t][:, :], st.ctxT[:, j, tile_cols(t)], wk[:, j, :],
                                         start=j == 0, stop=j == DC - 1)
                    last.then_inc(k_projected, 1)
                for g in range(KV):
                    for j in range(DC):
                        last = pe.matmul(proj[2 + g // 2][:, (g % 2) * CTX:(g % 2 + 1) * CTX],
                                         wv[:, j, g * HD:(g + 1) * HD], st.ctxT[:, j, :],
                                         start=j == 0, stop=j == DC - 1)
                    if g % 2:
                        last.then_inc(v_projected, 1)
                pe.wait_ge(vT_ready, 2)
                pe.wait_ge(wo_loaded, 16)
                for r in range(2 * PAIRS):
                    pair, half = r // 2, r % 2
                    if r >= 2:
                        pe.wait_ge(vw_ready, r - 1)
                    for b in range(2):
                        for s in range(2):
                            h = 2 * pair + s
                            last = pe.matmul(score[r % 2][s * KEYS:(s + 1) * KEYS, b * DM:(b + 1) * DM],
                                             vT[:, h // GROUP, (2 * half + b) * KEYS:(2 * half + b + 1) * KEYS],
                                             wo[:, h, :], start=True, stop=True)
                    last.then_inc(vw_done, 1)
                pe.wait_ge(k_normed, 1)
                for g in range(KV):
                    for t in range(2):
                        last = pe.transpose(square[g // 2][:, (g % 2) * CTX + t * P:(g % 2) * CTX + (t + 1) * P],
                                            k[:, t, g * HD:(g + 1) * HD], st.ident[:])
                    if g % 2:
                        last.then_inc(k_turned, 1)

                def project(h, s):
                    pe.wait_ge(w_split, 2 * h + 2)
                    for f in range(2):
                        wait_past(pe, q_ready, 2 * h + f - 3)
                        for j, (k, m), first, end in products():
                            last = pe.matmul(proj[2 * s + f][:, :], ws[s][:, k, j, :],
                                             xs.parts[:, m, j, f * BANK:(f + 1) * BANK], start=first, stop=end)
                        last.then_inc(q_projected, 1)

                def scores(h, i, s):
                    pe.wait_ge(qsq_ready, 2 * h + 2)
                    wait_past(pe, qmean_ready, h - 1)
                    for t in range(TILES):
                        pe.matmul(square[s][:, t * KEYS:(t + 1) * KEYS], qsq[s][:, tile_cols(t)], ones[:, :], start=True, stop=True)
                    wait_past(pe, scaled, h - 1)
                    for t in range(TILES):
                        last = pe.matmul(score[s][:, t * KEYS:(t + 1) * KEYS], qT[s][:, tile_cols(t)],
                                         kT[:, bass.ds(i, 1), (t // 2) * KEYS:(t // 2 + 1) * KEYS].squeeze(1),
                                         start=True, stop=True)
                    last.then_inc(scored, 1)

                pe.wait_ge(xs.lo_ready, xs.base + HALVES)
                pe.wait_ge(kT_ready, 2)
                pe.wait_ge(k_biased, 2)
                pe.wait_ge(vw_ready, 2 * PAIRS)
                project(0, 0)

                def step(i, u, more=True):
                    h = GROUP * i + u
                    if more:
                        project(h + 1, (u + 1) % 2)
                    scores(h, i, u % 2)
                for u in range(GROUP):
                    step(0, u)
                with pe.Fori(1, KV - 1) as i:
                    for u in range(GROUP):
                        step(i, u)
                for u in range(GROUP):
                    step(KV - 1, u, u < GROUP - 1)
                pe.wait_ge(scaled, HEADS)
                for t in range(TILES + 2):
                    if t < TILES:
                        cross_turn(pe, st, c, proj[0:2], t, HEADS)
                    if 0 <= t - 1 < TILES:
                        cross_out(pe, c, n, part, t - 1)
                    if t >= 3:
                        norm_tensor(pe, st, n, turns, t - 3)
                norm_tensor(pe, st, n, turns, TILES - 1)

            @block.scalar
            def _(act):
                split_x_scalar(act, st, xs)
                act.wait_ge(consts_ready, 1)
                for j in range(2):
                    act.wait_ge(v_projected, j + 1)
                    for g in range(2 * j, 2 * j + 2):
                        last = act.activation(vT[:, g, :], proj[2 + j][:, (g % 2) * CTX:(g % 2 + 1) * CTX],
                                              ACT.Identity, bias=bv[:, g:g + 1])
                    last.then_inc(vT_ready, 1)
                act.wait_ge(k_summed, 1)
                act.activation(kstd[:, :], kss[:, :], ACT.Sqrt, bias=rms_eps[:, :],
                               scale=1.0 / HD).then_inc(k_std, 1)
                for j in range(2):
                    act.wait_ge(k_turned, j + 1)
                    act.activation(kT[:, 2 * j:2 * j + 2, :], square[j][:, :].rearrange("p (g n) -> p g n", g=2),
                                   ACT.Copy, scale=gain[:, :]).then_inc(kT_ready, 1)

                def keep_q(h, s, slot):
                    act.wait_ge(headbias_ready, h + 1)
                    wait_past(act, scored, h - 1)
                    for f in range(2):
                        cols = slice(f * BANK, (f + 1) * BANK)
                        act.wait_ge(q_projected, 2 * h + f + 1)
                        act.activation(qT[s][:, cols], proj[2 * s + f][:, :], ACT.Identity,
                                       bias=headbias[:, slot:slot + 1]).then_inc(q_ready, 1)
                    for f in range(2):
                        cols = slice(f * BANK, (f + 1) * BANK)
                        act.wait_ge(q_ready, 2 * h + f + 1)
                        act.activation(qsq[s][:, cols], qT[s][:, cols], ACT.Square).then_inc(qsq_ready, 1)

                def exps(h, slot):
                    act.wait_ge(c.shifted, h + 1)
                    act.activation(cells[:, slot, :, :], cells[:, slot, :, :], ACT.Exp).then_inc(c.exp_ready, 1)

                keep_q(0, 0, 0)

                def step(h, u):
                    if not isinstance(h, int) or h + 1 < HEADS:
                        keep_q(h + 1, (u + 1) % 2, (u + 1) % 4)
                    if not isinstance(h, int) or h >= 2:
                        exps(h - 2, (u - 2) % 4)
                for h in range(GROUP):
                    step(h, h)
                with act.Fori(1, KV - 1) as i:
                    for u in range(GROUP):
                        step(GROUP * i + u, u)
                for h in range(HEADS - GROUP, HEADS + 2):
                    step(h, h % 4)
                for t in range(TILES + 4):
                    if 0 <= t - 1 < TILES:
                        cross_keep(act, c, proj[0:2], t - 1)
                    if 0 <= t - 4:
                        norm_keep(act, st, n, turns, t - 4)

            @block.vector
            def _(dve):
                dve.memset(ones[:], 1.0)
                dve.memset(rms_eps[:], RMS_EPS)
                split_x_vector(dve, st, xs)
                dve.wait_ge(e.loaded, e.loads)
                dve.scalar_tensor_tensor(gain[:], norms[:, 0:1], SCALE, norms[:, 1:2],
                                         ALU.mult, ALU.mult).then_inc(consts_ready, 1)
                for t in range(2):
                    dve.wait_ge(k_projected, t + 1)
                    dve.tensor_tensor(k[:, t, :], proj[t][:, :], bk[:, :], ALU.add).then_inc(k_biased, 1)
                dve.wait_ge(k_biased, 2)
                dve.tensor_tensor(ksq[:], k[:], k[:], ALU.mult).then_inc(k_squared, 1)
                dve.wait_ge(k_squared, 1)
                dve.tensor_reduce(kss[:, :], ksq[:].rearrange("p t (g e) -> p (t g) e", g=KV),
                                  X_AXIS, ALU.add).then_inc(k_summed, 1)
                dve.wait_ge(k_std, 1)
                dve.reciprocal(krms[:, :], kstd[:, :]).then_inc(k_rms, 1)
                dve.wait_ge(k_rms, 1)
                kk = k[:].rearrange("p t (g e) -> p (t g) e", g=KV)
                dve.tensor_tensor(kk, kk, krms[:, :].unsqueeze(2).broadcast_to([P, 2 * KV, HD]),
                                  ALU.mult).then_inc(k_normed, 1)
                for r in range(2 * PAIRS):
                    dve.wait_ge(vw_done, r + 1)
                    dve.tensor_copy(c.vw[:, 2 * (r % 2):2 * (r % 2) + 2, r // 2, :],
                                    score[r % 2][:, :].rearrange("p (b n) -> p b n", b=2)).then_inc(vw_ready, 1)

                def head_bias(h, slot):
                    dve.tensor_copy(headbias[:, slot:slot + 1], bq[:, bass.ds(h, 1)]).then_inc(headbias_ready, 1)

                def mean_squares(h, s, slot):
                    dve.wait_ge(scored, h + 1)
                    sums = square[s][:, :].rearrange("p (t k) -> p t k", t=TILES)[:, :, 0]
                    dve.tensor_scalar(qmean[:, slot, :], sums, 1.0 / HD, RMS_EPS,
                                      ALU.mult, ALU.add).then_inc(qmean_ready, 1)

                def scale_scores(h, s, slot):
                    dve.wait_ge(qrms_ready, h + 1)
                    wait_past(dve, c.probs_ready, h - 3)
                    dve.tensor_tensor(cells[:, slot, :, :], score[s][:, :].rearrange("p (t k) -> p t k", t=TILES),
                                      over_keys(qrms[:, slot, :]), ALU.mult).then_inc(scaled, 1)

                def shift(h, slot):
                    dve.wait_ge(masked, h + 1)
                    dve.tensor_reduce(rowmax[:, slot, :], cells[:, slot, :, :], X_AXIS, ALU.max).then_inc(c.max_ready, 1)
                    dve.wait_ge(c.max_ready, h + 1)
                    dve.tensor_tensor(cells[:, slot, :, :], cells[:, slot, :, :], over_keys(rowmax[:, slot, :]),
                                      ALU.subtract).then_inc(c.shifted, 1)

                def normalise(h, slot):
                    dve.wait_ge(c.exp_ready, h + 1)
                    dve.tensor_reduce(rowsum[:, slot, :], cells[:, slot, :, :], X_AXIS, ALU.add).then_inc(c.sum_ready, 1)
                    dve.wait_ge(c.sum_ready, h + 1)
                    dve.reciprocal(rowinv[:, slot, :], rowsum[:, slot, :]).then_inc(c.inv_ready, 1)
                    dve.wait_ge(c.inv_ready, h + 1)
                    dve.tensor_tensor(c.rows[:, :, bass.ds(h, 1), :].squeeze(2), cells[:, slot, :, :],
                                      over_keys(rowinv[:, slot, :]), ALU.mult).then_inc(c.probs_ready, 1)

                head_bias(0, 0)
                head_bias(1, 1)

                def step(h, u):
                    inside = not isinstance(h, int)
                    if inside or h < HEADS:
                        mean_squares(h, u % 2, u)
                    if inside or h + 2 < HEADS:
                        head_bias(h + 2, (u + 2) % 4)
                    if inside or 0 <= h - 1 < HEADS:
                        scale_scores(h - 1, (u - 1) % 2, (u - 1) % 4)
                    if inside or 0 <= h - 2 < HEADS:
                        shift(h - 2, (u - 2) % 4)
                    if inside or 0 <= h - 3 < HEADS:
                        normalise(h - 3, (u - 3) % 4)
                for h in range(GROUP):
                    step(h, h)
                with dve.Fori(1, KV - 1) as i:
                    for u in range(GROUP):
                        step(GROUP * i + u, u)
                for h in range(HEADS - GROUP, HEADS + 3):
                    step(h, h % 4)
                for t in range(TILES + 3):
                    if 0 <= t - 2 < TILES:
                        norm_sum(dve, st, n, part, t - 2)
                    if 0 <= t - 3:
                        norm_apply(dve, st, n, t - 3)

            @block.gpsimd
            def _(pool):
                def split_w(h, s, loads):
                    pool.wait_ge(w_loaded[s], 16 * loads)
                    wait_past(pool, q_projected, 2 * h - 2)
                    split_on(pool, ones_like(st, DC, HD), w[s][:], ws[s][:, 0], ws[s][:, 1], w_split, 2 * h)
                split_w(0, 0, 1)
                split_w(1, 1, 1)

                def q_rms(h, slot):
                    pool.wait_ge(qmean_ready, h + 1)
                    pool.tensor_tensor(qrms[:, slot, :], qmean[:, slot, :], st.minus_half[:, :].broadcast_to([P, TILES]),
                                       ALU.pow).then_inc(qrms_ready, 1)

                def add_mask(h, slot):
                    pool.wait_ge(scaled, h + 1)
                    cell = cells[:, slot, :, :].rearrange("p (b q) k -> p b (q k)", q=2)
                    pool.tensor_tensor(cell, cell, amask.rearrange("p q k -> p (q k)").unsqueeze(1).broadcast_to(
                        [P, BATCH, 2 * KEYS]), ALU.add).then_inc(masked, 1)

                def step(h, u, loads):
                    inside = not isinstance(h, int)
                    if inside or h + 2 < HEADS:
                        split_w(h + 2, u % 2, loads)
                    if inside or h < HEADS:
                        q_rms(h, u)
                    if inside or 0 <= h - 1:
                        add_mask(h - 1, (u - 1) % 4)
                for h in range(GROUP):
                    step(h, h, 2 + h // 2)
                with pool.Fori(1, KV - 1) as i:
                    for u in range(GROUP):
                        step(GROUP * i + u, u, 2 * i + 2 + u // 2)
                for h in range(HEADS - GROUP, HEADS + 1):
                    step(h, h % 4, 2 + h // 2)
                norm_pool(pool, st, n)



VD = DM // HEADS
VCOLS = VD + 1


COUNT = HEADS // 2
RECURRENT_FIRST = dict(wq=(DC, DM), wk=(DC, DM), wv=(DC, DM), rowmask=(COUNT,), roww=(3, 2))


def recurrent_loads(sp, st, d):
    e = st.first3
    for name in RECURRENT_FIRST:
        sp.dma_start(e[name], d[f"ra_{name}"]).then_inc(e.loaded, 16)


def recurrent_attention(nc, st, sem, d):
    name = "ra"
    e = st.first3
    wq, wk, wv, rowmask, roww = (e[key] for key in RECURRENT_FIRST)
    with Memory(nc) as mem:
        wo = mem.sb(f"{name}_wo", [P, DC, DM])
        qT = mem.sb(f"{name}_qT", [P, 2, TOK])
        kT = mem.sb(f"{name}_kT", [P, 2, TOK])
        qhead = [mem.sb(f"{name}_qhead{s}", [P, TOK]) for s in range(2)]
        v = mem.sb(f"{name}_v", [P, TILES, HEADS, VCOLS])
        shift = mem.sb(f"{name}_shift", [P, 4, 2])
        probs = mem.sb(f"{name}_probs", [P, 4, BANK])
        probsT = mem.sb(f"{name}_probsT", [P, 2, BANK])
        heads_out = mem.sb(f"{name}_heads_out", [P, TILES, 2, COUNT, VCOLS])
        y = mem.sb(f"{name}_y", [P, TILES, DM])
        rinv = mem.sb(f"{name}_rinv", [P, TILES, 2 * COUNT])
        yT = mem.sb(f"{name}_yT", [P, 2, DC, P])
        score = [mem.psum(f"{name}_score{i}", [P, BANK]) for i in range(4)]
        turn = [mem.psum(f"{name}_turn{i}", [P, BANK]) for i in range(2)]
        out = [mem.psum(f"{name}_out{i}", [P, BANK]) for i in range(2)]
        n = norm_tensors(mem, st, name)

        wo_loaded = sem(f"{name}_wo_loaded")
        consts_ready = sem(f"{name}_consts_ready")
        q_projected = sem(f"{name}_q_projected")
        k_projected = sem(f"{name}_k_projected")
        v_projected = sem(f"{name}_v_projected")
        crossed = sem(f"{name}_crossed")
        qk_ready = sem(f"{name}_qk_ready")
        v_ready = sem(f"{name}_v_ready")
        qhead_ready = sem(f"{name}_qhead_ready")
        scored = sem(f"{name}_scored")
        shift_ready = sem(f"{name}_shift_ready")
        exp_ready = sem(f"{name}_exp_ready")
        probs_turned = sem(f"{name}_probs_turned")
        probsT_even = sem(f"{name}_probsT_even")
        probsT_odd = sem(f"{name}_probsT_odd")
        weighed = sem(f"{name}_weighed")
        heads_kept = sem(f"{name}_heads_kept")
        chain = sem(f"{name}_chain")
        y_ready = sem(f"{name}_y_ready")
        y_turned = sem(f"{name}_y_turned")
        yT_ready = sem(f"{name}_yT_ready")

        part = lambda t: score[t % 2][:, 0:DM]
        yturn = [out[i][:, 0:DM].rearrange("p (c n) -> p c n", c=DC) for i in range(2)]
        turns = [turn[i][:, 0:DM].rearrange("p (c n) -> p c n", c=DC) for i in range(2)]
        widths = (P, SEQ)
        block_at = {(0, 0): 0, (0, 1): P, (1, 1): 2 * P}
        turned_cols = P * len(block_at)

        rowscale = mem.sb(f"{name}_rowscale", [P, 2])
        swap = mem.sb(f"{name}_swap", [P, 2])
        factors = mem.sb(f"{name}_factors", [P, 4, 2])
        cross = mem.sb(f"{name}_cross", [P, 4, BANK])

        def ahead(i, u, lead):
            return (i, u + lead) if u + lead < 8 else (i + 1, u + lead - 8)

        with nc.Block() as block:
            @block.sync
            def _(sp):
                sp.dma_start(wo[:], d["ra_wo"]).then_inc(wo_loaded, 16)
                differential_loads(sp, st, d)

            @block.tensor
            def _(pe):
                pe.wait_ge(e.loaded, e.loads)
                for j in range(4):
                    s, f = j // 2, j % 2
                    for w, banks, ready in ((wq, score[0:2], q_projected), (wk, score[2:4], k_projected)):
                        if j >= 2 and w is wq:
                            pe.wait_ge(qk_ready, 2 * (j - 2) + 2)
                        for c in range(DC):
                            last = pe.matmul(banks[j % 2][:, :], w[:, c, tile_cols(s)],
                                             st.xT[:, c, f * BANK:(f + 1) * BANK], start=c == 0, stop=c == DC - 1)
                        last.then_inc(ready, 1)
                for t in range(TILES):
                    if t >= 2:
                        pe.wait_ge(v_ready, t - 1)
                    for c in range(DC):
                        last = pe.matmul(turn[t % 2][:, 0:DM], st.xT[:, c, tile_cols(t)], wv[:, c, :],
                                         start=c == 0, stop=c == DC - 1)
                    last.then_inc(v_projected, 1)

                def scores(i, u):
                    s, b = u // 4, u % 4
                    if b == 0:
                        pe.wait_ge(qhead_ready, 2 * i + s + 1)
                    k0 = b * SEQ
                    for q, width in enumerate(widths):
                        o = score[u % 4][:, q * SEQ:q * SEQ + width]
                        last = pe.matmul(o, qhead[s][:, k0 + q * P:k0 + (q + 1) * P],
                                         kT[:, s, k0:k0 + width], start=True, stop=False)
                        last = pe.matmul(o[:, width - P:width], st.identb[:], st.mask[:], start=False, stop=True)
                    last.then_inc(scored, 1)

                def turn_probs(i, u):
                    unit = 8 * i + u
                    pe.wait_ge(exp_ready, 2 * unit + 2)
                    wait_past(pe, (probsT_even, probsT_odd)[u % 2], 4 * i + u // 2)
                    for (kt, q), at in block_at.items():
                        last = pe.transpose(turn[u % 2][:, at:at + P],
                                            probs[:, u % 4, q * SEQ + kt * P:q * SEQ + (kt + 1) * P], st.ident[:])
                    last.then_inc(probs_turned, 1)

                def weigh(i, u, fresh):
                    s, b = u // 4, u % 4
                    if b == 0 and not fresh:
                        pe.wait_ge(heads_kept, 2 * i + s - 1)
                    pe.wait_ge((probsT_even, probsT_odd)[u % 2], 4 * i + u // 2 + 1)
                    for q in range(2):
                        o = out[s][:, (2 * b + q) * VCOLS:(2 * b + q + 1) * VCOLS]
                        kts = [kt for kt in range(2) if (kt, q) in block_at]
                        for kt in kts:
                            at = block_at[kt, q]
                            values = v[:, 2 * b + kt, bass.ds(s * COUNT + i, 1), :]
                            last = pe.matmul(o, probsT[:, u % 2, at:at + P], values.squeeze(1),
                                             start=kt == 0, stop=kt == kts[-1])
                    if b == 3:
                        last.then_inc(weighed, 1)

                def units(i, first=False, final=False):
                    for u in range(8):
                        if not (final and u + 3 >= 8):
                            scores(*ahead(i, u, 3))
                        turn_probs(i, u)
                        if u > 0:
                            weigh(i, u - 1, first)
                        elif not first:
                            weigh(i - 1, 7, False)

                pe.wait_ge(qk_ready, 8)
                pe.wait_ge(v_ready, TILES)
                for u in range(3):
                    scores(0, u)
                units(0, first=True)
                with pe.Fori(1, COUNT - 1) as i:
                    units(i)
                units(COUNT - 1, final=True)
                weigh(COUNT - 1, 7, False)

                pe.wait_ge(heads_kept, 2 * COUNT)
                pe.wait_ge(wo_loaded, 16)
                for t in range(TILES + 2):
                    if t < TILES:
                        pe.wait_ge(y_ready, t + 1)
                        if t >= 2:
                            pe.wait_ge(yT_ready, t - 1)
                        for c in range(DC):
                            last = pe.transpose(yturn[t % 2][:, c, :], y[:, t, tile_cols(c)], st.ident[:])
                        last.then_inc(y_turned, 1)
                    if 0 <= t - 1 < TILES:
                        r = t - 1
                        pe.wait_ge(yT_ready, r + 1)
                        if r >= 2:
                            pe.wait_ge(n.summed, n.base + r - 1)
                        for c in range(DC):
                            last = pe.matmul(part(r), yT[:, r % 2, c, :], wo[:, c, :], start=c == 0, stop=c == DC - 1)
                        last.then_inc(n.out_ready, 1)
                    if t >= 3:
                        norm_tensor(pe, st, n, turns, t - 3)
                norm_tensor(pe, st, n, turns, TILES - 1)

            @block.scalar
            def _(act):
                act.wait_ge(e.loaded, e.loads)
                act.wait_ge(chain, 1)
                act.activation(rowscale[:], roww[:, 0, :], ACT.Sqrt).then_inc(consts_ready, 1)
                act.wait_ge(chain, 7)
                for j in range(4):
                    s = j // 2
                    act.wait_ge(k_projected, j + 1)
                    if j >= 2:
                        act.wait_ge(qk_ready, 2 * (j - 2) + 2)
                    act.activation(cross[:, 2 * (j % 2), :], score[2 + j % 2][:, :], ACT.Copy,
                                   scale=factors[:, 1, s:s + 1]).then_inc(crossed, 1)
                    act.activation(cross[:, 2 * (j % 2) + 1, :], score[j % 2][:, :], ACT.Copy,
                                   scale=factors[:, 3, s:s + 1]).then_inc(crossed, 1)
                for t in range(TILES):
                    act.wait_ge(v_projected, t + 1)
                    act.activation(v[:, t, :, 0:VD], turn[t % 2][:, 0:DM].rearrange("p (h e) -> p h e", h=HEADS),
                                   ACT.Copy).then_inc(v_ready, 1)

                def exps(i, u, fresh=False):
                    unit = 8 * i + u
                    act.wait_ge(shift_ready, 2 * unit + 2)
                    if not fresh:
                        act.wait_ge(probs_turned, unit - 3)
                    for q, width in enumerate(widths):
                        act.activation(probs[:, u % 4, q * SEQ:q * SEQ + width], score[u % 4][:, q * SEQ:q * SEQ + width],
                                       ACT.Exp, bias=shift[:, u % 4, q:q + 1]).then_inc(exp_ready, 1)

                def keep_odd(i, u):
                    act.wait_ge(probs_turned, 8 * i + u + 1)
                    act.activation(probsT[:, 1, 0:turned_cols], turn[1][:, 0:turned_cols],
                                   ACT.Copy).then_inc(probsT_odd, 1)

                def units(i, first=False, final=False):
                    for u in range(8):
                        if not (final and u + 1 >= 8):
                            exps(*ahead(i, u, 1), fresh=first and u + 1 < 4)
                        if u % 2:
                            keep_odd(i, u)

                exps(0, 0, fresh=True)
                units(0, first=True)
                with act.Fori(1, COUNT - 1) as i:
                    units(i)
                units(COUNT - 1, final=True)
                for t in range(TILES + 4):
                    if t < TILES:
                        act.wait_ge(y_turned, t + 1)
                        act.activation(yT[:, t % 2, :, :], yturn[t % 2], ACT.Copy).then_inc(yT_ready, 1)
                    if 0 <= t - 4:
                        norm_keep(act, st, n, turns, t - 4)

            @block.vector
            def _(dve):
                links = [0]

                def link(ins):
                    links[0] += 1
                    ins.then_inc(chain, 1)
                    dve.wait_ge(chain, links[0])

                dve.wait_ge(e.loaded, e.loads)
                link(dve.tensor_scalar(roww[:, 0, :], roww[:, 0, :], 1e-8, None, ALU.max))
                link(dve.scalar_tensor_tensor(swap[:], roww[:, 1, :], 0.1, roww[:, 2, :], ALU.is_gt, ALU.mult))
                dve.wait_ge(consts_ready, 1)
                link(dve.tensor_tensor(factors[:, 3, :], rowscale[:], swap[:], ALU.mult))
                link(dve.tensor_tensor(factors[:, 2, :], rowscale[:], factors[:, 3, :], ALU.subtract))
                link(dve.tensor_scalar(factors[:, 1, :], factors[:, 3, :], float(VD) ** -0.5, None, ALU.mult))
                link(dve.tensor_scalar(factors[:, 0, :], factors[:, 2, :], float(VD) ** -0.5, None, ALU.mult))
                link(dve.memset(v[:, :, :, VD:VCOLS], 1.0))
                for j in range(4):
                    s, f = j // 2, j % 2
                    cols = slice(f * BANK, (f + 1) * BANK)
                    dve.wait_ge(crossed, 2 * j + 2)
                    dve.scalar_tensor_tensor(qT[:, s, cols], score[j % 2][:, :], factors[:, 0, s:s + 1],
                                             cross[:, 2 * (j % 2), :], ALU.mult, ALU.add).then_inc(qk_ready, 1)
                    dve.scalar_tensor_tensor(kT[:, s, cols], score[2 + j % 2][:, :], factors[:, 2, s:s + 1],
                                             cross[:, 2 * (j % 2) + 1, :], ALU.mult, ALU.add).then_inc(qk_ready, 1)
                dve.wait_ge(qk_ready, 8)

                def mask_q(i, s):
                    dve.tensor_scalar(qhead[s][:, :], qT[:, s, :], rowmask[:, bass.ds(i, 1)], None,
                                      ALU.mult).then_inc(qhead_ready, 1)

                def maxima(i, u, fresh=False):
                    unit = 8 * i + u
                    dve.wait_ge(scored, unit + 1)
                    if not fresh:
                        dve.wait_ge(exp_ready, 2 * unit - 6)
                    for q, width in enumerate(widths):
                        src = score[u % 4][:, q * SEQ:q * SEQ + width]
                        dve.tensor_reduce(shift[:, u % 4, q:q + 1], src, X_AXIS, ALU.max,
                                          negate=True).then_inc(shift_ready, 1)

                def keep_even(i, u):
                    dve.wait_ge(probs_turned, 8 * i + u + 1)
                    dve.tensor_copy(probsT[:, 0, 0:turned_cols], turn[0][:, 0:turned_cols]).then_inc(probsT_even, 1)

                def keep_heads(i, s):
                    dve.wait_ge(weighed, 2 * i + s + 1)
                    dve.tensor_scalar(heads_out[:, :, s, bass.ds(i, 1), :].squeeze(2),
                                      out[s][:, 0:TILES * VCOLS].rearrange("p (t e) -> p t e", t=TILES),
                                      1.0, None, ALU.mult).then_inc(heads_kept, 1)

                def units(i, first=False, final=False):
                    for u in range(8):
                        if not (final and u + 2 >= 8):
                            maxima(*ahead(i, u, 2), fresh=first and u + 2 < 4)
                        if u % 2 == 0:
                            keep_even(i, u)
                        if u == 1 and not first:
                            keep_heads(i - 1, 1)
                        if u in (1, 5) and not final:
                            dve.wait_ge(scored, 8 * i + u + 3)
                            mask_q(i + 1, u // 4)
                        if u == 5:
                            keep_heads(i, 0)

                mask_q(0, 0)
                mask_q(0, 1)
                maxima(0, 0, fresh=True)
                maxima(0, 1, fresh=True)
                units(0, first=True)
                with dve.Fori(1, COUNT - 1) as i:
                    units(i)
                units(COUNT - 1, final=True)
                keep_heads(COUNT - 1, 1)

                dve.wait_ge(heads_kept, 2 * COUNT)
                for t in range(TILES + 3):
                    if t < TILES:
                        o = heads_out[:, t, :, :, :]
                        r = rinv[:, t, :].rearrange("p (s h) -> p s h", s=2)
                        link(dve.reciprocal(r, o[:, :, :, VD]))
                        oo = heads_out[:, t, :, :, 0:VD].rearrange("p s h e -> p (s h) e")
                        dve.tensor_tensor(y[:, t, :].rearrange("p (h e) -> p h e", h=HEADS), oo,
                                          rinv[:, t, :].unsqueeze(2).broadcast_to([P, HEADS, VD]),
                                          ALU.mult).then_inc(y_ready, 1)
                    if 0 <= t - 2 < TILES:
                        norm_sum(dve, st, n, part, t - 2)
                    if 0 <= t - 3:
                        norm_apply(dve, st, n, t - 3)

            @block.gpsimd
            def _(pool):
                norm_pool(pool, st, n)



def fold_tensors(mem, sem):
    class F:
        pass
    f = F()
    f.w = [mem.sb(f"fa_w{s}", [P, 4, DM]) for s in range(2)]
    f.kv = [mem.sb(f"fa_kv{s}", [P, 2, CTX]) for s in range(2)]
    f.folded = mem.sb("fa_folded", [P, DC, BATCH, HEADS, KEYS])
    f.vw = mem.sb("fa_vw", [P, BATCH, PAIRS, DM])
    f.kv_bank = mem.psum("fa_kv_bank", [P, BANK])
    f.fold_bank = mem.psum("fa_fold_bank", [P, BANK])
    f.vw_bank = [mem.psum(f"fa_vw_bank{j}", [P, BANK]) for j in range(2)]
    f.w_loaded = [sem(f"fa_w_loaded{s}") for s in range(2)]
    f.kv_projected = sem("fa_kv_projected")
    f.kv_ready = sem("fa_kv_ready")
    f.fold_done = sem("fa_fold_done")
    f.folded_ready = sem("fa_folded_ready")
    f.vw_done = sem("fa_vw_done")
    f.vw_ready = sem("fa_vw_ready")
    return f


def fold_load(sp, f, d, h):
    if h >= 2:
        sp.wait_ge(f.vw_done, h - 1)
    sp.dma_start(f.w[h % 2][:], d["fa_w"][h]).then_inc(f.w_loaded[h % 2], 16)


def fold_tensor(pe, st, f, h):
    s = h % 2
    pe.wait_ge(f.w_loaded[s], 16 * (h // 2 + 1))
    if h:
        pe.wait_ge(f.kv_ready, h)
    for r in range(2):
        for j in range(DC):
            last = pe.matmul(f.kv_bank[:, r * CTX:(r + 1) * CTX], f.w[s][:, r, j * HD:(j + 1) * HD],
                             st.ctxT[:, j, :], start=j == 0, stop=j == DC - 1)
    last.then_inc(f.kv_projected, 1)
    pe.wait_ge(f.kv_ready, h + 1)
    if h:
        pe.wait_ge(f.folded_ready, h)
    for j in range(DC):
        last = pe.matmul(f.fold_bank[:, j * CTX:(j + 1) * CTX], f.w[s][:, 2, j * P:(j + 1) * P],
                         f.kv[s][:, 0, :], start=True, stop=True)
    last.then_inc(f.fold_done, 1)
    if s == 0 and h:
        pe.wait_ge(f.vw_ready, h)
    for b in range(BATCH):
        last = pe.matmul(f.vw_bank[b // 2][s * KEYS:(s + 1) * KEYS, (b % 2) * DM:(b % 2 + 1) * DM],
                         f.kv[s][:, 1, b * KEYS:(b + 1) * KEYS], f.w[s][:, 3, :], start=True, stop=True)
    last.then_inc(f.vw_done, 1)


def fold_scalar(act, f, h):
    s = h % 2
    act.wait_ge(f.kv_projected, h + 1)
    act.activation(f.kv[s][:].rearrange("p r n -> p (r n)"), f.kv_bank[:, :], ACT.Copy).then_inc(f.kv_ready, 1)
    act.wait_ge(f.fold_done, h + 1)
    act.activation(f.folded[:, :, :, h, :], f.fold_bank[:, :].rearrange("p (c b k) -> p c b k", c=DC, b=BATCH),
                   ACT.Copy, scale=float(HD) ** -0.5).then_inc(f.folded_ready, 1)
    if s:
        act.wait_ge(f.vw_done, h + 1)
        for j in range(2):
            act.activation(f.vw[:, 2 * j:2 * j + 2, h // 2, :],
                           f.vw_bank[j][:, :].rearrange("p (b n) -> p b n", b=2), ACT.Copy).then_inc(f.vw_ready, 1)


def folded_attention(nc, st, sem, d, f):
    with Memory(nc) as mem:
        c = cross_tensors(mem, sem, "fa", f.vw)
        turn_bank = [mem.psum(f"fa_turn{i}", [P, BANK]) for i in range(2)]
        norm_bank = [mem.psum(f"fa_norm{i}", [P, BANK]) for i in range(2)]
        n = norm_tensors(mem, st, "fa")
        score = f.vw_bank
        out_bank = [f.kv_bank, f.fold_bank]
        part = lambda t: out_bank[t % 2][:, 0:DM]
        turns = [norm_bank[i][:, 0:DM].rearrange("p (c n) -> p c n", c=DC) for i in range(2)]
        scored = sem("fa_scored")

        with nc.Block() as block:
            @block.tensor
            def _(pe):
                def scores(t):
                    if t > 0:
                        pe.wait_ge(c.shifted, t)
                    for j in range(2):
                        for k in range(DC):
                            last = pe.matmul(score[j][:, :], st.xT[:, k, tile_cols(t)],
                                             f.folded[:, k, t // 2, 8 * j:8 * j + 8, :].rearrange("p h k -> p (h k)"),
                                             start=k == 0, stop=k == DC - 1)
                        last.then_inc(scored, 1)
                scores(0)
                for t in range(TILES + 2):
                    if t + 1 < TILES:
                        scores(t + 1)
                    if t < TILES:
                        cross_turn(pe, st, c, turn_bank, t)
                    if 0 <= t - 1 < TILES:
                        cross_out(pe, c, n, part, t - 1)
                    if t >= 3:
                        norm_tensor(pe, st, n, turns, t - 3)
                norm_tensor(pe, st, n, turns, TILES - 1)

            @block.scalar
            def _(act):
                for t in range(TILES + 4):
                    if t < TILES:
                        cross_exp(act, c, t)
                    if 0 <= t - 1 < TILES:
                        cross_keep(act, c, turn_bank, t - 1)
                    if 0 <= t - 4:
                        norm_keep(act, st, n, turns, t - 4)

            @block.vector
            def _(dve):
                for t in range(TILES + 3):
                    if t < TILES:
                        for j in range(2):
                            dve.wait_ge(scored, 2 * t + j + 1)
                            dve.tensor_reduce(c.max[:, t, 8 * j:8 * j + 8],
                                              score[j][:, :].rearrange("p (h k) -> p h k", h=8),
                                              X_AXIS, ALU.max).then_inc(c.max_ready, 1)
                        dve.wait_ge(c.max_ready, 2 * t + 2)
                        for j in range(2):
                            last = dve.tensor_tensor(c.rows[:, t, 8 * j:8 * j + 8, :],
                                                     score[j][:, :].rearrange("p (h k) -> p h k", h=8),
                                                     over_keys(c.max[:, t, 8 * j:8 * j + 8]), ALU.subtract)
                        last.then_inc(c.shifted, 1)
                        cross_normalise_sum(dve, c, t)
                    if 0 <= t - 2 < TILES:
                        norm_sum(dve, st, n, part, t - 2)
                    if 0 <= t - 3:
                        norm_apply(dve, st, n, t - 3)

            @block.gpsimd
            def _(pool):
                for t in range(TILES + 2):
                    if t < TILES:
                        cross_weights(pool, c, t)
                    if t >= 2:
                        norm_rstd(pool, st, n, t - 2)



HALVES_Q = 2 * HEADS
D = DM // HALVES_Q
DIFFERENTIAL_FIRST = dict(wqk=(DC, 2 * DM), wv=(DC, DM), wo=(DC, DM), lam=(2, 2, D), bo=(DM,))


def folds_of(t):
    return (2 * t, 2 * t + 1) if t < TILES else ()


def differential_loads(sp, st, d):
    e = st.first4
    for name in DIFFERENTIAL_FIRST:
        src = d[f"da_{name}"]
        sp.dma_start(e[name], src.partition_broadcast(P) if name in ("lam", "bo") else src).then_inc(e.loaded, 16)


def differential_attention(nc, st, sem, d, f):
    early = st.first4
    wqk, wv, wo, lam_in, bo = (early[name] for name in DIFFERENTIAL_FIRST)
    VD = DM // HEADS
    CHUNKS = 4
    CQ = HALVES_Q // CHUNKS
    with Memory(nc) as mem:
        lam_prod = mem.sb("da_lam_prod", [P, 2, D])
        lam_sum = mem.sb("da_lam_sum", [P, 2])
        lam_exp = mem.sb("da_lam_exp", [P, 2])
        neg_lam = mem.sb("da_neg_lam", [P, 1])
        q = mem.sb("da_q", [P, TILES, HALVES_Q, D])
        k = mem.sb("da_k", [P, TILES, HALVES_Q, D])
        v = mem.sb("da_v", [P, TILES, HEADS, VD])
        prod_outer = mem.sb("da_prod_outer", [P, 2, D, CQ, HALVES_Q])
        prod_inner = mem.sb("da_prod_inner", [P, 2, CQ, HALVES_Q, D])
        above, below = (prod_inner[:, i, 0:CQ // 2, :, :].rearrange("p a b e -> p (a b e)").rearrange(
            "p (a b) -> p a b", a=HALVES_Q) for i in range(2))
        vprod = mem.sb("da_vprod", [P, HEADS, 2, HEADS // 2, VD])
        att = mem.sb("da_att", [P, 2, HALVES_Q, HALVES_Q])
        rowmax = mem.sb("da_rowmax", [P, HALVES_Q])
        rowsum = mem.sb("da_rowsum", [P, HALVES_Q])
        rinv = mem.sb("da_rinv", [P, HALVES_Q])
        first = mem.sb("da_first", [P, HEADS, HEADS])
        second = mem.sb("da_second", [P, HEADS, HEADS])
        diff = mem.sb("da_diff", [P, 2, HEADS, HEADS])
        squares = mem.sb("da_squares", [P, HEADS, VD])
        ssq = mem.sb("da_ssq", [P, HEADS])
        meansq = mem.sb("da_meansq", [P, HEADS])
        rms = mem.sb("da_rms", [P, HEADS])
        rrms = mem.sb("da_rrms", [P, HEADS])
        y = mem.sb("da_y", [P, 2, DM])
        yT = mem.sb("da_yT", [P, 2, DC, P])
        qk_bank = [mem.psum(f"da_qk_bank{i}", [P, BANK]) for i in range(2)]
        v_bank = [mem.psum(f"da_v_bank{i}", [P, BANK]) for i in range(2)]
        n = norm_tensors(mem, st, "da")
        score_bank = qk_bank[0]
        project_bank = lambda t, banks: banks[t if t < 2 else 1]
        part = lambda t: qk_bank[1][:, 0:DM]
        mixed = v_bank[0][:, DM:2 * DM].rearrange("p (h e) -> p h e", h=HEADS)
        yturn = v_bank[0][:, 0:DM].rearrange("p (c n) -> p c n", c=DC)
        turns = [v_bank[1][:, 0:DM].rearrange("p (c n) -> p c n", c=DC)] * 2

        qk_projected = sem("da_qk_projected")
        v_projected = sem("da_v_projected")
        qk_ready = sem("da_qk_ready")
        v_ready = sem("da_v_ready")
        lam_summed = sem("da_lam_summed")
        lam_ready = sem("da_lam_ready")
        pool_prod = sem("da_pool_prod")
        pe_reduced = sem("da_pe_reduced")
        guarded = sem("da_guarded")
        shifted = sem("da_shifted")
        exp_ready = sem("da_exp_ready")
        diff_ready = sem("da_diff_ready")
        pool_vprod = sem("da_pool_vprod")
        vreduced = sem("da_vreduced")
        ssq_ready = sem("da_ssq_ready")
        rms_ready = sem("da_rms_ready")
        y_ready = sem("da_y_ready")
        y_turned = sem("da_y_turned")
        yT_ready = sem("da_yT_ready")
        chain = sem("da_chain")

        def score_product(eng, out, t, j):
            return eng.tensor_tensor(
                out, q[:, t, j * CQ:(j + 1) * CQ, :].unsqueeze(2).broadcast_to([P, CQ, HALVES_Q, D]),
                k[:, t, :, :].unsqueeze(1).broadcast_to([P, CQ, HALVES_Q, D]), ALU.mult)

        def value_product(eng, t, j):
            half = HEADS // 2
            eng.tensor_tensor(
                vprod[:, :, j, :, :],
                diff[:, t % 2, j * half:(j + 1) * half, :].rearrange("p a h -> p h a").unsqueeze(3).broadcast_to(
                    [P, HEADS, half, VD]),
                v[:, t, :, :].unsqueeze(2).broadcast_to([P, HEADS, half, VD]), ALU.mult).then_inc(pool_vprod, 1)

        with nc.Block() as block:
            @block.sync
            def _(sp):
                for h in range(HEADS):
                    fold_load(sp, f, d, h)
                experts_loads(sp, st, d)

            @block.tensor
            def _(pe):
                pe.wait_ge(early.loaded, early.loads)
                def project(t):
                    if t == 2:
                        pe.wait_ge(qk_ready, 2 * t)
                        pe.wait_ge(v_ready, t)
                    elif t > 2:
                        pe.wait_ge(qk_ready, 2 * t)
                    for c in range(DC):
                        last = pe.matmul(project_bank(t, qk_bank)[:, :], st.xT[:, c, tile_cols(t)], wqk[:, c, :],
                                         start=c == 0, stop=c == DC - 1)
                    last.then_inc(qk_projected, 1)
                    if t > 2:
                        pe.wait_ge(v_ready, t)
                    for c in range(DC):
                        last = pe.matmul(project_bank(t, v_bank)[:, 0:DM], st.xT[:, c, tile_cols(t)], wv[:, c, :],
                                         start=c == 0, stop=c == DC - 1)
                    last.then_inc(v_projected, 1)

                def sum_products(t):
                    if t:
                        pe.wait_ge(guarded, t)
                    for j in range(2):
                        pe.wait_ge(pool_prod, 2 * t + j + 1)
                        for e in range(D):
                            last = pe.matmul(score_bank[:, j * CQ * HALVES_Q:(j + 1) * CQ * HALVES_Q],
                                             st.ident[:], prod_outer[:, j, e, :, :].rearrange("p a b -> p (a b)"),
                                             start=e == 0, stop=e == D - 1)
                        last.then_inc(pe_reduced, 1)

                def sum_values(t):
                    if t:
                        pe.wait_ge(yT_ready, t)
                    pe.wait_ge(pool_vprod, 3 * t + 3)
                    for h in range(HEADS // 2):
                        last = pe.matmul(v_bank[0][:, DM:2 * DM], st.ident[:],
                                         vprod[:, h, :, :, :].rearrange("p j a e -> p (j a e)"),
                                         start=h == 0, stop=h == HEADS // 2 - 1)
                    last.then_inc(vreduced, 1)

                for t in range(TILES // 2):
                    project(t)
                sum_products(0)
                for t in range(TILES // 2, TILES):
                    project(t)
                pe.wait_ge(qk_ready, 2 * TILES)
                pe.wait_ge(v_ready, TILES)
                sum_products(1)
                for t in range(TILES + 2):
                    for h in folds_of(t):
                        fold_tensor(pe, st, f, h)
                    if 0 <= t - 1 < TILES:
                        sum_values(t - 1)
                    if 1 <= t < TILES - 1:
                        sum_products(t + 1)
                    if t >= 2:
                        norm_tensor(pe, st, n, turns, t - 2, depth=1)
                    if 0 <= t - 1 < TILES:
                        r = t - 1
                        pe.wait_ge(y_ready, r + 1)
                        if r:
                            pe.wait_ge(yT_ready, r)
                        for c in range(DC):
                            last = pe.transpose(yturn[:, c, :], y[:, r % 2, tile_cols(c)], st.ident[:])
                        last.then_inc(y_turned, 1)
                        pe.wait_ge(yT_ready, r + 1)
                        if r:
                            pe.wait_ge(n.summed, n.base + r)
                        for c in range(DC):
                            last = pe.matmul(part(r), yT[:, r % 2, c, :], wo[:, c, :], start=c == 0, stop=c == DC - 1)
                        last.then_inc(n.out_ready, 1)

            @block.scalar
            def _(act):
                act.wait_ge(lam_summed, 1)
                act.activation(lam_exp[:], lam_sum[:], ACT.Exp).then_inc(lam_ready, 1)
                for t in range(TILES):
                    act.wait_ge(qk_projected, t + 1)
                    act.activation(q[:, t, :, :].rearrange("p a e -> p (a e)"), project_bank(t, qk_bank)[:, 0:DM], ACT.Copy,
                                   scale=float(D) ** -0.5).then_inc(qk_ready, 1)
                    act.activation(k[:, t, :, :].rearrange("p a e -> p (a e)"), project_bank(t, qk_bank)[:, DM:2 * DM],
                                   ACT.Copy).then_inc(qk_ready, 1)
                    act.wait_ge(v_projected, t + 1)
                    act.activation(v[:, t, :, :].rearrange("p h e -> p (h e)"), project_bank(t, v_bank)[:, 0:DM],
                                   ACT.Copy).then_inc(v_ready, 1)
                def exponentials(t):
                    act.wait_ge(shifted, t + 1)
                    act.activation(att[:, t % 2, :, :], att[:, t % 2, :, :], ACT.Exp).then_inc(exp_ready, 1)

                exponentials(0)
                for t in range(TILES + 2):
                    for h in folds_of(t):
                        fold_scalar(act, f, h)
                    if 1 <= t < TILES:
                        exponentials(t)
                    if 0 <= t - 1 < TILES:
                        act.wait_ge(vreduced, t)
                        act.activation(squares[:], mixed, ACT.Square).then_inc(rms_ready, 1)
                        act.wait_ge(ssq_ready, t)
                        act.activation(rms[:], meansq[:], ACT.Sqrt).then_inc(rms_ready, 1)
                    if t >= 2:
                        norm_keep(act, st, n, turns, t - 2)
                    if 0 <= t - 1 < TILES:
                        act.wait_ge(y_turned, t)
                        act.activation(yT[:, (t - 1) % 2, :, :], yturn, ACT.Copy).then_inc(yT_ready, 1)

            @block.gpsimd
            def _(pool):
                def score_products(t):
                    pool.wait_ge(qk_ready, 2 * t + 2)
                    for j in range(2):
                        if t > 0:
                            pool.wait_ge(pe_reduced, 2 * (t - 1) + j + 1)
                        score_product(pool, prod_outer[:, j, :, :, :].rearrange("p e a b -> p a b e"),
                                      t, j).then_inc(pool_prod, 1)

                score_products(0)
                for t in range(TILES + 2):
                    if t + 1 < TILES:
                        score_products(t + 1)
                    if t >= 2:
                        norm_rstd(pool, st, n, t - 2)
                    if t >= TILES:
                        continue
                    pool.wait_ge(diff_ready, t + 1)
                    pool.wait_ge(v_ready, t + 1)
                    if t > 0:
                        pool.wait_ge(vreduced, t)
                    value_product(pool, t, 0)
                    if t < TILES - 1:
                        value_product(pool, t, 1)
                    pool.wait_ge(pool_vprod, 3 * t + 2)
                    low, high = (vprod[:, h:h + HEADS // 2, :, :, :].rearrange("p h j a e -> p (h j a e)")
                                 for h in (0, HEADS // 2))
                    pool.tensor_tensor(low, low, high, ALU.add).then_inc(pool_vprod, 1)

            @block.vector
            def _(dve):
                links = [0]

                def link(ins):
                    links[0] += 1
                    ins.then_inc(chain, 1)
                    dve.wait_ge(chain, links[0])

                def over(a, count):
                    return a.unsqueeze(2).broadcast_to([P, a.shape[1], count])

                dve.wait_ge(early.loaded, early.loads)
                link(dve.tensor_tensor(lam_prod[:], lam_in[:, 0, :, :], lam_in[:, 1, :, :], ALU.mult))
                dve.tensor_reduce(lam_sum[:], lam_prod[:], X_AXIS, ALU.add).then_inc(lam_summed, 1)
                dve.wait_ge(lam_ready, 1)
                link(dve.scalar_tensor_tensor(neg_lam[:], lam_exp[:, 1:2], LAM_INIT, lam_exp[:, 0:1],
                                              ALU.subtract, ALU.subtract))
                for t in range(TILES):
                    link(dve.tensor_tensor(st.x[:, t, :], st.x[:, t, :], bo[:, :], ALU.add))

                def head_maps(t):
                    a = att[:, t % 2, :, :]
                    dve.wait_ge(qk_ready, 2 * t + 2)
                    score_product(dve, prod_inner[:, 0, :, :, :], t, 2)
                    link(score_product(dve, prod_inner[:, 1, :, :, :], t, 3))
                    link(dve.tensor_reduce(a[:, HEADS:, :], prod_inner[:].rearrange("p j a b e -> p (j a) b e"),
                                           X_AXIS, ALU.add))
                    dve.tensor_scalar(above[:, HEADS:, :], a[:, HEADS:, :], 0.0, LARGEST, ALU.max, ALU.min)
                    dve.tensor_scalar(below[:, HEADS:, :], a[:, HEADS:, :], 0.0, -LARGEST, ALU.min, ALU.max)
                    dve.wait_ge(pe_reduced, 2 * t + 2)
                    half = score_bank[:, :].rearrange("p (a b) -> p a b", a=HEADS)
                    dve.tensor_scalar(above[:, 0:HEADS, :], half, 0.0, LARGEST, ALU.max, ALU.min)
                    dve.tensor_scalar(below[:, 0:HEADS, :], half, 0.0, -LARGEST, ALU.min,
                                      ALU.max).then_inc(guarded, 1)
                    dve.wait_ge(guarded, t + 1)
                    link(dve.tensor_tensor(a, above[:], below[:], ALU.add))
                    link(dve.tensor_reduce(rowmax[:], a, X_AXIS, ALU.max))
                    dve.tensor_tensor(a, a, over(rowmax[:], HALVES_Q), ALU.subtract).then_inc(shifted, 1)

                def map_difference(t):
                    a = att[:, t % 2, :, :]
                    dve.wait_ge(exp_ready, t + 1)
                    link(dve.tensor_reduce(rowsum[:], a, X_AXIS, ALU.add))
                    link(dve.reciprocal(rinv[:], rowsum[:]))
                    dve.tensor_tensor(first[:], a[:, 0:HEADS, 0:HEADS], over(rinv[:, 0:HEADS], HEADS), ALU.mult)
                    link(dve.tensor_tensor(second[:], a[:, HEADS:, HEADS:], over(rinv[:, HEADS:], HEADS), ALU.mult))
                    dve.scalar_tensor_tensor(diff[:, t % 2, :, :].rearrange("p a h -> p (a h)"),
                                             second[:].rearrange("p a h -> p (a h)"), neg_lam[:, :],
                                             first[:].rearrange("p a h -> p (a h)"),
                                             ALU.mult, ALU.add).then_inc(diff_ready, 1)

                def mix(t):
                    dve.wait_ge(rms_ready, 2 * t + 1)
                    link(dve.tensor_reduce(ssq[:], squares[:], X_AXIS, ALU.add))
                    dve.tensor_scalar(meansq[:], ssq[:], 1.0 / VD, LN_EPS, ALU.mult, ALU.add).then_inc(ssq_ready, 1)

                def mix_norm(t):
                    dve.wait_ge(rms_ready, 2 * t + 2)
                    link(dve.reciprocal(rrms[:], rms[:]))
                    dve.scalar_tensor_tensor(y[:, t % 2, :].rearrange("p (h e) -> p h e", h=HEADS), mixed,
                                             1.0 - LAM_INIT, over(rrms[:], VD),
                                             ALU.mult, ALU.mult).then_inc(y_ready, 1)

                for t in range(TILES + 2):
                    if t < TILES:
                        head_maps(t)
                    if t >= 2:
                        norm_sum(dve, st, n, part, t - 2)
                    if t < TILES:
                        map_difference(t)
                    if 0 <= t - 1 < TILES:
                        mix(t - 1)
                    if t == TILES - 1:
                        dve.wait_ge(vreduced, t)
                        dve.wait_ge(diff_ready, t + 1)
                        value_product(dve, t, 1)
                    if t >= 2:
                        norm_apply(dve, st, n, t - 2)
                    if 0 <= t - 1 < TILES:
                        mix_norm(t - 1)


def differential_and_folded_attention(nc, st, sem, d):
    with Memory(nc) as mem:
        f = fold_tensors(mem, sem)
        differential_attention(nc, st, sem, d, f)
        folded_attention(nc, st, sem, d, f)



EXPERTS_FIRST = dict(router=(DC, EXPERTS), w0=(3 * DM,), w1=(3 * DM,))


def experts_loads(sp, st, d):
    e = st.first6
    sp.dma_start(e["router"], d["ex_router"]).then_inc(e.loaded, 16)
    for s in range(2):
        sp.dma_start(e[f"w{s}"], d["ex_w"][s]).then_inc(e.loaded, 16)


def experts(nc, st, sem, d):
    e = st.first6
    router = e["router"]
    w = [e["w0"], e["w1"]]
    PARTS = 3
    with Memory(nc) as mem:
        xs = split_x_tensors(mem, st, "ex")
        ws = [mem.sb(f"ex_ws{s}", [P, 2, 2, DC, P], F32R) for s in range(2)]
        wds = [mem.sb(f"ex_wds{s}", [P, 2, DM], F32R) for s in range(2)]
        spreadf = mem.sb("ex_spreadf", [PARTS * EXPERTS, FTILES, P])
        spread = mem.sb("ex_spread", [PARTS * EXPERTS, FTILES, P], BF16)
        logits = mem.sb("ex_logits", [P, TILES, EXPERTS])
        top = mem.sb("ex_top", [P, TILES, TOP_K])
        marked = mem.sb("ex_marked", [P, TILES, EXPERTS])
        chosen = mem.sb("ex_chosen", [P, TILES, EXPERTS])
        weights = mem.sb("ex_weights", [P, TILES, EXPERTS])
        wsum = mem.sb("ex_wsum", [P, TILES])
        winv = mem.sb("ex_winv", [P, TILES])
        parts = mem.sb("ex_parts", [P, TILES, PARTS, EXPERTS], BF16)
        partsT = mem.sb("ex_partsT", [PARTS * EXPERTS, TOK], BF16)
        silu = [mem.sb(f"ex_silu{f}", [P, BANK]) for f in range(2)]
        gated = [mem.sb(f"ex_gated{f}", [P, BANK]) for f in range(2)]
        hidden = [mem.sb(f"ex_hidden{f}", [P, BANK]) for f in range(2)]
        hs = [mem.sb(f"ex_hs{f}", [P, 2, BANK], F32R) for f in range(2)]
        gate_bank = [mem.psum(f"ex_gate{f}", [P, BANK]) for f in range(2)]
        up_bank = mem.psum("ex_up", [P, BANK])
        route_bank = mem.psum("ex_route", [P, BANK])
        out_bank = [mem.psum(f"ex_out{i}", [P, BANK]) for i in range(4)]
        logit_bank, parts_bank = out_bank[0], out_bank[2:4]
        n = norm_tensors(mem, st, "ex")
        part = lambda t: out_bank[t // 2][:, (t % 2) * DM:(t % 2 + 1) * DM]

        w_loaded = [sem(f"ex_w_loaded{s}") for s in range(2)]
        w_split = sem("ex_w_split")
        spread_loaded = sem("ex_spread_loaded")
        spread_ready = sem("ex_spread_ready")
        wd_split = sem("ex_wd_split")
        hi_ready = sem("ex_hi_ready")
        lo_ready = sem("ex_lo_ready")
        down_done = sem("ex_down_done")
        routed = sem("ex_routed")
        chain = sem("ex_chain")
        less_max = sem("ex_less_max")
        exp_ready = sem("ex_exp_ready")
        parts_ready = sem("ex_parts_ready")
        parts_turned = sem("ex_parts_turned")
        partsT_ready = sem("ex_partsT_ready")
        gate_done = sem("ex_gate_done")
        rest_done = sem("ex_rest_done")
        silu_ready = sem("ex_silu_ready")
        gated_ready = sem("ex_gated_ready")
        hidden_ready = sem("ex_hidden_ready")
        stored = sem("ex_stored")

        with nc.Block() as block:
            @block.sync
            def _(sp):
                sp.dma_start(spreadf[:], d["ex_spread"]).then_inc(spread_loaded, 16)
                with sp.Fori(0, FTILES // 2 - 1) as i:
                    for s in range(2):
                        sp.wait_ge(wd_split, 4 * i + 2 * s + 2)
                        sp.dma_start(w[s], d["ex_w"][2 * i + s + 2]).then_inc(w_loaded[s], 16)
                for t in range(TILES):
                    sp.wait_ge(n.x_ready, n.base + t + 1)
                    sp.dma_start(st.out[:, t, :], st.x[:, t, :]).then_inc(stored, 16)
                sp.wait_ge(stored, 16 * TILES)

            @block.tensor
            def _(pe):
                pe.wait_ge(e.loaded, e.loads)
                for t in range(TILES):
                    for c in range(DC):
                        last = pe.matmul(logit_bank[:, t * EXPERTS:(t + 1) * EXPERTS], st.xT[:, c, tile_cols(t)],
                                         router[:, c, :], start=c == 0, stop=c == DC - 1)
                last.then_inc(routed, 1)

                def gate(f, s):
                    for c, (k, m), first, end in products():
                        last = pe.matmul(gate_bank[f][:, :], ws[s][:, k, 0, c, :],
                                         xs.parts[:, m, c, f * BANK:(f + 1) * BANK], start=first, stop=end)
                    last.then_inc(gate_done, 1)

                def up(f, s):
                    for c, (k, m), first, end in products():
                        pe.matmul(up_bank[:, :], ws[s][:, k, 1, c, :],
                                  xs.parts[:, m, c, f * BANK:(f + 1) * BANK], start=first, stop=end)

                def route(j, f):
                    pe.matmul(route_bank[:, :], spread[:, bass.ds(j, 1), :].squeeze(1),
                              partsT[:, f * BANK:(f + 1) * BANK], start=True, stop=True).then_inc(rest_done, 1)

                def down(j, f, s, first=False, final=False):
                    u = 2 * j + f
                    pe.wait_ge(wd_split, 2 * j + 2)
                    pe.wait_ge(lo_ready, u + 1)
                    for q in range(TILES // 2):
                        for k, m in PASSES:
                            last = pe.matmul(part(f * TILES // 2 + q), hs[f][:, k, tile_cols(q)], wds[s][:, m, :],
                                             start=first and q % 2 == 0 and (k, m) == PASSES[0],
                                             stop=final and q % 2 == 1 and (k, m) == PASSES[-1])
                        if final and q % 2:
                            last.then_inc(n.out_ready, 2)
                    if not final:
                        last.then_inc(down_done, 1)

                pe.wait_ge(xs.lo_ready, xs.base + HALVES)
                pe.wait_ge(w_split, 2)
                gate(0, 0)
                gate(1, 0)
                up(0, 0)
                for t in range(TILES):
                    if t == 0:
                        pe.wait_ge(parts_ready, 1)
                    last = pe.matmul(parts_bank[t // 4][0:PARTS * EXPERTS, tile_cols(t % 4)],
                                     parts[:, t, :, :].rearrange("p r e -> p (r e)"), st.identb[:],
                                     start=True, stop=True)
                last.then_inc(parts_turned, 1)
                pe.wait_ge(spread_ready, 1)
                pe.wait_ge(partsT_ready, 2)
                route(0, 0)

                def unit(j, f, s, projected=False):
                    u = 2 * j + f
                    if f == 0:
                        pe.wait_ge(w_split, 2 * j + 2)
                    if not projected:
                        wait_past(pe, silu_ready, u - 1)
                        gate(f, s)
                    pe.wait_ge(gated_ready, u)
                    up(f, s)
                    pe.wait_ge(hidden_ready, u)
                    route(j, f)
                    if f == 0:
                        down(j - 1, 1, 1 - s, first=isinstance(j, int) and j == 1)
                    else:
                        down(j, 0, s, first=isinstance(j, int) and j == 0,
                             final=isinstance(j, int) and j == FTILES - 1)

                unit(0, 1, 0, projected=True)
                unit(1, 0, 1)
                unit(1, 1, 1)
                with pe.Fori(1, FTILES // 2 - 1) as i:
                    for s in range(2):
                        for f in range(2):
                            unit(2 * i + s, f, s)
                unit(FTILES - 2, 0, 0)
                unit(FTILES - 2, 1, 0)
                unit(FTILES - 1, 0, 1)
                unit(FTILES - 1, 1, 1)
                down(FTILES - 1, 1, 1, final=True)

            @block.scalar
            def _(act):
                split_x_scalar(act, st, xs)
                act.wait_ge(less_max, 1)
                act.activation(weights[:], weights[:], ACT.Exp).then_inc(exp_ready, 1)
                act.wait_ge(parts_turned, 1)
                for f in range(2):
                    act.activation(partsT[:, f * BANK:(f + 1) * BANK], parts_bank[f][0:PARTS * EXPERTS, :],
                                   ACT.Copy).then_inc(partsT_ready, 1)

                def silu_of(j, f):
                    u = 2 * j + f
                    act.wait_ge(gate_done, u + 1)
                    wait_past(act, gated_ready, u - 1)
                    act.activation(silu[f][:, :], gate_bank[f][:, :], ACT.Silu).then_inc(silu_ready, 1)

                def high_part(j, f):
                    u = 2 * j + f
                    act.wait_ge(hidden_ready, u + 1)
                    wait_past(act, down_done, u - 1)
                    act.activation(hs[f][:, 0, :], hidden[f][:, :], ACT.Copy).then_inc(hi_ready, 1)

                silu_of(0, 0)
                silu_of(0, 1)
                high_part(0, 0)
                high_part(0, 1)
                silu_of(1, 0)
                high_part(1, 0)
                silu_of(1, 1)
                with act.Fori(1, FTILES // 2) as i:
                    for s in range(2):
                        high_part(2 * i + s - 1, 1)
                        silu_of(2 * i + s, 0)
                        high_part(2 * i + s, 0)
                        silu_of(2 * i + s, 1)
                high_part(FTILES - 1, 1)

            @block.gpsimd
            def _(pool):
                def load_done(j, s, loads):
                    if isinstance(j, int):
                        pool.wait_ge(e.loaded, e.loads)
                    else:
                        pool.wait_ge(w_loaded[s], 16 * loads)

                def split_w(j, s, loads):
                    load_done(j, s, loads)
                    wait_past(pool, rest_done, 2 * j - 2)
                    whole = w[s][:, 0:2 * DM].rearrange("p (k n) -> p k n", n=P)
                    flat = [a.rearrange("p r c n -> p (r c) n") for a in (ws[s][:, 0], ws[s][:, 1])]
                    split_on(pool, ones_like(st, 2 * DC, P), whole, *flat, w_split, 2 * j)

                def split_wd(j, s):
                    wait_past(pool, down_done, 2 * j - 2)
                    split_on(pool, st.ones[:, :].broadcast_to([P, DM]), w[s][:, 2 * DM:3 * DM],
                             wds[s][:, 0, :], wds[s][:, 1, :], wd_split, 2 * j)
                split_w(0, 0, 1)
                pool.wait_ge(spread_loaded, 16)
                pool.tensor_copy(spread[:], spreadf[:]).then_inc(spread_ready, 1)
                split_wd(0, 0)
                split_w(1, 1, 1)
                split_wd(1, 1)
                with pool.Fori(1, FTILES // 2) as i:
                    for s in range(2):
                        split_w(2 * i + s, s, i)
                        split_wd(2 * i + s, s)
                norm_pool(pool, st, n)

            @block.vector
            def _(dve):
                links = [0]

                def link(ins):
                    links[0] += 1
                    ins.then_inc(chain, 1)
                    dve.wait_ge(chain, links[0])

                def over(a, count):
                    return a.unsqueeze(2).broadcast_to([P, a.shape[1], count])

                split_x_vector(dve, st, xs)
                dve.wait_ge(routed, 1)
                link(dve.tensor_copy(logits[:].rearrange("p t e -> p (t e)"), logit_bank[:, 0:TILES * EXPERTS]))
                for t in range(TILES):
                    last = dve.max(top[:, t, :], logits[:, t, :])
                link(last)
                for t in range(TILES):
                    last = dve.match_replace(marked[:, t, :], top[:, t, :], logits[:, t, :], -LARGEST)
                dve.tensor_tensor(weights[:], logits[:], over(top[:, :, 0], EXPERTS),
                                  ALU.subtract).then_inc(less_max, 1)
                link(last)
                link(dve.tensor_tensor(chosen[:], logits[:], marked[:], ALU.not_equal))
                dve.wait_ge(exp_ready, 1)
                link(dve.tensor_tensor(weights[:], weights[:], chosen[:], ALU.mult))
                link(dve.tensor_reduce(wsum[:], weights[:], X_AXIS, ALU.add))
                link(dve.reciprocal(winv[:], wsum[:]))
                link(dve.tensor_tensor(weights[:], weights[:], over(winv[:], EXPERTS), ALU.mult))
                for r in range(PARTS - 1):
                    link(dve.tensor_copy(parts[:, :, r, :], weights[:]))
                    link(dve.tensor_tensor(weights[:], weights[:], parts[:, :, r, :], ALU.subtract))
                dve.tensor_copy(parts[:, :, PARTS - 1, :], weights[:]).then_inc(parts_ready, 1)

                def unit(j, f):
                    u = 2 * j + f
                    dve.wait_ge(silu_ready, u + 1)
                    dve.wait_ge(rest_done, u + 1)
                    dve.tensor_tensor(gated[f][:, :], silu[f][:, :], up_bank[:, :], ALU.mult).then_inc(gated_ready, 1)
                    dve.wait_ge(gated_ready, u + 1)
                    wait_past(dve, lo_ready, u - 1)
                    dve.tensor_tensor(hidden[f][:, :], gated[f][:, :], route_bank[:, :],
                                      ALU.mult).then_inc(hidden_ready, 1)
                    dve.wait_ge(hi_ready, u + 1)
                    dve.wait_ge(hidden_ready, u + 1)
                    dve.tensor_tensor(hs[f][:, 1, :], hidden[f][:, :], hs[f][:, 0, :],
                                      ALU.subtract).then_inc(lo_ready, 1)
                unit(0, 0)
                unit(0, 1)
                with dve.Fori(1, FTILES) as j:
                    unit(j, 0)
                    unit(j, 1)
                norm_vector(dve, st, n, part)


STAGES = [self_attention, context_attention, recurrent_attention, differential_and_folded_attention, experts]


def values(shapes):
    return sum(int(np.prod(shape)) for shape in shapes.values())


EARLY_EVEN = max(values(CONTEXT_FIRST), values(DIFFERENTIAL_FIRST))
EARLY_ODD = max(values(RECURRENT_FIRST), values(EXPERTS_FIRST))


def build(nc, d, out):
    with ExitStack() as stack, Memory(nc) as mem:
        def sem(name):
            return stack.enter_context(nc.semaphore(name))
        st = State()
        st.x = mem.sb("x", [P, TILES, DM])
        st.xT = mem.sb("xT", [P, DC, TOK])
        st.ident = mem.sb("ident", [P, P])
        st.identb = mem.sb("identb", [P, P], BF16)
        st.mask = mem.sb("mask", [P, P], BF16)
        st.minus_half = mem.sb("minus_half", [P, 1])
        st.ones = mem.sb("ones", [P, 1])
        st.ctxT = mem.sb("ctxT", [P, DC, CTX])
        st.ctxT_loaded = sem("ctxT_loaded")
        st.xT_loaded = sem("xT_loaded")
        st.consts_ready = sem("consts_ready")
        st.out = out
        st.norm = norm_signals(sem)
        st.split = split_x_signals(sem)
        even = mem.sb("early_even", [P, EARLY_EVEN])
        odd = mem.sb("early_odd", [P, EARLY_ODD])
        st.first2 = Early(even, sem, "ca", **CONTEXT_FIRST)
        st.first3 = Early(odd, sem, "ra", **RECURRENT_FIRST)
        st.first4 = Early(even, sem, "da", **DIFFERENTIAL_FIRST)
        st.first6 = Early(odd, sem, "ex", **EXPERTS_FIRST)
        for stage in STAGES:
            stage(nc, st, sem, d)



def layouts(inp):
    g = {k: np.asarray(v) for k, v in inp.items()}
    o = {}
    rows = lambda a, t: a.reshape(t, P, -1).transpose(1, 0, 2)
    x = g["x"].reshape(TOK, DM)
    o["x"] = rows(x, TILES)
    o["xT"] = rows(x.T, DC)
    o["ident"] = np.eye(P, dtype=np.float32)
    o["mask"] = np.triu(np.full((P, P), MASKED, np.float32), 1)
    qk = np.stack([g["L0_attn_W_Q"], g["L0_attn_W_K"]], 1)
    o["sa_w"] = qk.reshape(HEADS, 2, DC, P, HD).transpose(0, 3, 1, 2, 4)
    o["sa_wv"] = g["L0_attn_W_V"].reshape(HEADS // 2, 2, DC, P, HD).transpose(0, 3, 2, 1, 4)
    o["sa_wo"] = g["L0_attn_W_O"].transpose(1, 0, 2)
    o["sa_bias"] = np.stack([g["L0_attn_b_Q"].T, g["L0_attn_b_K"].T, g["L0_attn_b_V"].T], 1)
    o["sa_bo"] = g["L0_attn_b_O"]
    o["ctxT"] = rows(g["ctx_2048"].reshape(CTX, DM).T, DC)
    o["ca_wq"] = g["L0_xattn_Wq"].reshape(DC, P, HEADS, HD).transpose(2, 1, 0, 3)
    o["ca_wk"] = rows(g["L0_xattn_Wk"], DC)
    o["ca_wv"] = rows(g["L0_xattn_Wv"], DC)
    o["ca_wo"] = g["L0_xattn_Wo"].reshape(HEADS, HD, DM).transpose(1, 0, 2)
    o["ca_bq"] = g["L0_xattn_bq"].reshape(HEADS, HD).T
    o["ca_bk"] = g["L0_xattn_bk"]
    o["ca_bv"] = g["L0_xattn_bv"].reshape(4, HD).T
    o["ca_norms"] = np.stack([g["L0_xattn_qn_w"], g["L0_xattn_kn_w"]], 1)
    o["ca_amask"] = g["mask_1xSxS2_ff0"][0].reshape(2, P, KEYS).transpose(1, 0, 2)
    wa = g["L0_ffn_Wa"]
    q_std, k_std, v, q_low, k_low = np.split(wa, [128, 256, 512, 640], axis=1)
    join = lambda a, b: np.concatenate([a.reshape(DM, HEADS, 8), b.reshape(DM, HEADS, 8)], 2).reshape(DM, DM)
    o["ra_wq"] = rows(join(q_std, q_low), DC)
    o["ra_wk"] = rows(join(k_std, k_low), DC)
    o["ra_wv"] = rows(v, DC)
    o["ra_wo"] = rows(g["L0_ffn_Wp"], DC)
    own = np.repeat(np.eye(8, dtype=np.float32), 16, 0)
    o["ra_rowmask"] = own
    is_low = np.tile(np.repeat(np.array([False, True]), 8), HEADS)
    std_row, rec_row = np.repeat(g["L0_ffn_w_std"], 16), np.repeat(g["L0_ffn_w_rec"], 16)
    w_row = np.where(is_low, rec_row, std_row)
    o["ra_roww"] = np.stack([w_row, rec_row, is_low.astype(np.float32)], 0).reshape(3, 2, P).transpose(2, 0, 1)
    half = lambda a: a.T.reshape(DM, HEADS, 8, 2).transpose(0, 3, 1, 2).reshape(DM, DM)
    o["da_wqk"] = rows(np.concatenate([half(g["L1_attn_Wq"]), half(g["L1_attn_Wk"])], 1), DC)
    o["da_wv"] = rows(g["L1_attn_Wv"].T, DC)
    o["da_wo"] = rows(g["L1_attn_Wo"].T, DC)
    o["da_lam"] = np.stack([np.stack([g["L1_attn_lq1"], g["L1_attn_lq2"]]),
                            np.stack([g["L1_attn_lk1"], g["L1_attn_lk2"]])])
    o["da_bo"] = g["L1_attn_bo"]
    by_head = lambda a: a.reshape(DC, P, HEADS, HD).transpose(2, 1, 0, 3).reshape(HEADS, P, 1, DM)
    o["fa_w"] = np.concatenate([by_head(g["L1_xattn_Wk"]), by_head(g["L1_xattn_Wv"]),
                                g["L1_xattn_Wq"].reshape(DM, HEADS, HD).transpose(1, 2, 0)[:, :, None, :],
                                g["L1_xattn_Wo"].reshape(HEADS, HD, 1, DM)], 2)
    stacked = lambda a: a.reshape(FTILES, P, DC, P).transpose(0, 3, 2, 1)
    wide = lambda a: stacked(a).reshape(FTILES, P, DM)
    o["ex_w"] = np.concatenate([wide(g["L1_ffn_w_gate_proj"]), wide(g["L1_ffn_w_up_proj"]),
                                g["L1_ffn_w_down_proj"].transpose(0, 2, 1).reshape(FTILES, P, DM)], 2)
    o["ex_router"] = rows(g["L1_ffn_gate_w"].T, DC)
    own = np.repeat(np.eye(EXPERTS), INNER, 1).reshape(EXPERTS, FTILES, P)
    o["ex_spread"] = np.concatenate([own] * 3, 0).astype(np.float32)
    return {k: np.ascontiguousarray(v) for k, v in o.items()}


def kernel(**inputs):
    import concourse.bacc as bacc
    from concourse.bass_utils import run_bass_kernel_spmd

    arrays = layouts(inputs)
    nc = bacc.Bacc("TRN2", target_bir_lowering=False, num_devices=1)
    d = {k: nc.dram_tensor(f"in_{k}", a.shape, mybir.dt.from_np(a.dtype), kind="ExternalInput").ap()
         for k, a in arrays.items()}
    out = nc.dram_tensor("out", (P, TILES, DM), F32, kind="ExternalOutput").ap()
    build(nc, d, out)
    r = run_bass_kernel_spmd(nc, [{f"in_{k}": a for k, a in arrays.items()}], core_ids=[0])
    y = r.results[0]["out"]
    return y.transpose(1, 0, 2).reshape(BATCH, SEQ, DM)
```
